# Optimizing a Trainium2 kernel written in Bass

```python
import numpy as np
import jax
import jax.numpy as jnp

def _softmax(x, axis=-1):
    return jax.nn.softmax(x, axis=axis)

def _gelu(x):
    return jax.nn.gelu(x, approximate=True)

def _silu(x):
    return jax.nn.silu(x)

def _sigmoid(x):
    return jax.nn.sigmoid(x)

def _layernorm(x, axis=-1, eps=1e-05):
    m = jnp.mean(x, axis=axis, keepdims=True)
    v = jnp.var(x, axis=axis, keepdims=True)
    return (x - m) / jnp.sqrt(v + eps)

def _scatter_add(tgt, idx, src, axis=0):
    return tgt.at[idx].add(src)

def _segment_sum(src, seg, n):
    return jax.ops.segment_sum(src, seg, n)
kernel_name = 'mk_xattn_ffn_d2_seqx_r8_fdcb9f'

def setup_inputs(seed: int=0):
    np.random.seed(seed)
    _w = jnp.asarray

    def _rec_inputs():
        import jax
        import jax.numpy as jnp
        _rk = jax.random.key(seed)
        x = 7.22e-05 + 1 * jax.random.normal(jax.random.fold_in(_rk, 1), (16, 128, 128), jnp.float32)
        _lenS = 128 - jax.random.randint(jax.random.fold_in(_rk, 7), (16,), 0, max(1, 128 // 4) + 1, jnp.int32)
        _lenS2 = 128 - jax.random.randint(jax.random.fold_in(_rk, 8), (16,), 0, max(1, 128 // 4) + 1, jnp.int32)
        _ctx_1024P = jax.random.normal(jax.random.fold_in(_rk, 11), (16, 16, 128), jnp.float32)
        _ctx_1024c = jax.random.dirichlet(jax.random.fold_in(_rk, 511), 0.3 * jnp.ones((16,), jnp.float32), (16, 128))
        _ctx_1024t = jnp.einsum('bsk,bkd->bsd', _ctx_1024c, _ctx_1024P)
        _ctx_1024t = _ctx_1024t * jax.lax.rsqrt(jnp.mean(jnp.square(_ctx_1024t)) + 1e-12) * 0.953939
        ctx_1024 = 4.13588e-05 + 0.999923 * (_ctx_1024t + 0.3 * jax.random.normal(jax.random.fold_in(_rk, 611), (16, 128, 128), jnp.float32))
        _validS = jnp.arange(128)[None, :] < _lenS[:, None]
        _validS2 = jnp.arange(128)[None, :] < _lenS2[:, None]
        _causal = jnp.tril(jnp.ones((128, 128), dtype=bool))
        mask_BxS2_bf1 = jnp.ones((16, 128), dtype=bool)
        return (x, ctx_1024, mask_BxS2_bf1)
    x, ctx_1024, mask_BxS2_bf1 = _rec_inputs()

    def _L0_xattn_setup():
        import jax, jax.numpy as jnp
        import numpy as np
        DIM = 128
        HEAD_NUM = 8
        D_HEAD = DIM // HEAD_NUM
        B, S = (4, 256)
        key = jax.random.key(seed)
        ks = jax.random.split(key, 7)
        scale = 0.02
        return {'Q': jax.random.normal(ks[0], (B, S, DIM), dtype=jnp.float32), 'K': jax.random.normal(ks[1], (B, S, DIM), dtype=jnp.float32), 'V': jax.random.normal(ks[2], (B, S, DIM), dtype=jnp.float32), 'W_Q': jax.random.normal(ks[3], (DIM, DIM), dtype=jnp.float32) * scale, 'W_K': jax.random.normal(ks[4], (DIM, DIM), dtype=jnp.float32) * scale, 'W_V': jax.random.normal(ks[5], (DIM, DIM), dtype=jnp.float32) * scale, 'W_O': jax.random.normal(ks[6], (DIM, DIM), dtype=jnp.float32) * scale}
    _L0_xattn_all = _L0_xattn_setup()
    _L0_xattn_in = {k: v for k, v in _L0_xattn_all.items() if k in ('W_Q', 'W_K', 'W_V', 'W_O')}
    del _L0_xattn_all

    def _L0_ffn_setup():
        import jax, jax.numpy as jnp
        import numpy as np
        INT8_MAX = 127.0

        def _absmax_scale(x, axes):
            amax = jnp.max(jnp.abs(x), axis=axes, keepdims=True)
            return jnp.maximum(amax, 1e-12) / INT8_MAX
        key = jax.random.key(seed)
        k1, k2 = jax.random.split(key)
        lhs = jax.random.normal(k1, (4, 1024, 128), dtype=jnp.float32)
        rhs = jax.random.normal(k2, (128, 128), dtype=jnp.float32)
        return {'lhs': lhs, 'rhs': rhs}
    _L0_ffn_all = _L0_ffn_setup()
    _L0_ffn_in = {k: v for k, v in _L0_ffn_all.items() if k in ('rhs',)}
    del _L0_ffn_all

    def _L1_xattn_setup():
        import jax, jax.numpy as jnp
        import numpy as np
        N_HEADS = 16
        D_MODEL = 128
        HEAD_DIM = D_MODEL // N_HEADS
        MASK_FILL = -100000000.0

        def _split_heads(x):
            B, S, _ = x.shape
            return x.reshape(B, S, N_HEADS, HEAD_DIM).transpose(0, 2, 1, 3)
        key = jax.random.key(seed)
        ks = jax.random.split(key, 12)
        B, L, P = (2, 256, 256)
        s = 1.0 / np.sqrt(D_MODEL).astype(np.float32)
        inp = {'q': jax.random.normal(ks[0], (B, L, D_MODEL), dtype=jnp.float32), 'k': jax.random.normal(ks[1], (B, P, D_MODEL), dtype=jnp.float32), 'v': jax.random.normal(ks[2], (B, P, D_MODEL), dtype=jnp.float32), 'attention_mask': jnp.ones((B, P), dtype=bool), 'Wq': jax.random.normal(ks[3], (D_MODEL, D_MODEL), dtype=jnp.float32) * s, 'bq': jnp.zeros((D_MODEL,), dtype=jnp.float32), 'Wk': jax.random.normal(ks[4], (D_MODEL, D_MODEL), dtype=jnp.float32) * s, 'bk': jnp.zeros((D_MODEL,), dtype=jnp.float32), 'Wv': jax.random.normal(ks[5], (D_MODEL, D_MODEL), dtype=jnp.float32) * s, 'bv': jnp.zeros((D_MODEL,), dtype=jnp.float32), 'Wo': jax.random.normal(ks[6], (D_MODEL, D_MODEL), dtype=jnp.float32) * s, 'bo': jnp.zeros((D_MODEL,), dtype=jnp.float32)}
        return inp
    _L1_xattn_all = _L1_xattn_setup()
    _L1_xattn_in = {k: v for k, v in _L1_xattn_all.items() if k in ('Wq', 'bq', 'Wk', 'bk', 'Wv', 'bv', 'Wo', 'bo')}
    del _L1_xattn_all

    def _L1_ffn_setup():
        import jax, jax.numpy as jnp
        import numpy as np
        TOP_K = 6

        def _glu_mlp(x, wg, wu, wd):
            return jax.nn.silu(x @ wg) * (x @ wu) @ wd
        key = jax.random.key(seed)
        ks = jax.random.split(key, 8)
        B, S, D, E, F, FS = (2, 256, 128, 8, 64, 128)
        sc = 0.02
        return {'hidden_states': jax.random.normal(ks[0], (B, S, D), jnp.float32), 'router_w': jax.random.normal(ks[1], (D, E), jnp.float32) * sc, 'w_gate': jax.random.normal(ks[2], (E, D, F), jnp.float32) * sc, 'w_up': jax.random.normal(ks[3], (E, D, F), jnp.float32) * sc, 'w_down': jax.random.normal(ks[4], (E, F, D), jnp.float32) * sc, 'ws_gate': jax.random.normal(ks[5], (D, FS), jnp.float32) * sc, 'ws_up': jax.random.normal(ks[6], (D, FS), jnp.float32) * sc, 'ws_down': jax.random.normal(ks[7], (FS, D), jnp.float32) * sc}
    _L1_ffn_all = _L1_ffn_setup()
    _L1_ffn_in = {k: v for k, v in _L1_ffn_all.items() if k in ('router_w', 'w_gate', 'w_up', 'w_down', 'ws_gate', 'ws_up', 'ws_down')}
    del _L1_ffn_all
    return {'x': x, 'ctx_1024': ctx_1024, 'mask_BxS2_bf1': mask_BxS2_bf1, 'L0_xattn_W_Q': _L0_xattn_in['W_Q'], 'L0_xattn_W_K': _L0_xattn_in['W_K'], 'L0_xattn_W_V': _L0_xattn_in['W_V'], 'L0_xattn_W_O': _L0_xattn_in['W_O'], 'L0_ffn_rhs': _L0_ffn_in['rhs'], 'L1_xattn_Wq': _L1_xattn_in['Wq'], 'L1_xattn_bq': _L1_xattn_in['bq'], 'L1_xattn_Wk': _L1_xattn_in['Wk'], 'L1_xattn_bk': _L1_xattn_in['bk'], 'L1_xattn_Wv': _L1_xattn_in['Wv'], 'L1_xattn_bv': _L1_xattn_in['bv'], 'L1_xattn_Wo': _L1_xattn_in['Wo'], 'L1_xattn_bo': _L1_xattn_in['bo'], 'L1_ffn_router_w': _L1_ffn_in['router_w'], 'L1_ffn_w_gate': _L1_ffn_in['w_gate'], 'L1_ffn_w_up': _L1_ffn_in['w_up'], 'L1_ffn_w_down': _L1_ffn_in['w_down'], 'L1_ffn_ws_gate': _L1_ffn_in['ws_gate'], 'L1_ffn_ws_up': _L1_ffn_in['ws_up'], 'L1_ffn_ws_down': _L1_ffn_in['ws_down']}

def reference(x, ctx_1024, mask_BxS2_bf1, L0_xattn_W_Q, L0_xattn_W_K, L0_xattn_W_V, L0_xattn_W_O, L0_ffn_rhs, L1_xattn_Wq, L1_xattn_bq, L1_xattn_Wk, L1_xattn_bk, L1_xattn_Wv, L1_xattn_bv, L1_xattn_Wo, L1_xattn_bo, L1_ffn_router_w, L1_ffn_w_gate, L1_ffn_w_up, L1_ffn_w_down, L1_ffn_ws_gate, L1_ffn_ws_up, L1_ffn_ws_down):
    import jax
    import jax.numpy as jnp

    def _L0_xattn_ref(Q, K, V, W_Q, W_K, W_V, W_O):
        import jax, jax.numpy as jnp
        import numpy as np
        DIM = 128
        HEAD_NUM = 8
        D_HEAD = DIM // HEAD_NUM
        B, S = (4, 256)
        b, s, d = Q.shape
        h, dh = (HEAD_NUM, d // HEAD_NUM)

        def proj_split(x, W):
            y = jnp.einsum('bsd,ed->bse', x, W)
            return y.reshape(b, s, h, dh).transpose(0, 2, 1, 3)
        q = proj_split(Q, W_Q)
        k = proj_split(K, W_K)
        v = proj_split(V, W_V)
        scores = jnp.einsum('bhqd,bhkd->bhqk', q, k) / jnp.sqrt(jnp.float32(dh))
        attn = jax.nn.softmax(scores, axis=1)
        ctx = jnp.einsum('bhqk,bhkd->bhqd', attn, v)
        ctx = ctx.transpose(0, 2, 1, 3).reshape(b, s, d)
        return jnp.einsum('bsd,ed->bse', ctx, W_O)

    def _L0_ffn_ref(lhs, rhs):
        import jax, jax.numpy as jnp
        import numpy as np
        INT8_MAX = 127.0

        def _absmax_scale(x, axes):
            amax = jnp.max(jnp.abs(x), axis=axes, keepdims=True)
            return jnp.maximum(amax, 1e-12) / INT8_MAX
        lhs_scale = _absmax_scale(lhs, (2,))
        rhs_scale = _absmax_scale(rhs, (0,))
        q_lhs = jnp.clip(jnp.round(lhs / lhs_scale), -INT8_MAX, INT8_MAX).astype(jnp.int8)
        q_rhs = jnp.clip(jnp.round(rhs / rhs_scale), -INT8_MAX, INT8_MAX).astype(jnp.int8)
        acc = jax.lax.dot_general(q_lhs, q_rhs, (((2,), (0,)), ((), ())), preferred_element_type=jnp.int32)
        return acc.astype(jnp.float32) * lhs_scale * rhs_scale

    def _L1_xattn_ref(q, k, v, attention_mask, Wq, bq, Wk, bk, Wv, bv, Wo, bo):
        import jax, jax.numpy as jnp
        import numpy as np
        N_HEADS = 16
        D_MODEL = 128
        HEAD_DIM = D_MODEL // N_HEADS
        MASK_FILL = -100000000.0

        def _split_heads(x):
            B, S, _ = x.shape
            return x.reshape(B, S, N_HEADS, HEAD_DIM).transpose(0, 2, 1, 3)
        qm = _split_heads(q @ Wq.T + bq)
        km = _split_heads(k @ Wk.T + bk)
        vm = _split_heads(v @ Wv.T + bv)
        scores = jnp.einsum('bnlh,bnph->bnlp', qm, km) / np.sqrt(HEAD_DIM).astype(np.float32)
        mask = attention_mask[:, None, None, :]
        scores = jnp.where(mask, scores, MASK_FILL)
        attn = jax.nn.softmax(scores, axis=-1)
        out = jnp.einsum('bnlp,bnph->bnlh', attn, vm)
        B, _, L, _ = out.shape
        out = out.transpose(0, 2, 1, 3).reshape(B, L, D_MODEL)
        return out @ Wo.T + bo

    def _L1_ffn_ref(hidden_states, router_w, w_gate, w_up, w_down, ws_gate, ws_up, ws_down):
        import jax, jax.numpy as jnp
        import numpy as np
        TOP_K = 6

        def _glu_mlp(x, wg, wu, wd):
            return jax.nn.silu(x @ wg) * (x @ wu) @ wd
        B, S, D = hidden_states.shape
        x = hidden_states.reshape(-1, D)
        scores = jax.nn.softmax(x @ router_w, axis=-1)
        topk_w, topk_idx = jax.lax.top_k(scores, TOP_K)
        g = jnp.einsum('td,edf->etf', x, w_gate)
        u = jnp.einsum('td,edf->etf', x, w_up)
        f_all = jnp.einsum('etf,efd->ted', jax.nn.silu(g) * u, w_down)
        picked = jnp.take_along_axis(f_all, topk_idx[:, :, None], axis=1)
        y = jnp.sum(picked * topk_w[:, :, None], axis=1).reshape(B, S, D)
        y = y + _glu_mlp(hidden_states, ws_gate, ws_up, ws_down)
        return y
    x = x + _L0_xattn_ref(_layernorm(x, axis=-1), ctx_1024, ctx_1024, L0_xattn_W_Q, L0_xattn_W_K, L0_xattn_W_V, L0_xattn_W_O)
    x = x + _L0_ffn_ref(_layernorm(x, axis=-1), L0_ffn_rhs)
    x = x + _L1_xattn_ref(_layernorm(x, axis=-1), ctx_1024, ctx_1024, mask_BxS2_bf1, L1_xattn_Wq, L1_xattn_bq, L1_xattn_Wk, L1_xattn_bk, L1_xattn_Wv, L1_xattn_bv, L1_xattn_Wo, L1_xattn_bo)
    x = x + _L1_ffn_ref(_layernorm(x, axis=-1), L1_ffn_router_w, L1_ffn_w_gate, L1_ffn_w_up, L1_ffn_w_down, L1_ffn_ws_gate, L1_ffn_ws_up, L1_ffn_ws_down)
    return x

_drawn_inputs = setup_inputs


def setup_inputs(seed=0):
    import zlib

    import numpy as np

    out = dict(_drawn_inputs(seed))
    spreads = {'L1_xattn_bq': (0.0, 0.8),
     'L1_xattn_bk': (0.0, 0.8),
     'L1_xattn_bv': (0.0, 0.8),
     'L1_xattn_bo': (0.0, 0.8)}
    factors = {'L0_xattn_W_Q': 4.106,
     'L0_xattn_W_K': 4.136,
     'L1_xattn_Wq': 2.949,
     'L1_xattn_Wk': 2.91,
     'L1_ffn_router_w': 8.0,
     'L1_ffn_w_gate': 8.0,
     'L1_ffn_w_up': 8.0,
     'L1_ffn_w_down': 8.0,
     'L1_ffn_ws_gate': 8.0,
     'L1_ffn_ws_up': 8.0,
     'L1_ffn_ws_down': 8.0}
    for name, (base, spread) in spreads.items():
        noise = np.random.default_rng([zlib.crc32(name.encode()), seed]).standard_normal(out[name].shape)
        drawn = base * np.exp(spread * noise) if base else spread * noise
        out[name] = jnp.asarray(drawn.astype(out[name].dtype))
    for name, factor in factors.items():
        out[name] = (out[name] * factor).astype(out[name].dtype)
    return out
```

```python
from contextlib import ExitStack

import numpy as np

import concourse.bass as bass
from concourse import mybir

F32 = mybir.dt.float32
F32R = mybir.dt.float32r
BF16 = mybir.dt.bfloat16
U8 = mybir.dt.uint8
ALU = mybir.AluOpType
ACT = mybir.ActivationFunctionType
AX = mybir.AxisListType

B, S, D = 16, 128, 128
GB = 4
NG = B // GB
T = GB * S
H0, DH0 = 8, 16
H1, DH1 = 16, 8
NE, FE, FS = 8, 64, 128
NC = NE * FE // 128
NB = NC + 1
TOPK = 6
EPS = 1e-5
MAGIC = 12582912.0
INV127 = float(np.float32(1.0) / np.float32(127.0))
SCALE1 = float(np.float32(1.0) / np.sqrt(np.float32(DH1)))

PACK = [("ident", 128), ("wq0", 128), ("wk0", 128), ("wv01", 256), ("mask0", 4), ("mask1", 4),
        ("bq1", 1), ("bk1", 1), ("bv1", 1), ("wo0", 128), ("rhsT", 128), ("wq1", 128), ("wk1", 128), ("wo1", 128),
        ("bo1", 128), ("maskM", 4), ("tri", 64),
        ("router", 8), ("down", NB * 128),
        ("selM", GB * 4 * 128), ("selW", NC * 128), ("gate", NB * 128), ("up", NB * 128)]
COL = {}
_at = 0
for _n, _w in PACK:
    COL[_n] = (_at, _at + _w)
    _at += _w
NPACK = _at
KEPT = COL["selM"][0]
SPLITS = [COL["wo0"][0], COL["router"][0], KEPT]

BANK_USES = {
    "A0": ["lnT0", "Q0", "V0", "cfT", "V1", "O0p", "qmm", "Q1"],
    "A1": ["ctxT", "K0", "K1", "qT", "lnT2"],
    "C0": [f"max{u}" for u in range(0, 16, 4)] + [f"s{u}" for u in range(0, 16, 3)] + ["TO0", "T3", "G0", "G2", "G4"],
    "C1": [f"max{u}" for u in range(1, 16, 4)] + [f"s{u}" for u in range(1, 16, 3)] + ["TO1", "lg", "G1", "G3"],
    "C2": [f"max{u}" for u in range(2, 16, 4)] + [f"s{u}" for u in range(2, 16, 3)] + ["OT", "lgT", "U0", "U2", "U4"],
    "C3": [f"max{u}" for u in range(3, 16, 4)] + ["AV01", "O1p", "WtT", "U1", "U3"],
    "D": ["MT", "AV23", "W0", "W1", "W2", "W3"],
}
BANK_OF = {use: bank for bank, uses in BANK_USES.items() for use in uses}


def upto(g, use):
    uses = BANK_USES[BANK_OF[use]]
    return g * len(uses) + uses.index(use) + 1


def wait(eng, sem, value):
    if not (isinstance(value, int) and value <= 0):
        eng.wait_ge(sem, value)


def build(nc, x_d, ctx_d, mask_d, pack_d, out_d):
    with ExitStack() as stack:
        def sb(name, shape, dt=F32):
            return stack.enter_context(nc.sbuf_tensor(name, shape, dt))

        def sem(name):
            return stack.enter_context(nc.semaphore(name))

        pack = sb("pack", [128, KEPT])

        def const(name):
            return pack[:, COL[name][0]:COL[name][1]]

        ident, mask0, mask1, maskM = const("ident"), const("mask0"), const("mask1"), const("maskM")
        down = const("down").rearrange("p (c d) -> p c d", c=NB)
        identr = sb("identr", [128, 128], F32R)
        selM = sb("selM", [128, GB * 4, 128], F32R)
        selW = sb("selW", [128, NC, 128], F32R)
        routerH, routerL = sb("routerH", [128, NE], F32R), sb("routerL", [128, NE], F32R)
        guH = sb("guH", [128, 2, NB, 128], F32R)
        guL = sb("guL", [128, 2, NB, 128], F32R)
        rhsq = sb("rhsq", [128, 128], BF16)
        rscale = sb("rscale", [128, 128])
        rq = sb("rq", [128, 2, 128])
        rtmp = sb("rtmp", [128, 4])
        bq1m, bk1m = sb("bq1m", [128, 4]), sb("bk1m", [128, 4])
        cb1 = sb("cb1", [128, 128])
        ones = sb("ones", [128, 128])
        nhalf = sb("nhalf", [128, GB])
        m8 = sb("m8", [B, S], U8)
        mf = sb("mf", [B, S])
        mcol = sb("mcol", [128, B])
        mkeep = sb("mkeep", [128, B])
        mfill = sb("mfill", [128, B])
        mtmp = sb("mtmp", [128, 3, B])
        mkeep4, mfill4 = sb("mkeep4", [128, GB]), sb("mfill4", [128, GB])

        xin, ctx = sb("xin", [128, GB, D]), sb("ctx", [128, GB, D])
        mk8 = sb("mk8", [128, GB, S], U8)
        mrow, omk, mdiag, fill = (sb(n, [128, GB, S]) for n in ("mrow", "omk", "mdiag", "fill"))
        lnst = [sb(f"lnst{i}", [128, GB, 6]) for i in range(4)]
        lnmv = [sb(f"lnmv{i}", [128, GB, 2]) for i in range(4)]
        lnve, lnrs, lnnm = ([sb(f"{n}{i}", [128, GB]) for i in range(4)] for n in ("lnve", "lnrs", "lnnm"))
        lnx = [sb(f"lnx{i}", [128, GB, D]) for i in (0, 1, 3)]
        lnx.insert(2, lnx[0])
        lnT0, ctxT, cfT = (sb(n, [128, T]) for n in ("lnT0", "ctxT", "cfT"))
        lnT2 = lnT0
        Qm0 = sb("Qm0", [128, 4, T])
        Kg0 = sb("Kg0", [128, 2, T])
        Vm0 = sb("Vm0", [128, GB, H0, 32])
        negM0 = sb("negM0", [128, S], F32R)
        E0 = [sb(f"E0_{i}", [128, H0, S]) for i in range(2)]
        hs = sb("hs", [128, 6, S])
        hsum = [sb(f"hsum{i}", [128, S]) for i in range(2)]
        hrec = [sb(f"hrec{i}", [128, S]) for i in range(2)]
        O0T = sb("O0T", [128, T])
        x1, x2, xb, x3, y3 = (sb(n, [128, GB, D]) for n in ("x1", "x2", "xb", "x3", "y3"))
        amax, lscale, lrec = (sb(n, [128, GB]) for n in ("amax", "lscale", "lrec"))
        qz = sb("qz", [128, GB, D])
        qT = sb("qT", [128, T], BF16)
        qres = qz
        Qm1 = sb("Qm1", [128, 4, T])
        Kd1 = sb("Kd1", [128, T])
        Kg1 = sb("Kg1", [128, 4, T])
        Km1 = sb("Km1", [128, 4, T], F32R)
        Qd1 = sb("Qd1", [128, T], F32R)
        Qg1 = sb("Qg1", [128, 4, T], F32R)
        VS1 = sb("VS1", [128, GB, H1, 64])
        negM1 = sb("negM1", [128, 128])
        pause = sb("pause", [128, 1])
        MX = sb("MX", [128, 4, S], F32R)
        E1 = [sb(f"E1_{i}", [128, 4, 4, S]) for i in range(2)]
        raw = [e[:].rearrange("p g j q -> p (g j q)") for e in E1]
        raw_sel, raw_gu = raw[1][:, 0:NC * 128], raw[1][:, NC * 128:(NC + 2 * NB) * 128]
        OU = sb("OU", [128, GB, 2, S])
        Rq = sb("Rq", [128, 2, 8, 4])
        Oq = sb("Oq", [128, GB, D])
        O1T = sb("O1T", [128, T])
        T3h, T3l = sb("T3h", [128, T], F32R), sb("T3l", [128, T], F32R)
        lgs = sb("lgs", [128, T])
        tk = {n: sb(f"tk_{n}", [128, GB]) for n in ("nmax", "sum", "rec")}
        tke, tkp, rank, Wt = (sb(n, [128, GB, NE]) for n in ("tke", "tkp", "rank", "Wt"))
        ge, gt, gmix = (sb(n, [128, GB, NE, NE]) for n in ("ge", "gt", "gmix"))
        Wx = sb("Wx", [128, T], F32R)
        sg = [sb(f"sg{i}", [128, T]) for i in range(2)]
        gu = [sb(f"gu{i}", [128, T]) for i in range(2)]
        hid = [sb(f"hid{i}", [128, T]) for i in range(2)]

        psA = stack.enter_context(nc.psum_tensor("psA", [128, 1024], F32))
        bank = {"A0": psA[:, 0:512], "A1": psA[:, 512:1024]}
        for n in ("C0", "C1", "C2", "C3", "D", "O"):
            bank[n] = stack.enter_context(nc.psum_tensor("ps" + n, [128, 512], F32))[:, :]

        full = {b: sem(f"full_{b}") for b in BANK_USES}
        drained = {b: sem(f"drained_{b}") for b in BANK_USES}
        s_pack = [sem(f"s_pack{i}") for i in range(4)]
        s_mask, s_x, s_ctx, s_mk, s_out = sem("s_mask"), sem("s_x"), sem("s_ctx"), sem("s_mk"), sem("s_out")
        zeroed = sem("zeroed")
        cst = {n: sem("c_" + n) for n in ("ones", "act", "dve", "mf", "psT", "mcol", "psN", "mtmp", "masks", "rq",
                                          "psR", "psC", "cb", "wlo", "whi")}
        mk = {n: sem("mk_" + n) for n in ("row", "diag", "four", "fill")}
        ln = [{n: sem(f"ln{i}_{n}") for n in ("stats", "mv", "var", "rstd", "shift", "out")} for i in range(4)]
        scored0, m0_ready, biased0, exp0 = sem("scored0"), sem("m0_ready"), sem("biased0"), sem("exp0")
        hs_step, hsum_ready, hrec_ready, attn0, av0 = (sem(n) for n in ("hs_step", "hsum_ready", "hrec_ready", "attn0", "av0"))
        o0_drained = sem("o0_drained")
        q_amax, q_scale, q_rec, q_int, q_res = (sem(n) for n in ("q_amax", "q_scale", "q_rec", "q_int", "q_res"))
        x2_ready, xb_ready = sem("x2_ready"), sem("xb_ready")
        kd1_ready, qd1_ready, kg1_dma, qg1_dma, ones1_ready = (sem(n) for n in ("kd1_ready", "qd1_ready", "kg1_dma",
                                                                                "qg1_dma", "ones1_ready"))
        rec1, av_even = sem("rec1"), sem("av_even")
        t3h_ready = sem("t3h_ready")
        tks = {n: sem("tk_" + n) for n in ("max", "exp", "sum", "rec", "p", "gt", "ge", "mix", "max2", "rank", "w")}
        wxh_ready = sem("wxh_ready")
        hid_ready, y_drained = sem("hid_ready"), sem("y_drained")
        down_done = sem("down_done")

        def flat(ap):
            return ap.rearrange("p b d -> p (b d)")

        def bank3(name, n=GB):
            return bank[name].rearrange("p (b d) -> p b d", b=n)

        block = stack.enter_context(nc.Block())

        def skewed(eng, stage_a, both, stage_c):
            stage_a(0)
            with eng.Fori(1, NG) as g:
                both(g)
            stage_c(NG - 1)

        @block.sync
        def _(sp):
            def loads(g):
                if not isinstance(g, int):
                    sp.wait_ge(drained["A0"], upto(g - 1, "O0p"))
                sp.dma_start(xin[:], x_d[bass.ts(g, GB)].rearrange("b t d -> t b d")).then_inc(s_x, 16)
                if not isinstance(g, int):
                    sp.wait_ge(full["A0"], upto(g - 1, "cfT"))
                    sp.wait_ge(mk["row"], g)
                sp.dma_start(ctx[:], ctx_d[bass.ts(g, GB)].rearrange("b t d -> t b d")).then_inc(s_ctx, 16)
                sp.dma_start(mk8[:], mask_d[bass.ts(g, GB)].partition_broadcast(128)).then_inc(s_mk, 16)

            def heads1(g):
                sp.wait_ge(kd1_ready, g + 1)
                for G in range(4):
                    r = slice(32 * G, 32 * G + 32)
                    sp.dma_start(Kg1[r, G, :], Kd1[r, :]).then_inc(kg1_dma, 16)
                sp.wait_ge(qd1_ready, g + 1)
                for G in range(4):
                    r = slice(32 * G, 32 * G + 32)
                    sp.dma_start(Qg1[r, G, :].bitcast(F32), Qd1[r, :].bitcast(F32)).then_inc(qg1_dma, 16)

            def store(m):
                sp.wait_ge(y_drained, m + 1)
                sp.dma_start(out_d[bass.ts(m, GB)].rearrange("b t d -> t b d"), y3[:]).then_inc(s_out, 16)

            sp.dma_start(m8[:], mask_d).then_inc(s_mask, 16)
            at = 0
            for i, end in enumerate(SPLITS):
                sp.dma_start(pack[:, at:end], pack_d[:, at:end]).then_inc(s_pack[i], 16)
                at = end
                if i == 0:
                    loads(0)
            for i, (begin, end) in enumerate(((KEPT, COL["selW"][0]), (COL["selW"][0], NPACK))):
                sp.dma_start(raw[i][:, 0:end - begin], pack_d[:, begin:end]).then_inc(s_pack[3], 16)

            def both(g):
                loads(g)
                heads1(g)
                store(g - 1)

            def last(m):
                store(m)

            skewed(sp, heads1, both, last)
            sp.wait_ge(s_out, 16 * NG + 1)

        @block.gpsimd
        def _(pool):
            p = nc.gpsimd
            p.memset(nhalf[:], -0.5).then_inc(zeroed, 1)
            p.memset(y3[:], 0.0).then_inc(s_out, 1)
            p.memset(ones[:], 1.0).then_inc(cst["ones"], 1)
            for t in (Kg0, Vm0, VS1, Kg1, Qg1, MX, Wx, negM1, lgs):
                a = t[:]
                p.memset(a.bitcast(F32) if a.dtype == F32R else a, 0.0).then_inc(zeroed, 1)

            def rstd(i, g):
                pool.wait_ge(ln[i]["var"], g + 1)
                p.tensor_tensor(lnrs[i][:], lnve[i][:], nhalf[:], ALU.pow).then_inc(ln[i]["rstd"], 1)

            def masks(g):
                pool.wait_ge(mk["row"], g + 1)
                wait(pool, mk["fill"], g * GB)
                p.tensor_tensor(omk[:], ones[:].unsqueeze(1).to_broadcast([128, GB, 128]), mrow[:], ALU.subtract)
                p.tensor_tensor(mdiag[:], mrow[:], ident.unsqueeze(1).to_broadcast([128, GB, 128]),
                                ALU.mult).then_inc(mk["diag"], 1)

            def headsum(g, b):
                n = GB * g + b
                pool.wait_ge(exp0, n + 1)
                e = E0[b % 2]
                if b >= 2 or not isinstance(g, int):
                    pool.wait_ge(hrec_ready, n - 1)
                p.tensor_tensor(hs[:, 0:4], e[:, 0:4], e[:, 4:8], ALU.add).then_inc(hs_step, 1)
                pool.wait_ge(hs_step, 2 * n + 1)
                p.tensor_tensor(hs[:, 4:6], hs[:, 0:2], hs[:, 2:4], ALU.add).then_inc(hs_step, 1)
                pool.wait_ge(hs_step, 2 * n + 2)
                p.tensor_tensor(hsum[b % 2][:], hs[:, 4], hs[:, 5], ALU.add).then_inc(hsum_ready, 1)

            def bias_residual(g):
                pool.wait_ge(x2_ready, g + 1)
                pool.wait_ge(cst["cb"], 1)
                if not isinstance(g, int):
                    pool.wait_ge(drained["C3"], upto(g - 1, "O1p"))
                p.tensor_tensor(xb[:], x2[:], cb1[:].unsqueeze(1).to_broadcast([128, GB, D]), ALU.add).then_inc(xb_ready, 1)

            def mix(m):
                pool.wait_ge(tks["ge"], m + 1)
                tri = const("tri").rearrange("p (i j) -> p i j", i=NE).unsqueeze(1).to_broadcast([128, GB, NE, NE])
                p.tensor_tensor(gmix[:], ge[:], tri, ALU.mult).then_inc(tks["mix"], 1)

            def first(g):
                rstd(0, g)
                masks(g)

            def third(g):
                rstd(1, g)
                rstd(2, g)
                bias_residual(g)

            def stage_a(g):
                pool.wait_ge(s_pack[0], 16)
                pool.wait_ge(s_pack[1], 16)
                pool.wait_ge(zeroed, 10)
                pool.wait_ge(cst["ones"], 1)
                first(g)
                for b in range(GB):
                    headsum(g, b)
                third(g)

            def both(g):
                first(g)
                for b in range(GB):
                    headsum(g, b)
                rstd(1, g)
                rstd(3, g - 1)
                rstd(2, g)
                mix(g - 1)
                bias_residual(g)

            def stage_c(m):
                rstd(3, m)
                mix(m)

            skewed(pool, stage_a, both, stage_c)

        @block.scalar
        def _(act):
            a = nc.scalar

            def wfull(use, g):
                act.wait_ge(full[BANK_OF[use]], upto(g, use))

            def normalize(i, src, g):
                act.wait_ge(ln[i]["shift"], g + 1)
                if i == 0:
                    wait(act, full["A1"], prev(g, "lnT2"))
                elif i == 1:
                    wait(act, q_int, g)
                elif i == 2:
                    act.wait_ge(full["A0"], upto(g, "lnT0"))
                for b in range(GB):
                    ins = a.activation(lnx[i][:, b], src[:, b], ACT.Identity, bias=lnnm[i][:, b:b + 1],
                                       scale=lnrs[i][:, b:b + 1])
                ins.then_inc(ln[i]["out"], 1)

            def prev(g, use):
                return 0 if isinstance(g, int) and g == 0 else upto(g - 1, use)

            def a1_ln(g):
                act.wait_ge(s_x, 16 * g + 16)
                normalize(0, xin, g)

            def a1_t(g):
                wfull("lnT0", g)
                a.copy(lnT0[:], bank["A0"]).then_inc(drained["A0"], 1)
                wfull("ctxT", g)
                a.copy(ctxT[:], bank["A1"]).then_inc(drained["A1"], 1)

            def a1_q(g):
                wfull("Q0", g)
                wait(act, biased0, GB * g)
                for j in range(4):
                    ins = a.activation(Qm0[:, j], bank["A0"], ACT.Copy, scale=mask0[:, j:j + 1])
                ins.then_inc(drained["A0"], 1)

            def a1_v(g):
                wfull("V0", g)
                wait(act, av0, GB * g)
                dst = bass.AP(tensor=Vm0[:].tensor, offset=0, ap=[[GB * H0 * 32, 128], [64, GB * 4], [48, 2], [1, DH0]])
                a.copy(dst, bank["A0"].rearrange("p (n j d) -> p n j d", j=2, d=DH0)).then_inc(drained["A0"], 1)

            def a2_exp(g, b):
                n = GB * g + b
                act.wait_ge(biased0, n + 1)
                if b >= 2 or not isinstance(g, int):
                    act.wait_ge(av0, n - 1)
                a.activation(E0[b % 2][:].rearrange("p h q -> p (h q)"), psA[:, :], ACT.Exp, scale=0.25).then_inc(exp0, 1)

            def a3_o0(g):
                act.wait_ge(av0, GB * g + GB)
                wait(act, full["A0"], prev(g, "O0p"))
                a.copy(O0T[:], bank["O"]).then_inc(o0_drained, 1)

            def a3_ctx(g):
                wfull("cfT", g)
                wait(act, full["A1"], prev(g, "K1"))
                a.copy(cfT[:], bank["A0"]).then_inc(drained["A0"], 1)

            def a3_k1(g):
                act.wait_ge(kd1_ready, g + 1)
                for j in range(4):
                    ins = a.activation(Km1[:, j], bank["A1"], ACT.Identity, bias=bk1m[:, j:j + 1], scale=mask1[:, j:j + 1])
                ins.then_inc(drained["A1"], 1)

            def a3_v1(g):
                wfull("V1", g)
                act.wait_ge(mk["four"], g + 1)
                for b in range(GB):
                    dst = bass.AP(tensor=VS1[:].tensor, offset=b * H1 * 64,
                                  ap=[[GB * H1 * 64, 128], [4 * 64, 4], [72, 4], [1, DH1]])
                    src = bank["A0"][:, 128 * b:128 * b + 128].rearrange("p (w j d) -> p w j d", w=4, j=4)
                    ins = a.activation(dst, src, ACT.Copy, scale=mkeep4[:, b:b + 1])
                ins.then_inc(drained["A0"], 1)

            def a3_t2(g):
                wfull("lnT2", g)
                a.copy(lnT2[:], bank["A1"]).then_inc(drained["A1"], 1)

            def a3_q1(g):
                act.wait_ge(qd1_ready, g + 1)
                for j in range(4):
                    ins = a.activation(Qm1[:, j], bank["A0"], ACT.Identity, bias=bq1m[:, j:j + 1], scale=mask1[:, j:j + 1])
                ins.then_inc(drained["A0"], 1)

            def c1_exp(m, u):
                use = f"s{u}"
                wfull(use, m)
                if u == 8:
                    act.wait_ge(av_even, 2 * m + 1)
                elif u == 12:
                    act.wait_ge(full["C3"], upto(m, "AV01"))
                a.activation(E1[u // 4 % 2][:, u % 4].rearrange("p j q -> p (j q)"), bank[BANK_OF[use]], ACT.Exp,
                             scale=SCALE1).then_inc(drained[BANK_OF[use]], 1)

            def c1_out(m, half):
                use = ("AV01", "AV23")[half]
                wfull(use, m)
                a.copy(OU[:, 2 * half:2 * half + 2].rearrange("p b w q -> p (b w q)"),
                       bank[BANK_OF[use]]).then_inc(drained[BANK_OF[use]], 1)

            def c2_oT(m):
                wfull("OT", m)
                a.copy(O1T[:], bank["C2"]).then_inc(drained["C2"], 1)

            def c2_ln(m):
                normalize(3, x3, m)

            def c2_t(m):
                wfull("T3", m)
                a.copy(T3h[:], bank["C0"]).then_inc(t3h_ready, 1)

            def c2_router(m):
                wfull("lg", m)
                a.copy(lgs[0:NE, :], bank["C1"][0:NE, :]).then_inc(drained["C1"], 1)

            def c2_exp(m):
                act.wait_ge(drained["C2"], upto(m, "lgT"))
                a.activation(tke[:], tke[:], ACT.Exp).then_inc(tks["exp"], 1)

            def c2_w(m):
                wfull("WtT", m)
                a.copy(Wx[0:NE, :], bank["C3"][0:NE, :]).then_inc(wxh_ready, 1)

            def c2_silu(m, i):
                wfull(f"G{i}", m)
                if i >= 2:
                    act.wait_ge(drained[BANK_OF[f"U{i - 2}"]], upto(m, f"U{i - 2}"))
                a.activation(sg[i % 2][:], bank[BANK_OF[f"G{i}"]], ACT.Silu).then_inc(drained[BANK_OF[f"G{i}"]], 1)

            act.wait_ge(s_pack[0], 16)
            a.copy(identr[:], ident).then_inc(cst["act"], 1)

            def late_constants():
                act.wait_ge(s_pack[1], 16)
                act.wait_ge(s_pack[2], 16)
                act.wait_ge(s_pack[3], 32)
                a.copy(routerH[:], const("router"))
                a.copy(guH[:].rearrange("p k c f -> p (k c f)"), raw_gu)
                a.copy(selM[:].rearrange("p u k -> p (u k)"), raw[0])
                a.copy(selW[:].rearrange("p c k -> p (c k)"), raw_sel).then_inc(cst["whi"], 1)

            def stage_a(g):
                a1_ln(g)
                a1_t(g)
                a1_q(g)
                a1_v(g)
                act.wait_ge(zeroed, 10)
                for b in range(GB):
                    a2_exp(g, b)
                    if b == 0:
                        late_constants()
                a3_ctx(g)
                a3_k1(g)
                a3_v1(g)
                a3_o0(g)
                normalize(1, x1, g)
                normalize(2, x2, g)
                a3_t2(g)
                a3_q1(g)

            def both(g):
                m = g - 1
                a1_ln(g)
                a1_t(g)
                a1_q(g)
                a1_v(g)
                for b in range(GB):
                    c1_exp(m, 4 * b)
                    c1_exp(m, 4 * b + 1)
                    a2_exp(g, b)
                    c1_exp(m, 4 * b + 2)
                    c1_exp(m, 4 * b + 3)
                    if b == 2:
                        c1_out(m, 0)
                c1_out(m, 1)
                a3_ctx(g)
                a3_k1(g)
                a3_o0(g)
                a3_v1(g)
                c2_oT(m)
                normalize(1, x1, g)
                c2_ln(m)
                c2_t(m)
                c2_router(m)
                c2_exp(m)
                normalize(2, x2, g)
                c2_silu(m, 0)
                a3_t2(g)
                c2_w(m)
                c2_silu(m, 1)
                a3_q1(g)
                for i in range(2, NB):
                    c2_silu(m, i)

            def stage_c(m):
                for u in range(16):
                    c1_exp(m, u)
                    if u == 11:
                        c1_out(m, 0)
                c1_out(m, 1)
                c2_oT(m)
                c2_ln(m)
                c2_t(m)
                c2_router(m)
                c2_exp(m)
                c2_silu(m, 0)
                c2_w(m)
                for i in range(1, NB):
                    c2_silu(m, i)

            skewed(act, stage_a, both, stage_c)

        @block.vector
        def _(dve):
            v = nc.vector

            def wfull(use, g):
                dve.wait_ge(full[BANK_OF[use]], upto(g, use))

            def stats(i, src, g):
                for b in range(GB):
                    ins = v.bn_stats(lnst[i][:, b], src[:, b])
                ins.then_inc(ln[i]["stats"], 1)
                dve.wait_ge(ln[i]["stats"], g + 1)
                v.memset(pause[:], 0.0)
                for b in range(GB):
                    ins = v.bn_aggr(lnmv[i][:, b], lnst[i][:, b])
                ins.then_inc(ln[i]["mv"], 1)
                dve.wait_ge(ln[i]["mv"], g + 1)
                v.tensor_scalar(lnve[i][:], lnmv[i][:, :, 1], EPS, None, ALU.add).then_inc(ln[i]["var"], 1)

            def shift(i, g):
                dve.wait_ge(ln[i]["rstd"], g + 1)
                v.scalar_tensor_tensor(out=lnnm[i][:], in0=lnmv[i][:, :, 0], scalar=-1.0, in1=lnrs[i][:],
                                       op0=ALU.mult, op1=ALU.mult).then_inc(ln[i]["shift"], 1)

            def a1_mask(g):
                dve.wait_ge(s_mk, 16 * g + 16)
                wait(dve, mk["diag"], g)
                v.tensor_copy(mrow[:], mk8[:]).then_inc(mk["row"], 1)

            def a1_k(g):
                wfull("K0", g)
                wait(dve, biased0, GB * g)
                v.tensor_copy(Kg0[0:64, 0], bank["A1"][0:64])
                v.tensor_copy(Kg0[64:128, 1], bank["A1"][64:128]).then_inc(drained["A1"], 1)

            def a2_max(g, b):
                dve.wait_ge(scored0, GB * g + b + 1)
                v.tensor_reduce(negM0[:], psA[:, :].rearrange("p (h q) -> p q h", h=H0), AX.X, ALU.max,
                                negate=True).then_inc(m0_ready, 1)

            def a2_norm(g, b):
                n = GB * g + b
                dve.wait_ge(hsum_ready, n + 1)
                if b >= 2 or not isinstance(g, int):
                    dve.wait_ge(attn0, n - 1)
                v.reciprocal(hrec[b % 2][:], hsum[b % 2][:]).then_inc(hrec_ready, 1)
                dve.wait_ge(hrec_ready, n + 1)
                e = E0[b % 2]
                v.tensor_tensor(e[:], e[:], hrec[b % 2][:].unsqueeze(1).to_broadcast([128, H0, S]), ALU.mult).then_inc(attn0, 1)

            def a3_fill(g):
                if not isinstance(g, int):
                    dve.wait_ge(drained["A0"], upto(g - 1, "V1"))
                    dve.wait_ge(full["A0"], upto(g - 1, "cfT"))
                v.tensor_copy(mkeep4[:], mkeep[:, bass.ts(g, GB)])
                v.tensor_copy(mfill4[:], mfill[:, bass.ts(g, GB)]).then_inc(mk["four"], 1)
                dve.wait_ge(mk["four"], g + 1)
                dve.wait_ge(mk["diag"], g + 1)
                for b in range(GB):
                    v.scalar_tensor_tensor(out=fill[:, b], in0=omk[:, b], scalar=mfill4[:, b:b + 1], in1=mdiag[:, b],
                                           op0=ALU.mult, op1=ALU.add).then_inc(mk["fill"], 1)

            def a3_sums(g):
                if not isinstance(g, int):
                    dve.wait_ge(full["D"], upto(g - 1, "AV23"))
                dst = bass.AP(tensor=VS1[:].tensor, offset=32, ap=[[GB * H1 * 64, 128], [H1 * 64, GB], [256, 4], [65, 4]])
                src = mkeep4[:].unsqueeze(2).unsqueeze(3).to_broadcast([128, GB, 4, 4])
                v.tensor_copy(dst, src).then_inc(ones1_ready, 1)

            def a3_k1(g):
                wfull("K1", g)
                wait(dve, kg1_dma, 64 * g)
                v.tensor_scalar(Kd1[:], bank["A1"], const("bk1"), None, ALU.add).then_inc(kd1_ready, 1)

            def a3_x1(g):
                wfull("O0p", g)
                v.tensor_tensor(x1[:], bank3("A0"), xin[:], ALU.add).then_inc(drained["A0"], 1)
                dve.wait_ge(drained["A0"], upto(g, "O0p"))
                stats(1, x1, g)

            def a3_quant(g):
                dve.wait_ge(ln[1]["out"], g + 1)
                v.tensor_reduce(amax[:], lnx[1][:], AX.X, ALU.max, apply_absolute_value=True).then_inc(q_amax, 1)
                dve.wait_ge(q_amax, g + 1)
                v.tensor_scalar(lscale[:], amax[:], 1e-12, INV127, ALU.max, ALU.mult).then_inc(q_scale, 1)
                dve.wait_ge(q_scale, g + 1)
                v.reciprocal(lrec[:], lscale[:]).then_inc(q_rec, 1)
                dve.wait_ge(q_rec, g + 1)
                for b in range(GB):
                    ins = v.tensor_scalar(qz[:, b], lnx[1][:, b], lrec[:, b:b + 1], MAGIC, ALU.mult, ALU.add)
                ins.then_inc(q_int, 1)

            def a3_qT(g):
                wfull("qT", g)
                v.tensor_scalar(qT[:], bank["A1"], -MAGIC, None, ALU.add).then_inc(drained["A1"], 1)

            def a3_x2(g):
                wfull("qmm", g)
                for b in range(GB):
                    ins = v.scalar_tensor_tensor(out=qres[:, b], in0=bank3("A0")[:, b], scalar=lscale[:, b:b + 1],
                                                 in1=rscale[:], op0=ALU.mult, op1=ALU.mult)
                ins.then_inc(drained["A0"], 1)
                dve.wait_ge(drained["A0"], upto(g, "qmm"))
                wait(dve, xb_ready, g)
                v.tensor_tensor(x2[:], x1[:], qres[:], ALU.add).then_inc(x2_ready, 1)
                dve.wait_ge(x2_ready, g + 1)
                stats(2, x2, g)

            def a3_q1(g):
                wfull("Q1", g)
                wait(dve, qg1_dma, 64 * g)
                v.tensor_scalar(Qd1[:], bank["A0"], const("bq1"), None, ALU.add).then_inc(qd1_ready, 1)

            def b_max(m, u):
                use = f"max{u}"
                wfull(use, m)
                v.tensor_reduce(negM1[:, 4 * u:4 * u + 4], bank[BANK_OF[use]].rearrange("p (j k) -> p j k", j=4), AX.X,
                                ALU.max, negate=True).then_inc(drained[BANK_OF[use]], 1)

            def b_mx(m):
                wfull("MT", m)
                src = bank["D"][0:64, 0:128].unsqueeze(1).to_broadcast([64, 4, 128])
                v.tensor_tensor(MX[0:64], src, maskM[0:64].unsqueeze(2).to_broadcast([64, 4, 128]),
                                ALU.mult).then_inc(drained["D"], 1)

            def c2_rec(m):
                for half in range(2):
                    use = f"TO{half}"
                    wfull(use, m)
                    ps = bank[BANK_OF[use]].rearrange("p (n c) -> p n c", n=8)
                    v.reciprocal(Rq[:, half], ps[:, :, 32:36]).then_inc(rec1, 1)
                for half in range(2):
                    use = f"TO{half}"
                    ps = bank[BANK_OF[use]].rearrange("p (n c) -> p n c", n=8)
                    dve.wait_ge(rec1, 2 * m + half + 1)
                    out = Oq[:, 2 * half:2 * half + 2].rearrange("p b (n j d) -> p (b n) j d", j=4, d=DH1)
                    v.tensor_tensor(out, ps[:, :, 0:32].rearrange("p n (j d) -> p n j d", j=4),
                                    Rq[:, half].unsqueeze(3).to_broadcast([128, 8, 4, DH1]),
                                    ALU.mult).then_inc(drained[BANK_OF[use]], 1)

            def c2_x3(m):
                wfull("O1p", m)
                dve.wait_ge(xb_ready, m + 1)
                v.tensor_tensor(x3[:], bank3("C3"), xb[:], ALU.add).then_inc(drained["C3"], 1)
                dve.wait_ge(drained["C3"], upto(m, "O1p"))
                stats(3, x3, m)

            def c2_t(m):
                dve.wait_ge(t3h_ready, m + 1)
                v.tensor_tensor(T3l[:], bank["C0"], T3h[:].bitcast(F32), ALU.subtract).then_inc(drained["C0"], 1)

            def c2_soft(m):
                wfull("lgT", m)
                lg = bank3("C2")[:, :, 0:NE]
                v.tensor_reduce(tk["nmax"][:], lg, AX.X, ALU.max, negate=True).then_inc(tks["max"], 1)
                dve.wait_ge(tks["max"], m + 1)
                v.tensor_tensor(tke[:], lg, tk["nmax"][:].unsqueeze(2).to_broadcast([128, GB, NE]), ALU.add)\
                    .then_inc(drained["C2"], 1)

            def c2_topk(m):
                dve.wait_ge(tks["exp"], m + 1)
                v.tensor_reduce(tk["sum"][:], tke[:], AX.X, ALU.add).then_inc(tks["sum"], 1)
                dve.wait_ge(tks["sum"], m + 1)
                v.reciprocal(tk["rec"][:], tk["sum"][:]).then_inc(tks["rec"], 1)
                dve.wait_ge(tks["rec"], m + 1)
                v.tensor_tensor(tkp[:], tke[:], tk["rec"][:].unsqueeze(2).to_broadcast([128, GB, NE]), ALU.mult)\
                    .then_inc(tks["p"], 1)
                dve.wait_ge(tks["p"], m + 1)
                pj = tkp[:].unsqueeze(2).to_broadcast([128, GB, NE, NE])
                pi = tkp[:].unsqueeze(3).to_broadcast([128, GB, NE, NE])
                v.tensor_tensor(gt[:], pj, pi, ALU.is_gt)
                v.tensor_tensor(ge[:], pj, pi, ALU.is_ge).then_inc(tks["ge"], 1)

            def c2_keep(m):
                dve.wait_ge(tks["mix"], m + 1)
                v.tensor_tensor(gt[:], gt[:], gmix[:], ALU.max).then_inc(tks["max2"], 1)
                dve.wait_ge(tks["max2"], m + 1)
                v.tensor_reduce(rank[:], gt[:], AX.X, ALU.add).then_inc(tks["rank"], 1)
                dve.wait_ge(tks["rank"], m + 1)
                v.scalar_tensor_tensor(out=Wt[:], in0=rank[:], scalar=TOPK - 0.5, in1=tkp[:], op0=ALU.is_lt,
                                       op1=ALU.mult).then_inc(tks["w"], 1)

            def c2_w(m):
                dve.wait_ge(wxh_ready, m + 1)
                v.tensor_tensor(Wx[32:32 + NE, :], bank["C3"][0:NE, :], Wx[0:NE, :].bitcast(F32),
                                ALU.subtract).then_inc(drained["C3"], 1)

            def c2_hidden(m, i):
                n = NB * m + i
                bG, bU = BANK_OF[f"G{i}"], BANK_OF[f"U{i}"]
                dve.wait_ge(drained[bG], upto(m, f"G{i}"))
                wfull(f"U{i}", m)
                if i == 0:
                    v.tensor_tensor(hid[0][:], sg[0][:], bank[bU], ALU.mult).then_inc(drained[bU], 1)
                    return
                v.tensor_tensor(gu[i % 2][:], sg[i % 2][:], bank[bU], ALU.mult).then_inc(drained[bU], 1)
                wfull(f"W{i - 1}", m)
                dve.wait_ge(drained[bU], upto(m, f"U{i}"))
                if i >= 2:
                    dve.wait_ge(down_done, n - 1)
                v.tensor_tensor(hid[i % 2][:], gu[i % 2][:], bank["D"], ALU.mult).then_inc(drained["D"], 1)

            def c2_out(m):
                dve.wait_ge(down_done, NB * m + NB)
                dve.wait_ge(s_out, 16 * m + 1)
                v.tensor_tensor(y3[:], bank3("O"), x3[:], ALU.add).then_inc(y_drained, 1)

            def setup():
                dve.wait_ge(s_mask, 16)
                v.tensor_copy(mf[:], m8[:]).then_inc(cst["mf"], 1)
                dve.wait_ge(cst["psT"], 1)
                v.tensor_copy(mcol[:], bank["C0"][:, 0:B]).then_inc(cst["mcol"], 1)
                dve.wait_ge(cst["psN"], 1)
                dve.wait_ge(cst["mcol"], 1)
                v.tensor_scalar(mtmp[:, 0], bank["C1"][:, 0:B], 1.0, None, ALU.max).then_inc(cst["mtmp"], 1)
                v.tensor_scalar(mtmp[:, 2], bank["C1"][:, 0:B], 0.5, None, ALU.is_lt).then_inc(cst["mtmp"], 1)
                dve.wait_ge(cst["mtmp"], 2)
                v.reciprocal(mtmp[:, 1], mtmp[:, 0]).then_inc(cst["mtmp"], 1)
                v.tensor_tensor(mkeep[:], mcol[:], mtmp[:, 2], ALU.add).then_inc(cst["masks"], 1)
                dve.wait_ge(cst["mtmp"], 3)
                v.tensor_tensor(mfill[:], mcol[:], mtmp[:, 1], ALU.mult).then_inc(cst["masks"], 1)
                dve.wait_ge(cst["masks"], 2)

            def setup2():
                dve.wait_ge(s_pack[1], 16)
                for j in range(4):
                    v.tensor_tensor(bq1m[:, j:j + 1], mask1[:, j:j + 1], const("bq1"), ALU.mult)
                    v.tensor_tensor(bk1m[:, j:j + 1], mask1[:, j:j + 1], const("bk1"), ALU.mult)
                v.tensor_reduce(rtmp[:, 0:1], const("rhsT"), AX.X, ALU.max, apply_absolute_value=True).then_inc(cst["rq"], 1)
                dve.wait_ge(cst["rq"], 1)
                v.tensor_scalar(rtmp[:, 1:2], rtmp[:, 0:1], 1e-12, INV127, ALU.max, ALU.mult).then_inc(cst["rq"], 1)
                dve.wait_ge(cst["rq"], 2)
                v.reciprocal(rtmp[:, 2:3], rtmp[:, 1:2]).then_inc(cst["rq"], 1)
                dve.wait_ge(cst["rq"], 3)
                v.tensor_scalar(rq[:, 0], const("rhsT"), rtmp[:, 2:3], MAGIC, ALU.mult, ALU.add).then_inc(cst["rq"], 1)
                v.tensor_copy(rq[:, 1], rtmp[:, 1:2].to_broadcast([128, 128])).then_inc(cst["rq"], 1)
                v.tensor_copy(y3[:, 0], const("bv1").to_broadcast([128, 128])).then_inc(cst["rq"], 1)
                dve.wait_ge(cst["psR"], 1)
                v.tensor_scalar(rhsq[:], bank["C2"][:, 0:128], -MAGIC, None, ALU.add)
                v.tensor_copy(rscale[:], bank["C2"][:, 128:256])
                v.tensor_tensor(cb1[:], bank["C2"][:, 256:384], const("bo1"), ALU.add).then_inc(cst["cb"], 1)

            def setup3():
                dve.wait_ge(s_pack[2], 16)
                dve.wait_ge(cst["whi"], 1)
                v.tensor_tensor(routerL[:], const("router"), routerH[:].bitcast(F32), ALU.subtract)
                dve.wait_ge(s_pack[3], 32)
                v.tensor_tensor(guL[:].rearrange("p k c f -> p (k c f)"), raw_gu,
                                guH[:].rearrange("p k c f -> p (k c f)").bitcast(F32), ALU.subtract).then_inc(cst["wlo"], 1)

            def stage_a(g):
                dve.wait_ge(s_pack[0], 16)
                dve.wait_ge(s_x, 16)
                stats(0, xin, g)
                a1_mask(g)
                setup()
                shift(0, g)
                dve.wait_ge(zeroed, 10)
                a1_k(g)
                a3_fill(g)
                a3_sums(g)
                a2_max(g, 0)
                setup2()
                for b in range(1, GB):
                    a2_max(g, b)
                    a2_norm(g, b - 1)
                a2_norm(g, GB - 1)
                a3_k1(g)
                a3_x1(g)
                setup3()
                shift(1, g)
                a3_quant(g)
                a3_qT(g)
                a3_x2(g)
                shift(2, g)
                a3_q1(g)

            def both(g):
                m = g - 1
                dve.wait_ge(s_x, 16 * g + 16)
                stats(0, xin, g)
                a1_mask(g)
                for u in range(3):
                    b_max(m, u)
                shift(0, g)
                for u in range(3, 9):
                    b_max(m, u)
                a1_k(g)
                for u in range(9, 16):
                    b_max(m, u)
                b_mx(m)
                for b in range(GB):
                    a2_max(g, b)
                    if b > 0:
                        a2_norm(g, b - 1)
                a2_norm(g, GB - 1)
                a3_fill(g)
                a3_k1(g)
                a3_sums(g)
                c2_rec(m)
                a3_x1(g)
                shift(1, g)
                c2_x3(m)
                a3_quant(g)
                shift(3, m)
                a3_qT(g)
                c2_t(m)
                a3_x2(g)
                c2_soft(m)
                shift(2, g)
                c2_topk(m)
                c2_hidden(m, 0)
                c2_keep(m)
                c2_w(m)
                a3_q1(g)
                for i in range(1, NB):
                    c2_hidden(m, i)
                c2_out(m)

            def stage_c(m):
                for u in range(16):
                    b_max(m, u)
                b_mx(m)
                c2_rec(m)
                c2_x3(m)
                shift(3, m)
                c2_t(m)
                c2_soft(m)
                c2_topk(m)
                c2_hidden(m, 0)
                c2_keep(m)
                c2_w(m)
                for i in range(1, NB):
                    c2_hidden(m, i)
                c2_out(m)

            skewed(dve, stage_a, both, stage_c)

        @block.tensor
        def _(pe):
            t = nc.tensor

            def claim(use, g):
                bk = BANK_OF[use]
                if bk in ("A0", "A1") or BANK_USES[bk].index(use) > 0:
                    wait(pe, drained[bk], upto(g, use) - 1)
                return bank[bk]

            def done(ins, use):
                ins.then_inc(full[BANK_OF[use]], 1)

            def wdrained(use, g):
                pe.wait_ge(drained[BANK_OF[use]], upto(g, use))

            def turn(use, src, g):
                ps = claim(use, g)
                for b in range(GB):
                    ins = t.transpose(ps[:, 128 * b:128 * b + 128], src[:, b], ident)
                done(ins, use)

            def project(use, w, xT, g):
                ps = claim(use, g)
                done(t.matmul(ps, w, xT, start=True, stop=True), use)

            def a1(g):
                pe.wait_ge(ln[0]["out"], g + 1)
                turn("lnT0", lnx[0], g)
                pe.wait_ge(s_ctx, 16 * g + 16)
                turn("ctxT", ctx, g)

            def a1_p(g):
                wdrained("lnT0", g)
                project("Q0", const("wq0"), lnT0[:], g)
                wdrained("ctxT", g)
                project("K0", const("wk0"), ctxT[:], g)

            def a1_v(g):
                ps = claim("V0", g)
                for b in range(GB):
                    ins = t.matmul(ps[:, 128 * b:128 * b + 128], ctxT[:, 128 * b:128 * b + 128], const("wv01")[:, 0:128],
                                   start=True, stop=True)
                done(ins, "V0")

            def a2_scores(g, b):
                n = GB * g + b
                if b == 0:
                    pe.wait_ge(drained["A0"], upto(g, "V0"))
                    pe.wait_ge(drained["A1"], upto(g, "K0"))
                else:
                    pe.wait_ge(exp0, n)
                cols = slice(128 * b, 128 * b + 128)
                for k in range(2):
                    ins = t.matmul(psA[:, 512 * k:512 * k + 512], Kg0[:, k, cols], Qm0[:, :, cols], start=True, stop=True)
                ins.then_inc(scored0, 1)

            def a2_bias(g, b):
                n = GB * g + b
                pe.wait_ge(m0_ready, n + 1)
                mv = negM0[:].unsqueeze(1).to_broadcast([128, 4, S])
                for k in range(2):
                    ins = t.matmul(psA[:, 512 * k:512 * k + 512], identr[:], mv, start=False, stop=True,
                                   skip_group_check=True)
                ins.then_inc(biased0, 1)

            def a2_av(g, b):
                n = GB * g + b
                pe.wait_ge(attn0, n + 1)
                if b == 0:
                    wait(pe, o0_drained, g)
                cols = slice(128 * b, 128 * b + 128)
                for j in range(2):
                    for p in range(4):
                        ins = t.matmul(bank["O"][32 * p:32 * p + 32, cols], Vm0[:, b, 2 * p + j, :], E0[b % 2][:, 2 * p + j, :],
                                       start=(j == 0), stop=(j == 1), tile_position=(0, 32 * p))
                ins.then_inc(av0, 1)

            def a3_ctx(g):
                pe.wait_ge(mk["fill"], GB * g + GB)
                pe.wait_ge(exp0, GB * g + GB)
                ps = claim("cfT", g)
                for b in range(GB):
                    ins = t.matmul(ps[:, 128 * b:128 * b + 128], ctx[:, b], fill[:, b], start=True, stop=True)
                done(ins, "cfT")

            def a3_k1(g):
                wdrained("cfT", g)
                project("K1", const("wk1"), cfT[:], g)

            def a3_v1(g):
                ps = claim("V1", g)
                for b in range(GB):
                    ins = t.matmul(ps[:, 128 * b:128 * b + 128], ctxT[:, 128 * b:128 * b + 128],
                                   const("wv01")[:, 128:256], start=True, stop=True)
                done(ins, "V1")

            def a3_o0(g):
                pe.wait_ge(o0_drained, g + 1)
                ps = claim("O0p", g)
                for b in range(GB):
                    ins = t.matmul(ps[:, 128 * b:128 * b + 128], O0T[:, 128 * b:128 * b + 128], const("wo0"),
                                   start=True, stop=True)
                done(ins, "O0p")

            def a3_qT(g):
                pe.wait_ge(q_int, g + 1)
                turn("qT", qz, g)

            def a3_qmm(g):
                wdrained("qT", g)
                ps = claim("qmm", g)
                for b in range(GB):
                    ins = t.matmul(ps[:, 128 * b:128 * b + 128], qT[:, 128 * b:128 * b + 128], rhsq[:], start=True, stop=True)
                done(ins, "qmm")

            def a3_t2(g):
                pe.wait_ge(ln[2]["out"], g + 1)
                turn("lnT2", lnx[2], g)

            def a3_q1(g):
                wdrained("lnT2", g)
                project("Q1", const("wq1"), lnT2[:], g)

            def b_scores(m, u):
                b, G = divmod(u, 4)
                cols = slice(128 * b, 128 * b + 128)
                if u == 0:
                    pe.wait_ge(qg1_dma, 64 * m + 64)
                    wdrained("K1", m)
                ps = claim(f"max{u}", m)
                done(t.matmul(ps, Qg1[:, G, cols], Km1[:, :, cols], start=True, stop=True), f"max{u}")

            def b_turn(m):
                for u in (12, 13, 14, 15):
                    wdrained(f"max{u}", m)
                ps = claim("MT", m)
                done(t.transpose(ps[:, 0:128], negM1[:], ident), "MT")

            def c1_scores(m, u):
                b, G = divmod(u, 4)
                cols = slice(128 * b, 128 * b + 128)
                if u == 0:
                    pe.wait_ge(kg1_dma, 64 * m + 64)
                    wdrained("Q1", m)
                    wdrained("MT", m)
                ps = claim(f"s{u}", m)
                t.matmul(ps, Kg1[:, G, cols], Qm1[:, :, cols], start=True, stop=False)
                done(t.matmul(ps, selM[:, u], MX[:].rearrange("p j q -> p (j q)"), start=False, stop=True), f"s{u}")

            def c1_av(m, b):
                for u in range(4 * b + 1, 4 * b + 4):
                    wdrained(f"s{u}", m)
                use = ("AV01", "AV23")[b // 2]
                if b == 0:
                    pe.wait_ge(ones1_ready, m + 1)
                    wdrained("V1", m)
                if b % 2 == 0:
                    claim(use, m)
                for w in range(2):
                    cols = slice(256 * (b % 2) + 128 * w, 256 * (b % 2) + 128 * w + 128)
                    for j in range(4):
                        for k in range(2):
                            G = 2 * w + k
                            ins = t.matmul(bank[BANK_OF[use]][64 * k:64 * k + 64, cols], VS1[:, b, 4 * G + j, :],
                                           E1[b % 2][:, G, j, :], start=(j == 0), stop=(j == 3), tile_position=(0, 64 * k))
                if b % 2:
                    done(ins, use)
                else:
                    ins.then_inc(av_even, 1)

            def c2_back(m, half):
                wdrained(("AV01", "AV23")[half], m)
                use = f"TO{half}"
                ps = claim(use, m)
                for n in range(4):
                    ins = t.transpose(ps[:, 128 * n:128 * n + 128], OU[:, 2 * half + n // 2, n % 2], ident)
                done(ins, use)

            def c2_oT(m):
                wdrained("TO0", m)
                wdrained("TO1", m)
                turn("OT", Oq, m)

            def c2_o(m):
                wdrained("OT", m)
                ps = claim("O1p", m)
                for b in range(GB):
                    ins = t.matmul(ps[:, 128 * b:128 * b + 128], O1T[:, 128 * b:128 * b + 128], const("wo1"),
                                   start=True, stop=True)
                done(ins, "O1p")

            def c2_t(m):
                pe.wait_ge(ln[3]["out"], m + 1)
                turn("T3", lnx[3], m)

            def split_product(ps, wh, wl):
                t.matmul(ps, wh, T3h[:], start=True, stop=False)
                t.matmul(ps, wl, T3h[:], start=False, stop=False)
                return t.matmul(ps, wh, T3l[:], start=False, stop=True)

            def c2_router(m):
                wdrained("T3", m)
                ps = claim("lg", m)
                done(split_product(ps[0:NE, :], routerH[:], routerL[:]), "lg")

            def c2_lgT(m):
                wdrained("lg", m)
                ps = claim("lgT", m)
                for b in range(GB):
                    ins = t.transpose(ps[:, 128 * b:128 * b + 128], lgs[:, 128 * b:128 * b + 128], ident)
                done(ins, "lgT")

            def c2_wT(m):
                pe.wait_ge(tks["w"], m + 1)
                ps = claim("WtT", m)
                for b in range(GB):
                    ins = t.transpose(ps[0:NE, 128 * b:128 * b + 128], Wt[:, b], ident)
                done(ins, "WtT")

            def c2_up(m, i):
                c = (i - 1) % NB
                for k, nm in ((0, f"G{i}"), (1, f"U{i}")):
                    done(split_product(claim(nm, m), guH[:, k, c], guL[:, k, c]), nm)

            def c2_w(m, i):
                if i == 1:
                    wdrained("WtT", m)
                ps = claim(f"W{i - 1}", m)
                done(t.matmul(ps, selW[:, i - 1], Wx[:], start=True, stop=True), f"W{i - 1}")

            def c2_down(m, i):
                c = (i - 1) % NB
                if i == 0:
                    wdrained("U0", m)
                    pe.wait_ge(o0_drained, m + 2 if not isinstance(m, int) else NG)
                else:
                    wdrained(f"W{i - 1}", m)
                for b in range(GB):
                    ins = t.matmul(bank["O"][:, 128 * b:128 * b + 128], hid[i % 2][:, 128 * b:128 * b + 128], down[:, c, :],
                                   start=(i == 0 and b == 0), stop=(i == NB - 1), skip_group_check=True)
                ins.then_inc(down_done, 1)

            def setup():
                pe.wait_ge(s_pack[0], 16)
                pe.wait_ge(cst["mf"], 1)
                t.transpose(bank["C0"][:, 0:B], mf[:], ident[0:B, 0:B]).then_inc(cst["psT"], 1)
                pe.wait_ge(cst["mcol"], 1)
                pe.wait_ge(cst["ones"], 1)
                t.matmul(bank["C1"][:, 0:B], ones[:], mcol[:], start=True, stop=True).then_inc(cst["psN"], 1)

            def setup2():
                pe.wait_ge(cst["rq"], 6)
                t.transpose(bank["C2"][:, 0:128], rq[:, 0], ident)
                t.transpose(bank["C2"][:, 128:256], rq[:, 1], ident)
                t.matmul(bank["C2"][:, 256:384], y3[:, 0], const("wo1"), start=True, stop=True).then_inc(cst["psR"], 1)

            def stage_a(g):
                setup()
                a1(g)
                a1_p(g)
                a1_v(g)
                pe.wait_ge(cst["act"], 1)
                for b in range(GB):
                    a2_scores(g, b)
                    a2_bias(g, b)
                    if b == 0:
                        setup2()
                    if b > 0:
                        a2_av(g, b - 1)
                a3_ctx(g)
                a2_av(g, GB - 1)
                pe.wait_ge(s_pack[1], 16)
                a3_k1(g)
                a3_v1(g)
                a3_o0(g)
                a3_qT(g)
                a3_qmm(g)
                a3_t2(g)
                a3_q1(g)
                pe.wait_ge(cst["wlo"], 1)

            def both(g):
                m = g - 1
                for u in range(4):
                    b_scores(m, u)
                a1(g)
                for u in range(4, 8):
                    b_scores(m, u)
                a1_p(g)
                for u in range(8, 12):
                    b_scores(m, u)
                a1_v(g)
                for u in range(12, 16):
                    b_scores(m, u)
                a2_scores(g, 0)
                b_turn(m)
                for b in range(GB):
                    if b > 0:
                        a2_scores(g, b)
                    c1_scores(m, 4 * b)
                    c1_scores(m, 4 * b + 1)
                    a2_bias(g, b)
                    c1_scores(m, 4 * b + 2)
                    if b > 0:
                        a2_av(g, b - 1)
                    c1_scores(m, 4 * b + 3)
                    if b > 0:
                        c1_av(m, b - 1)
                c2_back(m, 0)
                c1_av(m, GB - 1)
                a3_ctx(g)
                a2_av(g, GB - 1)
                c2_back(m, 1)
                a3_k1(g)
                a3_v1(g)
                c2_oT(m)
                a3_o0(g)
                c2_o(m)
                a3_qT(g)
                c2_t(m)
                a3_qmm(g)
                c2_router(m)
                c2_lgT(m)
                a3_t2(g)
                c2_up(m, 0)
                c2_down(m, 0)
                c2_wT(m)
                a3_q1(g)
                c2_up(m, 1)
                for i in range(1, NB):
                    c2_w(m, i)
                    if i + 1 < NB:
                        c2_up(m, i + 1)
                    c2_down(m, i)

            def stage_c(m):
                for u in range(16):
                    b_scores(m, u)
                b_turn(m)
                for b in range(GB):
                    for u in range(4):
                        c1_scores(m, 4 * b + u)
                    if b > 0:
                        c1_av(m, b - 1)
                c2_back(m, 0)
                c1_av(m, GB - 1)
                c2_back(m, 1)
                c2_oT(m)
                c2_o(m)
                c2_t(m)
                c2_router(m)
                c2_lgT(m)
                c2_up(m, 0)
                c2_down(m, 0)
                c2_wT(m)
                c2_up(m, 1)
                for i in range(1, NB):
                    c2_w(m, i)
                    if i + 1 < NB:
                        c2_up(m, i + 1)
                    c2_down(m, i)

            skewed(pe, stage_a, both, stage_c)


_INS = ["x", "ctx", "mask", "pack"]


def kernel(x, ctx_1024, mask_BxS2_bf1, L0_xattn_W_Q, L0_xattn_W_K, L0_xattn_W_V, L0_xattn_W_O, L0_ffn_rhs,
           L1_xattn_Wq, L1_xattn_bq, L1_xattn_Wk, L1_xattn_bk, L1_xattn_Wv, L1_xattn_bv, L1_xattn_Wo, L1_xattn_bo,
           L1_ffn_router_w, L1_ffn_w_gate, L1_ffn_w_up, L1_ffn_w_down, L1_ffn_ws_gate, L1_ffn_ws_up, L1_ffn_ws_down):
    import concourse.bacc as bacc
    from concourse.bass_utils import run_bass_kernel_spmd

    def arr(a):
        return np.asarray(a)

    def experts_in(w, ws):
        return np.concatenate([arr(w).transpose(1, 0, 2).reshape(D, NE * FE), arr(ws)], axis=1)

    def experts_out(w, ws):
        return np.concatenate([arr(w).reshape(NC, 128, D), arr(ws)[None]], axis=0).transpose(1, 0, 2).reshape(128, NB * D)

    p = np.arange(128)
    j4 = np.arange(4)
    e8 = np.arange(NE)
    f = np.float32
    parts = {
        "ident": np.eye(128, dtype=f),
        "wq0": arr(L0_xattn_W_Q).T, "wk0": arr(L0_xattn_W_K).T,
        "wv01": np.concatenate([arr(L0_xattn_W_V).T, arr(L1_xattn_Wv).T], axis=1),
        "mask0": (p[:, None] // DH0 % 4 == j4).astype(f), "mask1": (p[:, None] // DH1 % 4 == j4).astype(f),
        "bq1": arr(L1_xattn_bq)[:, None], "bk1": arr(L1_xattn_bk)[:, None], "bv1": arr(L1_xattn_bv)[:, None],
        "wo0": arr(L0_xattn_W_O).T, "rhsT": arr(L0_ffn_rhs).T,
        "wq1": arr(L1_xattn_Wq).T, "wk1": arr(L1_xattn_Wk).T, "wo1": arr(L1_xattn_Wo).T,
        "bo1": np.broadcast_to(arr(L1_xattn_bo), (128, D)),
        "maskM": (p[:, None] % 4 == j4).astype(f),
        "tri": np.broadcast_to((e8[None, :] < e8[:, None]).astype(f).reshape(1, NE * NE), (128, NE * NE)),
        "router": arr(L1_ffn_router_w),
        "gate": experts_in(L1_ffn_w_gate, L1_ffn_ws_gate), "up": experts_in(L1_ffn_w_up, L1_ffn_ws_up),
        "down": experts_out(L1_ffn_w_down, L1_ffn_ws_down),
        "selM": np.repeat((p[:, None] // 4 == np.arange(4 * GB)).astype(f)[:, :, None], 128, axis=2).reshape(128, -1),
        "selW": ((p[:, None, None] % 32 == 2 * np.arange(NC)[None, :, None] + (p // FE)[None, None, :])
                 & (p[:, None, None] < 64)).astype(f).reshape(128, -1),
    }
    arrays = {
        "x": np.ascontiguousarray(arr(x)),
        "ctx": np.ascontiguousarray(arr(ctx_1024)),
        "mask": np.ascontiguousarray(arr(mask_BxS2_bf1)).view(np.uint8),
        "pack": np.ascontiguousarray(np.concatenate([parts[n] for n, _ in PACK], axis=1)),
    }
    nc = bacc.Bacc("TRN2", target_bir_lowering=False, num_devices=1)
    ins = [nc.dram_tensor("in_" + n, arrays[n].shape, mybir.dt.from_np(arrays[n].dtype), kind="ExternalInput").ap() for n in _INS]
    out = nc.dram_tensor("out", (B, S, D), F32, kind="ExternalOutput").ap()
    build(nc, *ins, out)
    r = run_bass_kernel_spmd(nc, [{"in_" + n: a for n, a in arrays.items()}], core_ids=[0])
    return r.results[0]["out"]
```

```python
from contextlib import ExitStack

import numpy as np

import concourse.bass as bass
from concourse import mybir

F32 = mybir.dt.float32
F32R = mybir.dt.float32r
BF16 = mybir.dt.bfloat16
U8 = mybir.dt.uint8
ALU = mybir.AluOpType
ACT = mybir.ActivationFunctionType
AX = mybir.AxisListType

B, S, D = 16, 128, 128
GB = 4
NG = B // GB
T = GB * S
H0, DH0 = 8, 16
H1, DH1 = 16, 8
NE, FE, FS = 8, 64, 128
NC = NE * FE // 128
NB = NC + 1
TOPK = 6
EPS = 1e-5
MAGIC = 12582912.0
INV127 = float(np.float32(1.0) / np.float32(127.0))
SCALE1 = float(np.float32(1.0) / np.sqrt(np.float32(DH1)))

PACK = [("ident", 128), ("wq0", 128), ("wk0", 128), ("wv01", 256), ("mask0", 4), ("mask1", 4),
        ("bq1", 1), ("bk1", 1), ("bv1", 1), ("wo0", 128), ("rhsT", 128), ("wq1", 128), ("wk1", 128), ("wo1", 128),
        ("bo1", 128), ("maskM", 4), ("tri", 64), ("rowM", GB * 4),
        ("router", 8), ("down", NB * 128),
        ("selW", NC * 128), ("gate", NB * 128), ("up", NB * 128)]
COL = {}
_at = 0
for _n, _w in PACK:
    COL[_n] = (_at, _at + _w)
    _at += _w
NPACK = _at
KEPT = COL["selW"][0]
SPLITS = [COL["wo0"][0], COL["router"][0], KEPT]

BANK_USES = {
    "A0": ["lnT0", "Q0", "V0", "cfT", "O0p", "V1", "qmm", "Q1"],
    "A1": ["ctxT", "K0", "K1", "qT", "lnT2"],
    "C0": [f"max{u}" for u in range(0, 16, 4)] + [f"s{u}" for u in range(0, 16, 3)] + ["TO0", "T3", "G0", "G2", "G4"],
    "C1": [f"max{u}" for u in range(1, 16, 4)] + [f"s{u}" for u in range(1, 16, 3)] + ["TO1", "lg", "G1", "G3"],
    "C2": [f"max{u}" for u in range(2, 16, 4)] + [f"s{u}" for u in range(2, 16, 3)] + ["OT", "lgT", "U0", "U2", "U4"],
    "C3": [f"max{u}" for u in range(3, 16, 4)] + ["AV01", "O1p", "U1", "U3"],
    "D": ["MT", "AV23", "WtT", "W0", "W1", "W2", "W3"],
}
BANK_OF = {use: bank for bank, uses in BANK_USES.items() for use in uses}


def upto(g, use):
    uses = BANK_USES[BANK_OF[use]]
    return g * len(uses) + uses.index(use) + 1


def first_group(g):
    return isinstance(g, int) and g == 0


def wait(eng, sem, value):
    if not (isinstance(value, int) and value <= 0):
        eng.wait_ge(sem, value)


def build(nc, x_d, ctx_d, mask_d, pack_d, out_d):
    with ExitStack() as stack:
        def sb(name, shape, dt=F32):
            return stack.enter_context(nc.sbuf_tensor(name, shape, dt))

        def sem(name):
            return stack.enter_context(nc.semaphore(name))

        pack = sb("pack", [128, KEPT])

        def const(name):
            return pack[:, COL[name][0]:COL[name][1]]

        ident, mask0, mask1, maskM = const("ident"), const("mask0"), const("mask1"), const("maskM")
        down = const("down").rearrange("p (c d) -> p c d", c=NB)
        identr = sb("identr", [128, 128], F32R)
        rowM = sb("rowM", [128, GB * 4], F32R)
        selW = sb("selW", [128, NC, 128], F32R)
        routerH, routerL = sb("routerH", [128, NE], F32R), sb("routerL", [128, NE], F32R)
        guH = sb("guH", [128, 2, NB, 128], F32R)
        guL = sb("guL", [128, 2, NB, 128], F32R)
        rhsq = sb("rhsq", [128, 128], BF16)
        rscale = sb("rscale", [128, 128])
        rq = sb("rq", [128, 2, 128])
        rtmp = sb("rtmp", [128, 4])
        cb1 = sb("cb1", [128, 128])
        ones = sb("ones", [128, 128])
        nhalf = sb("nhalf", [128, GB])
        m8 = sb("m8", [B, S], U8)
        mf = sb("mf", [B, S])
        mcol = sb("mcol", [128, B])
        mkeep = sb("mkeep", [128, B])
        mfill = sb("mfill", [128, B])
        mtmp = sb("mtmp", [128, 3, B])
        mkeep4, mfill4 = sb("mkeep4", [128, GB]), sb("mfill4", [128, GB])

        xin, ctx = sb("xin", [128, GB, D]), sb("ctx", [128, GB, D])
        mk8 = sb("mk8", [128, GB, S], U8)
        mrow, omk, mdiag, fill = (sb(n, [128, GB, S]) for n in ("mrow", "omk", "mdiag", "fill"))
        lnst = [sb(f"lnst{i}", [128, GB, 6]) for i in range(4)]
        lnmv = [sb(f"lnmv{i}", [128, GB, 2]) for i in range(4)]
        lnve, lnrs, lnnm = ([sb(f"{n}{i}", [128, GB]) for i in range(4)] for n in ("lnve", "lnrs", "lnnm"))
        lnx = [sb(f"lnx{i}", [128, GB, D]) for i in (0, 1, 3)]
        lnx.insert(2, lnx[0])
        lnT0, ctxT, cfT = (sb(n, [128, T]) for n in ("lnT0", "ctxT", "cfT"))
        lnT2 = lnT0
        Qm0 = sb("Qm0", [128, 4, T])
        Kg0 = sb("Kg0", [128, 2, T])
        Vm0 = sb("Vm0", [128, GB, H0, 32])
        negM0 = sb("negM0", [128, S], F32R)
        E0 = [sb(f"E0_{i}", [128, H0, S]) for i in range(2)]
        hs = sb("hs", [128, 6, S])
        hsum = [sb(f"hsum{i}", [128, S]) for i in range(2)]
        hrec = [sb(f"hrec{i}", [128, S]) for i in range(2)]
        O0T = sb("O0T", [128, T])
        x1, x2, xb, x3, y3 = (sb(n, [128, GB, D]) for n in ("x1", "x2", "xb", "x3", "y3"))
        amax, lscale, lrec = (sb(n, [128, GB]) for n in ("amax", "lscale", "lrec"))
        qz = sb("qz", [128, GB, D])
        qT = sb("qT", [128, T], BF16)
        qres = qz
        Kh1, Kl1, Qh1, Ql1 = (sb(n, [128, T], F32R) for n in ("Kh1", "Kl1", "Qh1", "Ql1"))
        KS1 = sb("KS1", [96, 4, T], F32R)
        QS1 = sb("QS1", [96, 2, 4, 4, S], F32R)
        Km1 = sb("Km1", [128, 4, T], F32R)
        Qg1 = sb("Qg1", [128, 4, T], F32R)
        VS1 = sb("VS1", [128, GB, H1, 64])
        negM1 = sb("negM1", [128, 128])
        pause = sb("pause", [128, 1])
        MX = sb("MX", [128, 4, S], F32R)
        E1 = [sb(f"E1_{i}", [128, 4, 4, S]) for i in range(2)]
        raw = E1[1][:].rearrange("p g j q -> p (g j q)")
        raw_sel, raw_gu = raw[:, 0:NC * 128], raw[:, NC * 128:(NC + 2 * NB) * 128]
        OU = sb("OU", [128, GB, 2, S])
        Rq = sb("Rq", [128, 2, 8, 4])
        Oq = sb("Oq", [128, GB, D])
        O1T = sb("O1T", [128, T])
        T3h, T3l = sb("T3h", [128, T], F32R), sb("T3l", [128, T], F32R)
        lgs = sb("lgs", [128, T])
        tk = {n: sb(f"tk_{n}", [128, GB]) for n in ("nmax", "sum", "rec")}
        tke, tkp, rank, Wt = (sb(n, [128, GB, NE]) for n in ("tke", "tkp", "rank", "Wt"))
        ge, gt, gmix = (sb(n, [128, GB, NE, NE]) for n in ("ge", "gt", "gmix"))
        Wx = sb("Wx", [128, T], F32R)
        sg = [sb(f"sg{i}", [128, T]) for i in range(2)]
        hid = [sb(f"hid{i}", [128, T]) for i in range(2)]

        psA = stack.enter_context(nc.psum_tensor("psA", [128, 1024], F32))
        bank = {"A0": psA[:, 0:512], "A1": psA[:, 512:1024]}
        for n in ("C0", "C1", "C2", "C3", "D", "O"):
            bank[n] = stack.enter_context(nc.psum_tensor("ps" + n, [128, 512], F32))[:, :]

        k_stack, q_stack = (nc.dram_tensor(n, (3 * D, T), F32).ap() for n in ("k_stack", "q_stack"))
        k_part, q_part = (a.rearrange("(p s) t -> s p t", s=3) for a in (k_stack, q_stack))

        full = {b: sem(f"full_{b}") for b in BANK_USES}
        drained = {b: sem(f"drained_{b}") for b in BANK_USES}
        s_pack = [sem(f"s_pack{i}") for i in range(4)]
        s_mask, s_x, s_ctx, s_mk, s_out = sem("s_mask"), sem("s_x"), sem("s_ctx"), sem("s_mk"), sem("s_out")
        zeroed = sem("zeroed")
        cst = {n: sem("c_" + n) for n in ("ones", "act", "dve", "mf", "psT", "mcol", "psN", "mtmp", "masks", "rq",
                                          "psR", "psC", "cb", "wlo", "whi")}
        mk = {n: sem("mk_" + n) for n in ("row", "diag", "four", "fill")}
        ln = [{n: sem(f"ln{i}_{n}") for n in ("stats", "mv", "var", "rstd", "shift", "out")} for i in range(4)]
        scored0, m0_ready, biased0, exp0 = sem("scored0"), sem("m0_ready"), sem("biased0"), sem("exp0")
        hs_step, hsum_ready, hrec_ready, attn0, av0 = (sem(n) for n in ("hs_step", "hsum_ready", "hrec_ready", "attn0", "av0"))
        o0_drained = sem("o0_drained")
        q_amax, q_scale, q_rec, q_int, q_res = (sem(n) for n in ("q_amax", "q_scale", "q_rec", "q_int", "q_res"))
        x2_ready, xb_ready = sem("x2_ready"), sem("xb_ready")
        kh1_ready, km1_ready, qh1_ready, qg1_dma, ones1_ready = (sem(n) for n in ("kh1_ready", "kl1_ready", "qh1_ready",
                                                                                  "qg1_dma", "ones1_ready"))
        k_written, q_written, ks1_dma = sem("k_written"), sem("q_written"), sem("ks1_dma")
        qs1_dma = [sem(f"qs1_dma{i}") for i in range(2)]
        rec1, av_even = sem("rec1"), sem("av_even")
        t3h_ready = sem("t3h_ready")
        tks = {n: sem("tk_" + n) for n in ("max", "exp", "sum", "rec", "p", "gt", "ge", "mix", "max2", "rank", "w")}
        wxh_ready = sem("wxh_ready")
        hid_ready, y_drained = sem("hid_ready"), sem("y_drained")
        down_done = sem("down_done")

        def flat(ap):
            return ap.rearrange("p b d -> p (b d)")

        def bank3(name, n=GB):
            return bank[name].rearrange("p (b d) -> p b d", b=n)

        block = stack.enter_context(nc.Block())

        def skewed(eng, stage_a, both, stage_c):
            stage_a(0)
            with eng.Fori(1, NG - 1) as g:
                both(g)
            both(NG - 1)
            stage_c(NG - 1)

        def has_next(g):
            return not (isinstance(g, int) and g == NG - 1)

        @block.sync
        def _(sp):
            def load_x(g):
                if not first_group(g):
                    sp.wait_ge(drained["A0"], upto(g - 1, "O0p"))
                sp.dma_start(xin[:], x_d[bass.ts(g, GB)].rearrange("b t d -> t b d")).then_inc(s_x, 16)

            def load_ctx(g):
                if not first_group(g):
                    sp.wait_ge(full["A0"], upto(g - 1, "cfT"))
                    sp.wait_ge(mk["row"], g)
                sp.dma_start(ctx[:], ctx_d[bass.ts(g, GB)].rearrange("b t d -> t b d")).then_inc(s_ctx, 16)
                sp.dma_start(mk8[:], mask_d[bass.ts(g, GB)].partition_broadcast(128)).then_inc(s_mk, 16)

            def keys_out(g):
                sp.wait_ge(kh1_ready, g + 1)
                sp.dma_start(k_part[0], Kh1[:].bitcast(F32)).then_inc(k_written, 16)
                sp.dma_start(k_part[2], Kh1[:].bitcast(F32)).then_inc(k_written, 16)
                sp.wait_ge(drained["A1"], upto(g, "K1"))
                sp.dma_start(k_part[1], Kl1[:].bitcast(F32)).then_inc(k_written, 16)

            def keys_in(g):
                sp.wait_ge(k_written, 48 * g + 48)
                sp.dma_start(KS1[:].bitcast(F32), k_stack.rearrange("(w r) t -> r w t", w=4)).then_inc(ks1_dma, 16)

            def queries_out(g):
                sp.wait_ge(qh1_ready, g + 1)
                for G in range(4):
                    r = slice(32 * G, 32 * G + 32)
                    sp.dma_start(Qg1[r, G, :].bitcast(F32), Qh1[r, :].bitcast(F32)).then_inc(qg1_dma, 16)
                for part in range(2):
                    sp.dma_start(q_part[part], Qh1[:].bitcast(F32)).then_inc(q_written, 16)
                sp.wait_ge(drained["A0"], upto(g, "Q1"))
                sp.dma_start(q_part[2], Ql1[:].bitcast(F32)).then_inc(q_written, 16)

            def queries_in(g, b):
                if b == 0:
                    sp.wait_ge(q_written, 48 * g + 48)
                if b >= 2:
                    use = f"s{4 * b - 5}"
                    sp.wait_ge(full[BANK_OF[use]], upto(g, use))
                src = q_stack.rearrange("(w j r) t -> j r w t", w=4, j=4)
                for j in range(4):
                    sp.dma_start(QS1[24 * j:24 * j + 24, b % 2, :, j].bitcast(F32),
                                 src[j][:, :, 128 * b:128 * b + 128]).then_inc(qs1_dma[b % 2], 16)

            def store(m):
                sp.wait_ge(y_drained, m + 1)
                sp.dma_start(out_d[bass.ts(m, GB)].rearrange("b t d -> t b d"), y3[:]).then_inc(s_out, 16)

            load_x(0)
            sp.dma_start(m8[:], mask_d).then_inc(s_mask, 16)
            at = 0
            for i, end in enumerate(SPLITS):
                sp.dma_start(pack[:, at:end], pack_d[:, at:end]).then_inc(s_pack[i], 16)
                at = end
                if i == 0:
                    load_ctx(0)
            sp.dma_start(raw[:, 0:NPACK - KEPT], pack_d[:, KEPT:]).then_inc(s_pack[3], 16)

            def stage_a(g):
                keys_out(g)
                if has_next(g):
                    load_ctx(g + 1)
                keys_in(g)
                if has_next(g):
                    load_x(g + 1)
                queries_out(g)
                queries_in(g, 0)
                queries_in(g, 1)

            def both(g):
                queries_in(g - 1, 2)
                queries_in(g - 1, 3)
                stage_a(g)
                store(g - 1)

            def stage_c(m):
                queries_in(m, 2)
                queries_in(m, 3)
                store(m)

            skewed(sp, stage_a, both, stage_c)
            sp.wait_ge(s_out, 16 * NG + 1)

        @block.gpsimd
        def _(pool):
            p = nc.gpsimd
            p.memset(nhalf[:], -0.5).then_inc(zeroed, 1)

            def zeros():
                p.memset(ones[:], 1.0).then_inc(cst["ones"], 1)
                for t in (Kg0, Vm0, VS1, negM1, MX, lgs, Wx, Qg1, QS1):
                    a = t[:]
                    p.memset(a.bitcast(F32) if a.dtype == F32R else a, 0.0).then_inc(zeroed, 1)
                p.memset(y3[:], 0.0).then_inc(s_out, 1)

            def rstd(i, g):
                pool.wait_ge(ln[i]["var"], g + 1)
                p.tensor_tensor(lnrs[i][:], lnve[i][:], nhalf[:], ALU.pow).then_inc(ln[i]["rstd"], 1)

            def masks(g):
                pool.wait_ge(mk["row"], g + 1)
                wait(pool, mk["fill"], g * GB)
                p.tensor_tensor(omk[:], ones[:].unsqueeze(1).to_broadcast([128, GB, 128]), mrow[:], ALU.subtract)
                p.tensor_tensor(mdiag[:], mrow[:], ident.unsqueeze(1).to_broadcast([128, GB, 128]),
                                ALU.mult).then_inc(mk["diag"], 1)

            def headsum(g, b):
                n = GB * g + b
                pool.wait_ge(exp0, n + 1)
                e = E0[b % 2]
                if b >= 2 or not first_group(g):
                    pool.wait_ge(hrec_ready, n - 1)
                p.tensor_tensor(hs[:, 0:4], e[:, 0:4], e[:, 4:8], ALU.add).then_inc(hs_step, 1)
                pool.wait_ge(hs_step, 2 * n + 1)
                p.tensor_tensor(hs[:, 4:6], hs[:, 0:2], hs[:, 2:4], ALU.add).then_inc(hs_step, 1)
                pool.wait_ge(hs_step, 2 * n + 2)
                p.tensor_tensor(hsum[b % 2][:], hs[:, 4], hs[:, 5], ALU.add).then_inc(hsum_ready, 1)

            def bias_residual(g):
                pool.wait_ge(x2_ready, g + 1)
                pool.wait_ge(cst["cb"], 1)
                if not first_group(g):
                    pool.wait_ge(drained["C3"], upto(g - 1, "O1p"))
                p.tensor_tensor(xb[:], x2[:], cb1[:].unsqueeze(1).to_broadcast([128, GB, D]), ALU.add).then_inc(xb_ready, 1)

            def stage_a(g):
                pool.wait_ge(zeroed, 1)
                rstd(0, g)
                zeros()
                pool.wait_ge(s_pack[0], 16)
                pool.wait_ge(s_pack[1], 16)
                pool.wait_ge(s_pack[2], 16)
                pool.wait_ge(zeroed, 10)
                pool.wait_ge(cst["ones"], 1)
                masks(g)
                for b in range(GB):
                    headsum(g, b)
                rstd(1, g)
                rstd(2, g)
                bias_residual(g)
                rstd(0, g + 1)

            def both(g):
                masks(g)
                for b in range(GB):
                    headsum(g, b)
                rstd(3, g - 1)
                rstd(1, g)
                if has_next(g):
                    rstd(0, g + 1)
                rstd(2, g)
                bias_residual(g)

            def stage_c(m):
                rstd(3, m)

            skewed(pool, stage_a, both, stage_c)

        @block.scalar
        def _(act):
            a = nc.scalar

            def wfull(use, g):
                act.wait_ge(full[BANK_OF[use]], upto(g, use))

            def normalize(i, src, g):
                act.wait_ge(ln[i]["shift"], g + 1)
                if i == 0:
                    wait(act, full["A1"], prev(g, "lnT2"))
                elif i == 1:
                    wait(act, q_int, g)
                elif i == 2:
                    act.wait_ge(full["A0"], upto(g, "lnT0"))
                for b in range(GB):
                    ins = a.activation(lnx[i][:, b], src[:, b], ACT.Identity, bias=lnnm[i][:, b:b + 1],
                                       scale=lnrs[i][:, b:b + 1])
                ins.then_inc(ln[i]["out"], 1)

            def prev(g, use):
                return 0 if first_group(g) else upto(g - 1, use)

            def a1_ln(g):
                act.wait_ge(s_x, 16 * g + 16)
                normalize(0, xin, g)

            def a1_t(g):
                wfull("lnT0", g)
                a.copy(lnT0[:], bank["A0"]).then_inc(drained["A0"], 1)
                wfull("ctxT", g)
                a.copy(ctxT[:], bank["A1"]).then_inc(drained["A1"], 1)

            def a1_q(g):
                wfull("Q0", g)
                wait(act, biased0, GB * g)
                for j in range(4):
                    ins = a.activation(Qm0[:, j], bank["A0"], ACT.Copy, scale=mask0[:, j:j + 1])
                ins.then_inc(drained["A0"], 1)

            def a1_v(g):
                wfull("V0", g)
                wait(act, av0, GB * g)
                dst = bass.AP(tensor=Vm0[:].tensor, offset=0, ap=[[GB * H0 * 32, 128], [64, GB * 4], [48, 2], [1, DH0]])
                a.copy(dst, bank["A0"].rearrange("p (n j d) -> p n j d", j=2, d=DH0)).then_inc(drained["A0"], 1)

            def a2_exp(g, b):
                n = GB * g + b
                act.wait_ge(biased0, n + 1)
                if b >= 2 or not first_group(g):
                    act.wait_ge(av0, n - 1)
                a.activation(E0[b % 2][:].rearrange("p h q -> p (h q)"), psA[:, :], ACT.Exp, scale=0.25).then_inc(exp0, 1)

            def a3_o0(g):
                act.wait_ge(av0, GB * g + GB)
                wait(act, full["A0"], prev(g, "O0p"))
                a.copy(O0T[:], bank["O"]).then_inc(o0_drained, 1)

            def a3_ctx(g):
                wfull("cfT", g)
                wait(act, full["A1"], prev(g, "K1"))
                a.copy(cfT[:], bank["A0"]).then_inc(drained["A0"], 1)

            def a3_k1(g):
                wfull("K1", g)
                wait(act, k_written, 48 * g)
                a.activation(Kh1[:], bank["A1"], ACT.Identity, bias=const("bk1")).then_inc(kh1_ready, 1)

            def a3_km(g):
                act.wait_ge(kh1_ready, g + 1)
                for j in range(4):
                    a.activation(Km1[:, j], Kh1[:].bitcast(F32), ACT.Copy, scale=mask1[:, j:j + 1]).then_inc(km1_ready, 1)

            def a3_v1(g):
                wfull("V1", g)
                act.wait_ge(mk["four"], g + 1)
                for b in range(GB):
                    dst = bass.AP(tensor=VS1[:].tensor, offset=b * H1 * 64,
                                  ap=[[GB * H1 * 64, 128], [4 * 64, 4], [72, 4], [1, DH1]])
                    src = bank["A0"][:, 128 * b:128 * b + 128].rearrange("p (w j d) -> p w j d", w=4, j=4)
                    ins = a.activation(dst, src, ACT.Copy, scale=mkeep4[:, b:b + 1])
                ins.then_inc(drained["A0"], 1)

            def a3_t2(g):
                wfull("lnT2", g)
                a.copy(lnT2[:], bank["A1"]).then_inc(drained["A1"], 1)

            def a3_q1(g):
                wfull("Q1", g)
                wait(act, q_written, 48 * g)
                wait(act, qg1_dma, 64 * g)
                a.activation(Qh1[:], bank["A0"], ACT.Identity, bias=const("bq1")).then_inc(qh1_ready, 1)

            def c1_exp(m, u):
                use = f"s{u}"
                wfull(use, m)
                if u == 8:
                    act.wait_ge(av_even, 2 * m + 1)
                elif u == 12:
                    act.wait_ge(full["C3"], upto(m, "AV01"))
                a.activation(E1[u // 4 % 2][:, u % 4].rearrange("p j q -> p (j q)"), bank[BANK_OF[use]], ACT.Exp,
                             scale=SCALE1).then_inc(drained[BANK_OF[use]], 1)

            def c1_out(m, half):
                use = ("AV01", "AV23")[half]
                wfull(use, m)
                a.copy(OU[:, 2 * half:2 * half + 2].rearrange("p b w q -> p (b w q)"),
                       bank[BANK_OF[use]]).then_inc(drained[BANK_OF[use]], 1)

            def c2_oT(m):
                wfull("OT", m)
                a.copy(O1T[:], bank["C2"]).then_inc(drained["C2"], 1)

            def c2_ln(m):
                normalize(3, x3, m)

            def c2_t(m):
                wfull("T3", m)
                a.copy(T3h[:], bank["C0"]).then_inc(t3h_ready, 1)

            def c2_router(m):
                wfull("lg", m)
                a.copy(lgs[0:NE, :], bank["C1"][0:NE, :]).then_inc(drained["C1"], 1)

            def c2_exp(m):
                act.wait_ge(drained["C2"], upto(m, "lgT"))
                a.activation(tke[:], tke[:], ACT.Exp).then_inc(tks["exp"], 1)

            def c2_w(m):
                wfull("WtT", m)
                a.copy(Wx[0:NE, :], bank["D"][0:NE, :]).then_inc(wxh_ready, 1)

            def c2_silu(m, i):
                wfull(f"G{i}", m)
                if i >= 2:
                    last = "U0" if i == 2 else f"W{i - 3}"
                    act.wait_ge(drained[BANK_OF[last]], upto(m, last))
                a.activation(sg[i % 2][:], bank[BANK_OF[f"G{i}"]], ACT.Silu).then_inc(drained[BANK_OF[f"G{i}"]], 1)

            act.wait_ge(s_pack[0], 16)
            a.copy(identr[:], ident).then_inc(cst["act"], 1)

            def late_constants():
                act.wait_ge(s_pack[1], 16)
                act.wait_ge(s_pack[2], 16)
                act.wait_ge(s_pack[3], 16)
                a.copy(routerH[:], const("router"))
                a.copy(guH[:].rearrange("p k c f -> p (k c f)"), raw_gu)
                a.copy(rowM[:], const("rowM"))
                a.copy(selW[:].rearrange("p c k -> p (c k)"), raw_sel).then_inc(cst["whi"], 1)

            def stage_a(g):
                a1_ln(g)
                a1_t(g)
                a1_q(g)
                act.wait_ge(zeroed, 10)
                a1_v(g)
                for b in range(GB):
                    a2_exp(g, b)
                    if b == 0:
                        late_constants()
                a3_ctx(g)
                a3_o0(g)
                a3_k1(g)
                a3_km(g)
                a3_v1(g)
                normalize(1, x1, g)
                normalize(2, x2, g)
                a3_t2(g)
                a3_q1(g)
                a1_ln(g + 1)

            def both(g):
                m = g - 1
                a1_t(g)
                a1_q(g)
                a1_v(g)
                def exps(begin, end):
                    for u in range(begin, end):
                        c1_exp(m, u)

                a2_exp(g, 0)
                a2_exp(g, 1)
                exps(0, 5)
                a2_exp(g, 2)
                exps(5, 10)
                a2_exp(g, 3)
                exps(10, 13)
                c1_out(m, 0)
                exps(13, 16)
                c1_out(m, 1)
                a3_ctx(g)
                a3_o0(g)
                c2_oT(m)
                a3_k1(g)
                a3_km(g)
                a3_v1(g)
                c2_ln(m)
                normalize(1, x1, g)
                c2_t(m)
                c2_router(m)
                c2_exp(m)
                c2_silu(m, 0)
                c2_silu(m, 1)
                c2_w(m)
                normalize(2, x2, g)
                c2_silu(m, 2)
                a3_t2(g)
                c2_silu(m, 3)
                a3_q1(g)
                if has_next(g):
                    a1_ln(g + 1)
                c2_silu(m, 4)

            def stage_c(m):
                for u in range(16):
                    c1_exp(m, u)
                    if u == 11:
                        c1_out(m, 0)
                c1_out(m, 1)
                c2_oT(m)
                c2_ln(m)
                c2_t(m)
                c2_router(m)
                c2_exp(m)
                c2_silu(m, 0)
                c2_silu(m, 1)
                c2_w(m)
                for i in range(2, NB):
                    c2_silu(m, i)

            skewed(act, stage_a, both, stage_c)

        @block.vector
        def _(dve):
            v = nc.vector

            def wfull(use, g):
                dve.wait_ge(full[BANK_OF[use]], upto(g, use))

            def stats(i, src, g):
                for b in range(GB):
                    ins = v.bn_stats(lnst[i][:, b], src[:, b])
                ins.then_inc(ln[i]["stats"], 1)
                dve.wait_ge(ln[i]["stats"], g + 1)
                v.memset(pause[:], 0.0)
                for b in range(GB):
                    ins = v.bn_aggr(lnmv[i][:, b], lnst[i][:, b])
                ins.then_inc(ln[i]["mv"], 1)
                dve.wait_ge(ln[i]["mv"], g + 1)
                v.tensor_scalar(lnve[i][:], lnmv[i][:, :, 1], EPS, None, ALU.add).then_inc(ln[i]["var"], 1)

            def shift(i, g):
                dve.wait_ge(ln[i]["rstd"], g + 1)
                v.scalar_tensor_tensor(out=lnnm[i][:], in0=lnmv[i][:, :, 0], scalar=-1.0, in1=lnrs[i][:],
                                       op0=ALU.mult, op1=ALU.mult).then_inc(ln[i]["shift"], 1)

            def a1_mask(g):
                dve.wait_ge(s_mk, 16 * g + 16)
                wait(dve, mk["diag"], g)
                v.tensor_copy(mrow[:], mk8[:]).then_inc(mk["row"], 1)

            def a1_k(g):
                wfull("K0", g)
                wait(dve, biased0, GB * g)
                v.tensor_copy(Kg0[0:64, 0], bank["A1"][0:64])
                v.tensor_copy(Kg0[64:128, 1], bank["A1"][64:128]).then_inc(drained["A1"], 1)

            def a2_max(g, b):
                dve.wait_ge(scored0, GB * g + b + 1)
                v.tensor_reduce(negM0[:], psA[:, :].rearrange("p (h q) -> p q h", h=H0), AX.X, ALU.max,
                                negate=True).then_inc(m0_ready, 1)

            def a2_norm(g, b):
                n = GB * g + b
                dve.wait_ge(hsum_ready, n + 1)
                if b >= 2 or not first_group(g):
                    dve.wait_ge(attn0, n - 1)
                v.reciprocal(hrec[b % 2][:], hsum[b % 2][:]).then_inc(hrec_ready, 1)
                dve.wait_ge(hrec_ready, n + 1)
                e = E0[b % 2]
                v.tensor_tensor(e[:], e[:], hrec[b % 2][:].unsqueeze(1).to_broadcast([128, H0, S]), ALU.mult).then_inc(attn0, 1)

            def a3_fill(g):
                if not first_group(g):
                    dve.wait_ge(drained["A0"], upto(g - 1, "V1"))
                    dve.wait_ge(full["A0"], upto(g - 1, "cfT"))
                v.tensor_copy(mkeep4[:], mkeep[:, bass.ts(g, GB)])
                v.tensor_copy(mfill4[:], mfill[:, bass.ts(g, GB)]).then_inc(mk["four"], 1)
                dve.wait_ge(mk["four"], g + 1)
                dve.wait_ge(mk["diag"], g + 1)
                for b in range(GB):
                    v.scalar_tensor_tensor(out=fill[:, b], in0=omk[:, b], scalar=mfill4[:, b:b + 1], in1=mdiag[:, b],
                                           op0=ALU.mult, op1=ALU.add).then_inc(mk["fill"], 1)

            def a3_sums(g):
                if not first_group(g):
                    dve.wait_ge(full["D"], upto(g - 1, "AV23"))
                dst = bass.AP(tensor=VS1[:].tensor, offset=32, ap=[[GB * H1 * 64, 128], [H1 * 64, GB], [256, 4], [65, 4]])
                src = mkeep4[:].unsqueeze(2).unsqueeze(3).to_broadcast([128, GB, 4, 4])
                v.tensor_copy(dst, src).then_inc(ones1_ready, 1)

            def a3_k1(g):
                dve.wait_ge(kh1_ready, g + 1)
                wait(dve, k_written, 48 * g)
                v.scalar_tensor_tensor(out=Kl1[:], in0=bank["A1"], scalar=const("bk1"), in1=Kh1[:].bitcast(F32),
                                       op0=ALU.add, op1=ALU.subtract).then_inc(drained["A1"], 1)

            def a3_x1(g):
                wfull("O0p", g)
                v.tensor_tensor(x1[:], bank3("A0"), xin[:], ALU.add).then_inc(drained["A0"], 1)

            def a3_stats1(g):
                dve.wait_ge(drained["A0"], upto(g, "O0p"))
                stats(1, x1, g)

            def a3_quant(g):
                dve.wait_ge(ln[1]["out"], g + 1)
                v.tensor_reduce(amax[:], lnx[1][:], AX.X, ALU.max, apply_absolute_value=True).then_inc(q_amax, 1)
                dve.wait_ge(q_amax, g + 1)
                v.tensor_scalar(lscale[:], amax[:], 1e-12, INV127, ALU.max, ALU.mult).then_inc(q_scale, 1)
                dve.wait_ge(q_scale, g + 1)
                v.reciprocal(lrec[:], lscale[:]).then_inc(q_rec, 1)
                dve.wait_ge(q_rec, g + 1)
                for b in range(GB):
                    ins = v.tensor_scalar(qz[:, b], lnx[1][:, b], lrec[:, b:b + 1], MAGIC, ALU.mult, ALU.add)
                ins.then_inc(q_int, 1)

            def a3_qT(g):
                wfull("qT", g)
                v.tensor_scalar(qT[:], bank["A1"], -MAGIC, None, ALU.add).then_inc(drained["A1"], 1)

            def a3_x2(g):
                wfull("qmm", g)
                for b in range(GB):
                    ins = v.scalar_tensor_tensor(out=qres[:, b], in0=bank3("A0")[:, b], scalar=lscale[:, b:b + 1],
                                                 in1=rscale[:], op0=ALU.mult, op1=ALU.mult)
                ins.then_inc(drained["A0"], 1)
                dve.wait_ge(drained["A0"], upto(g, "qmm"))
                wait(dve, xb_ready, g)
                v.tensor_tensor(x2[:], x1[:], qres[:], ALU.add).then_inc(x2_ready, 1)
                dve.wait_ge(x2_ready, g + 1)
                stats(2, x2, g)

            def a3_q1(g):
                dve.wait_ge(qh1_ready, g + 1)
                wait(dve, q_written, 48 * g)
                v.scalar_tensor_tensor(out=Ql1[:], in0=bank["A0"], scalar=const("bq1"), in1=Qh1[:].bitcast(F32),
                                       op0=ALU.add, op1=ALU.subtract).then_inc(drained["A0"], 1)

            def b_max(m, u):
                use = f"max{u}"
                wfull(use, m)
                v.tensor_reduce(negM1[:, 4 * u:4 * u + 4], bank[BANK_OF[use]].rearrange("p (j k) -> p j k", j=4), AX.X,
                                ALU.max, negate=True).then_inc(drained[BANK_OF[use]], 1)

            def b_mx(m):
                wfull("MT", m)
                src = bank["D"][0:64, 0:128].unsqueeze(1).to_broadcast([64, 4, 128])
                v.tensor_tensor(MX[0:64], src, maskM[0:64].unsqueeze(2).to_broadcast([64, 4, 128]),
                                ALU.mult).then_inc(drained["D"], 1)

            def c2_rec(m):
                for half in range(2):
                    use = f"TO{half}"
                    wfull(use, m)
                    ps = bank[BANK_OF[use]].rearrange("p (n c) -> p n c", n=8)
                    v.reciprocal(Rq[:, half], ps[:, :, 32:36]).then_inc(rec1, 1)
                    dve.wait_ge(rec1, 2 * m + half + 1)
                    out = Oq[:, 2 * half:2 * half + 2].rearrange("p b (n j d) -> p (b n) j d", j=4, d=DH1)
                    v.tensor_tensor(out, ps[:, :, 0:32].rearrange("p n (j d) -> p n j d", j=4),
                                    Rq[:, half].unsqueeze(3).to_broadcast([128, 8, 4, DH1]),
                                    ALU.mult).then_inc(drained[BANK_OF[use]], 1)

            def c2_x3(m):
                wfull("O1p", m)
                dve.wait_ge(xb_ready, m + 1)
                v.tensor_tensor(x3[:], bank3("C3"), xb[:], ALU.add).then_inc(drained["C3"], 1)
                dve.wait_ge(drained["C3"], upto(m, "O1p"))
                stats(3, x3, m)

            def c2_t(m):
                dve.wait_ge(t3h_ready, m + 1)
                v.tensor_tensor(T3l[:], bank["C0"], T3h[:].bitcast(F32), ALU.subtract).then_inc(drained["C0"], 1)

            def c2_soft(m):
                wfull("lgT", m)
                lg = bank3("C2")[:, :, 0:NE]
                v.tensor_reduce(tk["nmax"][:], lg, AX.X, ALU.max, negate=True).then_inc(tks["max"], 1)
                dve.wait_ge(tks["max"], m + 1)
                v.tensor_tensor(tke[:], lg, tk["nmax"][:].unsqueeze(2).to_broadcast([128, GB, NE]), ALU.add)\
                    .then_inc(drained["C2"], 1)

            def c2_topk(m):
                dve.wait_ge(tks["exp"], m + 1)
                v.tensor_reduce(tk["sum"][:], tke[:], AX.X, ALU.add).then_inc(tks["sum"], 1)
                dve.wait_ge(tks["sum"], m + 1)
                v.reciprocal(tk["rec"][:], tk["sum"][:]).then_inc(tks["rec"], 1)
                dve.wait_ge(tks["rec"], m + 1)
                v.tensor_tensor(tkp[:], tke[:], tk["rec"][:].unsqueeze(2).to_broadcast([128, GB, NE]), ALU.mult)\
                    .then_inc(tks["p"], 1)
                dve.wait_ge(tks["p"], m + 1)
                pj = tkp[:].unsqueeze(2).to_broadcast([128, GB, NE, NE])
                pi = tkp[:].unsqueeze(3).to_broadcast([128, GB, NE, NE])
                v.tensor_tensor(gt[:], pj, pi, ALU.is_gt)
                v.tensor_tensor(ge[:], pj, pi, ALU.is_ge).then_inc(tks["ge"], 1)

            def c2_keep(m):
                dve.wait_ge(tks["ge"], m + 1)
                tri = const("tri").rearrange("p (i j) -> p i j", i=NE).unsqueeze(1).to_broadcast([128, GB, NE, NE])
                v.tensor_tensor(gmix[:], ge[:], tri, ALU.mult).then_inc(tks["mix"], 1)
                dve.wait_ge(tks["mix"], m + 1)
                v.tensor_tensor(gt[:], gt[:], gmix[:], ALU.max).then_inc(tks["max2"], 1)
                dve.wait_ge(tks["max2"], m + 1)
                v.tensor_reduce(rank[:], gt[:], AX.X, ALU.add).then_inc(tks["rank"], 1)
                dve.wait_ge(tks["rank"], m + 1)
                v.scalar_tensor_tensor(out=Wt[:], in0=rank[:], scalar=TOPK - 0.5, in1=tkp[:], op0=ALU.is_lt,
                                       op1=ALU.mult).then_inc(tks["w"], 1)

            def c2_w(m):
                dve.wait_ge(wxh_ready, m + 1)
                v.tensor_tensor(Wx[32:32 + NE, :], bank["D"][0:NE, :], Wx[0:NE, :].bitcast(F32),
                                ALU.subtract).then_inc(drained["D"], 1)

            def c2_hidden(m, i):
                n = NB * m + i
                bG, bU = BANK_OF[f"G{i}"], BANK_OF[f"U{i}"]
                dve.wait_ge(drained[bG], upto(m, f"G{i}"))
                wfull(f"U{i}", m)
                if i == 0:
                    v.tensor_tensor(hid[0][:], sg[0][:], bank[bU], ALU.mult).then_inc(drained[bU], 1)
                    return
                v.tensor_tensor(sg[i % 2][:], sg[i % 2][:], bank[bU], ALU.mult).then_inc(drained[bU], 1)
                wfull(f"W{i - 1}", m)
                dve.wait_ge(drained[bU], upto(m, f"U{i}"))
                if i >= 2:
                    dve.wait_ge(down_done, n - 1)
                v.tensor_tensor(hid[i % 2][:], sg[i % 2][:], bank["D"], ALU.mult).then_inc(drained["D"], 1)

            def c2_out(m):
                dve.wait_ge(down_done, NB * m + NB)
                dve.wait_ge(s_out, 16 * m + 1)
                v.tensor_tensor(y3[:], bank3("O"), x3[:], ALU.add).then_inc(y_drained, 1)

            def setup():
                dve.wait_ge(s_mask, 16)
                v.tensor_copy(mf[:], m8[:]).then_inc(cst["mf"], 1)
                dve.wait_ge(cst["psT"], 1)
                v.tensor_copy(mcol[:], bank["C0"][:, 0:B]).then_inc(cst["mcol"], 1)
                dve.wait_ge(cst["psN"], 1)
                dve.wait_ge(cst["mcol"], 1)
                v.tensor_scalar(mtmp[:, 0], bank["C1"][:, 0:B], 1.0, None, ALU.max).then_inc(cst["mtmp"], 1)
                v.tensor_scalar(mtmp[:, 2], bank["C1"][:, 0:B], 0.5, None, ALU.is_lt).then_inc(cst["mtmp"], 1)
                dve.wait_ge(cst["mtmp"], 2)
                v.reciprocal(mtmp[:, 1], mtmp[:, 0]).then_inc(cst["mtmp"], 1)
                v.tensor_tensor(mkeep[:], mcol[:], mtmp[:, 2], ALU.add).then_inc(cst["masks"], 1)
                dve.wait_ge(cst["mtmp"], 3)
                v.tensor_tensor(mfill[:], mcol[:], mtmp[:, 1], ALU.mult).then_inc(cst["masks"], 1)
                dve.wait_ge(cst["masks"], 2)

            def setup2():
                dve.wait_ge(s_pack[1], 16)
                v.tensor_reduce(rtmp[:, 0:1], const("rhsT"), AX.X, ALU.max, apply_absolute_value=True).then_inc(cst["rq"], 1)
                dve.wait_ge(cst["rq"], 1)
                v.tensor_scalar(rtmp[:, 1:2], rtmp[:, 0:1], 1e-12, INV127, ALU.max, ALU.mult).then_inc(cst["rq"], 1)
                dve.wait_ge(cst["rq"], 2)
                v.reciprocal(rtmp[:, 2:3], rtmp[:, 1:2]).then_inc(cst["rq"], 1)
                dve.wait_ge(cst["rq"], 3)
                v.tensor_scalar(rq[:, 0], const("rhsT"), rtmp[:, 2:3], MAGIC, ALU.mult, ALU.add).then_inc(cst["rq"], 1)
                v.tensor_copy(rq[:, 1], rtmp[:, 1:2].to_broadcast([128, 128])).then_inc(cst["rq"], 1)
                v.tensor_copy(y3[:, 0], const("bv1").to_broadcast([128, 128])).then_inc(cst["rq"], 1)
                dve.wait_ge(cst["psR"], 1)
                v.tensor_scalar(rhsq[:], bank["C2"][:, 0:128], -MAGIC, None, ALU.add)
                v.tensor_copy(rscale[:], bank["C2"][:, 128:256])
                v.tensor_tensor(cb1[:], bank["C2"][:, 256:384], const("bo1"), ALU.add).then_inc(cst["cb"], 1)

            def setup3():
                dve.wait_ge(s_pack[2], 16)
                dve.wait_ge(cst["whi"], 1)
                v.tensor_tensor(routerL[:], const("router"), routerH[:].bitcast(F32), ALU.subtract)
                dve.wait_ge(s_pack[3], 16)
                v.tensor_tensor(guL[:].rearrange("p k c f -> p (k c f)"), raw_gu,
                                guH[:].rearrange("p k c f -> p (k c f)").bitcast(F32), ALU.subtract).then_inc(cst["wlo"], 1)

            def a1_stats(g):
                dve.wait_ge(s_x, 16 * g + 16)
                stats(0, xin, g)

            def stage_a(g):
                a1_stats(g)
                dve.wait_ge(s_pack[0], 16)
                setup()
                shift(0, g)
                a1_mask(g)
                dve.wait_ge(zeroed, 10)
                a1_k(g)
                a3_fill(g)
                a3_sums(g)
                a2_max(g, 0)
                setup2()
                for b in range(1, GB):
                    a2_max(g, b)
                    a2_norm(g, b - 1)
                a2_norm(g, GB - 1)
                a3_k1(g)
                a3_x1(g)
                a3_stats1(g)
                setup3()
                shift(1, g)
                a3_quant(g)
                a3_qT(g)
                a3_x2(g)
                shift(2, g)
                a3_q1(g)
                a1_stats(g + 1)
                shift(0, g + 1)

            def both(g):
                m = g - 1
                a1_mask(g)
                def maxima(begin, end):
                    for u in range(begin, end):
                        b_max(m, u)

                maxima(0, 4)
                a1_k(g)
                maxima(4, 10)
                a2_max(g, 0)
                maxima(10, 16)
                a2_max(g, 1)
                b_mx(m)
                a2_norm(g, 0)
                a2_max(g, 2)
                a3_fill(g)
                a2_norm(g, 1)
                a2_max(g, 3)
                a2_norm(g, 2)
                a2_norm(g, GB - 1)
                c2_rec(m)
                c2_x3(m)
                a3_x1(g)
                a3_k1(g)
                shift(3, m)
                a3_stats1(g)
                a3_sums(g)
                shift(1, g)
                c2_t(m)
                if has_next(g):
                    a1_stats(g + 1)
                a3_quant(g)
                c2_soft(m)
                a3_qT(g)
                c2_topk(m)
                c2_keep(m)
                a3_x2(g)
                c2_hidden(m, 0)
                c2_w(m)
                shift(2, g)
                if has_next(g):
                    shift(0, g + 1)
                c2_hidden(m, 1)
                c2_hidden(m, 2)
                c2_hidden(m, 3)
                a3_q1(g)
                c2_hidden(m, 4)
                c2_out(m)

            def stage_c(m):
                for u in range(16):
                    b_max(m, u)
                b_mx(m)
                c2_rec(m)
                c2_x3(m)
                shift(3, m)
                c2_t(m)
                c2_soft(m)
                c2_topk(m)
                c2_keep(m)
                c2_hidden(m, 0)
                c2_w(m)
                for i in range(1, NB):
                    c2_hidden(m, i)
                c2_out(m)

            skewed(dve, stage_a, both, stage_c)

        @block.tensor
        def _(pe):
            t = nc.tensor

            def claim(use, g):
                bk = BANK_OF[use]
                if bk in ("A0", "A1") or BANK_USES[bk].index(use) > 0:
                    wait(pe, drained[bk], upto(g, use) - 1)
                return bank[bk]

            def done(ins, use):
                ins.then_inc(full[BANK_OF[use]], 1)

            def wdrained(use, g):
                pe.wait_ge(drained[BANK_OF[use]], upto(g, use))

            def turn(use, src, g):
                ps = claim(use, g)
                for b in range(GB):
                    ins = t.transpose(ps[:, 128 * b:128 * b + 128], src[:, b], ident)
                done(ins, use)

            def project(use, w, xT, g):
                ps = claim(use, g)
                done(t.matmul(ps, w, xT, start=True, stop=True), use)

            def a1(g):
                pe.wait_ge(ln[0]["out"], g + 1)
                turn("lnT0", lnx[0], g)
                pe.wait_ge(s_ctx, 16 * g + 16)
                turn("ctxT", ctx, g)

            def a1_p(g):
                wdrained("lnT0", g)
                project("Q0", const("wq0"), lnT0[:], g)
                wdrained("ctxT", g)
                project("K0", const("wk0"), ctxT[:], g)

            def a1_v(g):
                ps = claim("V0", g)
                for b in range(GB):
                    ins = t.matmul(ps[:, 128 * b:128 * b + 128], ctxT[:, 128 * b:128 * b + 128], const("wv01")[:, 0:128],
                                   start=True, stop=True)
                done(ins, "V0")

            def a2_scores(g, b):
                n = GB * g + b
                if b == 0:
                    pe.wait_ge(drained["A0"], upto(g, "V0"))
                    pe.wait_ge(drained["A1"], upto(g, "K0"))
                else:
                    pe.wait_ge(exp0, n)
                cols = slice(128 * b, 128 * b + 128)
                for k in range(2):
                    ins = t.matmul(psA[:, 512 * k:512 * k + 512], Kg0[:, k, cols], Qm0[:, :, cols], start=True, stop=True)
                ins.then_inc(scored0, 1)

            def a2_bias(g, b):
                n = GB * g + b
                pe.wait_ge(m0_ready, n + 1)
                mv = negM0[:].unsqueeze(1).to_broadcast([128, 4, S])
                for k in range(2):
                    ins = t.matmul(psA[:, 512 * k:512 * k + 512], identr[:], mv, start=False, stop=True,
                                   skip_group_check=True)
                ins.then_inc(biased0, 1)

            def a2_av(g, b):
                n = GB * g + b
                pe.wait_ge(attn0, n + 1)
                if b == 0:
                    wait(pe, o0_drained, g)
                cols = slice(128 * b, 128 * b + 128)
                for j in range(2):
                    for p in range(4):
                        ins = t.matmul(bank["O"][32 * p:32 * p + 32, cols], Vm0[:, b, 2 * p + j, :], E0[b % 2][:, 2 * p + j, :],
                                       start=(j == 0), stop=(j == 1), tile_position=(0, 32 * p))
                ins.then_inc(av0, 1)

            def a3_ctx(g):
                pe.wait_ge(mk["fill"], GB * g + GB)
                pe.wait_ge(exp0, GB * g + GB)
                ps = claim("cfT", g)
                for b in range(GB):
                    ins = t.matmul(ps[:, 128 * b:128 * b + 128], ctx[:, b], fill[:, b], start=True, stop=True)
                done(ins, "cfT")

            def a3_k1(g):
                wdrained("cfT", g)
                project("K1", const("wk1"), cfT[:], g)

            def a3_v1(g):
                ps = claim("V1", g)
                for b in range(GB):
                    ins = t.matmul(ps[:, 128 * b:128 * b + 128], ctxT[:, 128 * b:128 * b + 128],
                                   const("wv01")[:, 128:256], start=True, stop=True)
                done(ins, "V1")

            def a3_o0(g):
                pe.wait_ge(o0_drained, g + 1)
                ps = claim("O0p", g)
                for b in range(GB):
                    ins = t.matmul(ps[:, 128 * b:128 * b + 128], O0T[:, 128 * b:128 * b + 128], const("wo0"),
                                   start=True, stop=True)
                done(ins, "O0p")

            def a3_qT(g):
                pe.wait_ge(q_int, g + 1)
                turn("qT", qz, g)

            def a3_qmm(g):
                wdrained("qT", g)
                ps = claim("qmm", g)
                for b in range(GB):
                    ins = t.matmul(ps[:, 128 * b:128 * b + 128], qT[:, 128 * b:128 * b + 128], rhsq[:], start=True, stop=True)
                done(ins, "qmm")

            def a3_t2(g):
                pe.wait_ge(ln[2]["out"], g + 1)
                turn("lnT2", lnx[2], g)

            def a3_q1(g):
                wdrained("lnT2", g)
                project("Q1", const("wq1"), lnT2[:], g)

            def b_scores(m, u):
                b, G = divmod(u, 4)
                cols = slice(128 * b, 128 * b + 128)
                if u == 0:
                    pe.wait_ge(qg1_dma, 64 * m + 64)
                    pe.wait_ge(km1_ready, 4 * m + 4)
                ps = claim(f"max{u}", m)
                done(t.matmul(ps, Qg1[:, G, cols], Km1[:, :, cols], start=True, stop=True), f"max{u}")

            def b_turn(m):
                for u in (12, 13, 14, 15):
                    wdrained(f"max{u}", m)
                ps = claim("MT", m)
                done(t.transpose(ps[:, 0:128], negM1[:], ident), "MT")

            def c1_scores(m, u):
                b, G = divmod(u, 4)
                cols = slice(128 * b, 128 * b + 128)
                if u == 0:
                    pe.wait_ge(ks1_dma, 16 * m + 16)
                    wdrained("MT", m)
                if G == 0:
                    pe.wait_ge(qs1_dma[b % 2], 128 * m + 64 * (b // 2) + 64)
                ps = claim(f"s{u}", m)
                t.matmul(ps, KS1[:, G, cols], QS1[:, b % 2, G].rearrange("r j q -> r (j q)"), start=True, stop=False)
                done(t.matmul(ps, rowM[:, u:u + 1].to_broadcast([128, 128]), MX[:].rearrange("p j q -> p (j q)"), start=False, stop=True), f"s{u}")

            def c1_av(m, b):
                for u in range(4 * b + 1, 4 * b + 4):
                    wdrained(f"s{u}", m)
                use = ("AV01", "AV23")[b // 2]
                if b == 0:
                    pe.wait_ge(ones1_ready, m + 1)
                    wdrained("V1", m)
                if b % 2 == 0:
                    claim(use, m)
                for w in range(2):
                    cols = slice(256 * (b % 2) + 128 * w, 256 * (b % 2) + 128 * w + 128)
                    for j in range(4):
                        for k in range(2):
                            G = 2 * w + k
                            ins = t.matmul(bank[BANK_OF[use]][64 * k:64 * k + 64, cols], VS1[:, b, 4 * G + j, :],
                                           E1[b % 2][:, G, j, :], start=(j == 0), stop=(j == 3), tile_position=(0, 64 * k))
                if b % 2:
                    done(ins, use)
                else:
                    ins.then_inc(av_even, 1)

            def c2_back(m, half):
                wdrained(("AV01", "AV23")[half], m)
                use = f"TO{half}"
                ps = claim(use, m)
                for n in range(4):
                    ins = t.transpose(ps[:, 128 * n:128 * n + 128], OU[:, 2 * half + n // 2, n % 2], ident)
                done(ins, use)

            def c2_oT(m):
                wdrained("TO0", m)
                wdrained("TO1", m)
                turn("OT", Oq, m)

            def c2_o(m):
                wdrained("OT", m)
                ps = claim("O1p", m)
                for b in range(GB):
                    ins = t.matmul(ps[:, 128 * b:128 * b + 128], O1T[:, 128 * b:128 * b + 128], const("wo1"),
                                   start=True, stop=True)
                done(ins, "O1p")

            def c2_t(m):
                pe.wait_ge(ln[3]["out"], m + 1)
                turn("T3", lnx[3], m)

            def split_product(ps, wh, wl):
                t.matmul(ps, wh, T3h[:], start=True, stop=False)
                t.matmul(ps, wl, T3h[:], start=False, stop=False)
                return t.matmul(ps, wh, T3l[:], start=False, stop=True)

            def c2_router(m):
                wdrained("T3", m)
                ps = claim("lg", m)
                done(split_product(ps[0:NE, :], routerH[:], routerL[:]), "lg")

            def c2_lgT(m):
                wdrained("lg", m)
                ps = claim("lgT", m)
                for b in range(GB):
                    ins = t.transpose(ps[:, 128 * b:128 * b + 128], lgs[:, 128 * b:128 * b + 128], ident)
                done(ins, "lgT")

            def c2_wT(m):
                pe.wait_ge(tks["w"], m + 1)
                ps = claim("WtT", m)
                for b in range(GB):
                    ins = t.transpose(ps[0:NE, 128 * b:128 * b + 128], Wt[:, b], ident)
                done(ins, "WtT")

            def c2_gate(m, i):
                use = f"G{i}"
                done(split_product(claim(use, m), guH[:, 0, (i - 1) % NB], guL[:, 0, (i - 1) % NB]), use)

            def c2_up(m, i):
                use = f"U{i}"
                done(split_product(claim(use, m), guH[:, 1, (i - 1) % NB], guL[:, 1, (i - 1) % NB]), use)

            def c2_w(m, i):
                if i == 1:
                    wdrained("WtT", m)
                ps = claim(f"W{i - 1}", m)
                done(t.matmul(ps, selW[:, i - 1], Wx[:], start=True, stop=True), f"W{i - 1}")

            def c2_down(m, i):
                c = (i - 1) % NB
                if i == 0:
                    wdrained("U0", m)
                    pe.wait_ge(o0_drained, min(m + 2, NG) if isinstance(m, int) else m + 2)
                else:
                    wdrained(f"W{i - 1}", m)
                for b in range(GB):
                    ins = t.matmul(bank["O"][:, 128 * b:128 * b + 128], hid[i % 2][:, 128 * b:128 * b + 128], down[:, c, :],
                                   start=(i == 0 and b == 0), stop=(i == NB - 1), skip_group_check=True)
                ins.then_inc(down_done, 1)

            def setup():
                pe.wait_ge(s_pack[0], 16)
                pe.wait_ge(cst["mf"], 1)
                t.transpose(bank["C0"][:, 0:B], mf[:], ident[0:B, 0:B]).then_inc(cst["psT"], 1)
                pe.wait_ge(cst["mcol"], 1)
                pe.wait_ge(cst["ones"], 1)
                t.matmul(bank["C1"][:, 0:B], ones[:], mcol[:], start=True, stop=True).then_inc(cst["psN"], 1)

            def setup2():
                pe.wait_ge(cst["rq"], 6)
                t.transpose(bank["C2"][:, 0:128], rq[:, 0], ident)
                t.transpose(bank["C2"][:, 128:256], rq[:, 1], ident)
                t.matmul(bank["C2"][:, 256:384], y3[:, 0], const("wo1"), start=True, stop=True).then_inc(cst["psR"], 1)

            def stage_a(g):
                setup()
                a1(g)
                a1_p(g)
                a1_v(g)
                pe.wait_ge(cst["act"], 1)
                for b in range(GB):
                    a2_scores(g, b)
                    if b == 1:
                        setup2()
                    if b > 1:
                        a2_av(g, b - 2)
                    a2_bias(g, b)
                a2_av(g, GB - 2)
                a3_ctx(g)
                a2_av(g, GB - 1)
                pe.wait_ge(s_pack[1], 16)
                a3_k1(g)
                a3_o0(g)
                a3_v1(g)
                a3_qT(g)
                a3_qmm(g)
                a3_t2(g)
                a3_q1(g)
                pe.wait_ge(cst["wlo"], 1)

            def c2_blocks(m, i):
                c2_w(m, i)
                if i + 1 < NB:
                    c2_gate(m, i + 1)
                    c2_up(m, i + 1)
                c2_down(m, i)

            def both(g):
                m = g - 1
                def maxima(begin, end):
                    for u in range(begin, end):
                        b_scores(m, u)

                def scores(begin, end):
                    for u in range(begin, end):
                        c1_scores(m, u)

                a1(g)
                maxima(0, 4)
                a1_p(g)
                maxima(4, 8)
                a1_v(g)
                maxima(8, 10)
                a2_scores(g, 0)
                maxima(10, 14)
                a2_bias(g, 0)
                maxima(14, 16)
                a2_scores(g, 1)
                b_turn(m)
                a2_bias(g, 1)
                scores(0, 2)
                a2_scores(g, 2)
                scores(2, 4)
                a2_av(g, 0)
                scores(4, 5)
                a2_bias(g, 2)
                scores(5, 8)
                c1_av(m, 0)
                a2_scores(g, 3)
                a2_av(g, 1)
                scores(8, 10)
                a2_bias(g, 3)
                scores(10, 12)
                c1_av(m, 1)
                a2_av(g, 2)
                scores(12, 16)
                c1_av(m, 2)
                c2_back(m, 0)
                c1_av(m, GB - 1)
                a3_ctx(g)
                c2_back(m, 1)
                a2_av(g, GB - 1)
                a3_k1(g)
                c2_oT(m)
                a3_o0(g)
                c2_o(m)
                a3_v1(g)
                c2_t(m)
                c2_router(m)
                c2_gate(m, 0)
                c2_lgT(m)
                a3_qT(g)
                c2_gate(m, 1)
                c2_up(m, 0)
                a3_qmm(g)
                c2_up(m, 1)
                c2_wT(m)
                c2_down(m, 0)
                c2_blocks(m, 1)
                a3_t2(g)
                c2_blocks(m, 2)
                a3_q1(g)
                c2_blocks(m, 3)
                c2_blocks(m, 4)

            def stage_c(m):
                for u in range(16):
                    b_scores(m, u)
                b_turn(m)
                for b in range(GB):
                    for u in range(4):
                        c1_scores(m, 4 * b + u)
                    if b > 0:
                        c1_av(m, b - 1)
                c2_back(m, 0)
                c1_av(m, GB - 1)
                c2_back(m, 1)
                c2_oT(m)
                c2_o(m)
                c2_t(m)
                c2_router(m)
                c2_gate(m, 0)
                c2_lgT(m)
                c2_gate(m, 1)
                c2_up(m, 0)
                c2_up(m, 1)
                c2_wT(m)
                c2_down(m, 0)
                for i in range(1, NB):
                    c2_blocks(m, i)

            skewed(pe, stage_a, both, stage_c)


_INS = ["x", "ctx", "mask", "pack"]


def kernel(x, ctx_1024, mask_BxS2_bf1, L0_xattn_W_Q, L0_xattn_W_K, L0_xattn_W_V, L0_xattn_W_O, L0_ffn_rhs,
           L1_xattn_Wq, L1_xattn_bq, L1_xattn_Wk, L1_xattn_bk, L1_xattn_Wv, L1_xattn_bv, L1_xattn_Wo, L1_xattn_bo,
           L1_ffn_router_w, L1_ffn_w_gate, L1_ffn_w_up, L1_ffn_w_down, L1_ffn_ws_gate, L1_ffn_ws_up, L1_ffn_ws_down):
    import concourse.bacc as bacc
    from concourse.bass_utils import run_bass_kernel_spmd

    def arr(a):
        return np.asarray(a)

    def experts_in(w, ws):
        return np.concatenate([arr(w).transpose(1, 0, 2).reshape(D, NE * FE), arr(ws)], axis=1)

    def experts_out(w, ws):
        return np.concatenate([arr(w).reshape(NC, 128, D), arr(ws)[None]], axis=0).transpose(1, 0, 2).reshape(128, NB * D)

    p = np.arange(128)
    j4 = np.arange(4)
    e8 = np.arange(NE)
    f = np.float32
    parts = {
        "ident": np.eye(128, dtype=f),
        "wq0": arr(L0_xattn_W_Q).T, "wk0": arr(L0_xattn_W_K).T,
        "wv01": np.concatenate([arr(L0_xattn_W_V).T, arr(L1_xattn_Wv).T], axis=1),
        "mask0": (p[:, None] // DH0 % 4 == j4).astype(f), "mask1": (p[:, None] // DH1 % 4 == j4).astype(f),
        "bq1": arr(L1_xattn_bq)[:, None], "bk1": arr(L1_xattn_bk)[:, None], "bv1": arr(L1_xattn_bv)[:, None],
        "wo0": arr(L0_xattn_W_O).T, "rhsT": arr(L0_ffn_rhs).T,
        "wq1": arr(L1_xattn_Wq).T, "wk1": arr(L1_xattn_Wk).T, "wo1": arr(L1_xattn_Wo).T,
        "bo1": np.broadcast_to(arr(L1_xattn_bo), (128, D)),
        "maskM": (p[:, None] % 4 == j4).astype(f),
        "tri": np.broadcast_to((e8[None, :] < e8[:, None]).astype(f).reshape(1, NE * NE), (128, NE * NE)),
        "router": arr(L1_ffn_router_w),
        "gate": experts_in(L1_ffn_w_gate, L1_ffn_ws_gate), "up": experts_in(L1_ffn_w_up, L1_ffn_ws_up),
        "down": experts_out(L1_ffn_w_down, L1_ffn_ws_down),
        "rowM": (p[:, None] // 4 == np.arange(4 * GB)).astype(f),
        "selW": ((p[:, None, None] % 32 == 2 * np.arange(NC)[None, :, None] + (p // FE)[None, None, :])
                 & (p[:, None, None] < 64)).astype(f).reshape(128, -1),
    }
    arrays = {
        "x": np.ascontiguousarray(arr(x)),
        "ctx": np.ascontiguousarray(arr(ctx_1024)),
        "mask": np.ascontiguousarray(arr(mask_BxS2_bf1)).view(np.uint8),
        "pack": np.ascontiguousarray(np.concatenate([parts[n] for n, _ in PACK], axis=1)),
    }
    nc = bacc.Bacc("TRN2", target_bir_lowering=False, num_devices=1)
    ins = [nc.dram_tensor("in_" + n, arrays[n].shape, mybir.dt.from_np(arrays[n].dtype), kind="ExternalInput").ap() for n in _INS]
    out = nc.dram_tensor("out", (B, S, D), F32, kind="ExternalOutput").ap()
    build(nc, *ins, out)
    r = run_bass_kernel_spmd(nc, [{"in_" + n: a for n, a in arrays.items()}], core_ids=[0])
    return r.results[0]["out"]
```

```python
from contextlib import ExitStack

import numpy as np

import concourse.bass as bass
from concourse import mybir

F32 = mybir.dt.float32
F32R = mybir.dt.float32r
BF16 = mybir.dt.bfloat16
U8 = mybir.dt.uint8
ALU = mybir.AluOpType
ACT = mybir.ActivationFunctionType
AX = mybir.AxisListType

B, S, D = 16, 128, 128
GB = 4
NG = B // GB
T = GB * S
H0, DH0 = 8, 16
H1, DH1 = 16, 8
NE, FE, FS = 8, 64, 128
NC = NE * FE // 128
NB = NC + 1
TOPK = 6
EPS = 1e-5
MAGIC = 12582912.0
INV127 = float(np.float32(1.0) / np.float32(127.0))
SCALE1 = float(np.float32(1.0) / np.sqrt(np.float32(DH1)))

PACK = [("ident", 128), ("wq0", 128), ("wk0", 128), ("wv01", 256), ("mask0", 4), ("mask1", 4),
        ("bq1", 1), ("bk1", 1), ("bv1", 1), ("wo0", 128), ("rhsT", 128), ("wq1", 128), ("wk1", 128), ("wo1", 128),
        ("bo1", 128), ("maskM", 4), ("tri", 64), ("rowM", GB * 4),
        ("router", 8), ("down", NB * 128),
        ("selW", NC * 128), ("gate", NB * 128), ("up", NB * 128)]
COL = {}
_at = 0
for _n, _w in PACK:
    COL[_n] = (_at, _at + _w)
    _at += _w
NPACK = _at
KEPT = COL["selW"][0]
SPLITS = [COL["wo0"][0], COL["router"][0], KEPT]

BANK_USES = {
    "A0": ["lnT0", "Q0", "cfT", "O0p", "V1", "qmm", "Q1"],
    "A1": ["ctxT", "K0", "K1", "qT", "lnT2"],
    "C0": [f"max{u}" for u in range(0, 16, 4)] + [f"s{u}" for u in range(0, 16, 3)] + ["T3", "G0", "G2", "G4"],
    "C1": [f"max{u}" for u in range(1, 16, 4)] + [f"s{u}" for u in range(1, 16, 3)] + ["TO1", "lg", "G1", "G3"],
    "C2": [f"max{u}" for u in range(2, 16, 4)] + [f"s{u}" for u in range(2, 16, 3)] + ["OT0", "OT1", "lgT", "U0", "U2", "U4"],
    "C3": [f"max{u}" for u in range(3, 16, 4)] + ["AV01", "TO0", "O1p0", "O1p1", "U1", "U3"],
    "D": ["MT", "AV23", "WtT", "W0", "W1", "W2", "W3"],
}
LAST_USES = {bank: [use for use in uses if use[:3] != "max"] for bank, uses in BANK_USES.items()}
LAST_USES["A0"] += [f"max{u}" for u in range(0, 16, 2)]
LAST_USES["A1"] += [f"max{u}" for u in range(1, 16, 2)]
for _use, _from, _to in (("G2", "C0", "A0"), ("U2", "C2", "A1")):
    LAST_USES[_from].remove(_use)
    LAST_USES[_to].append(_use)
LAST_USES["D"][:1] = [f"MT{b}" for b in range(GB)]
BANK_OF, LAST_BANK_OF = ({use: bank for bank, uses in table.items() for use in uses} for table in (BANK_USES, LAST_USES))


def is_last(g):
    return isinstance(g, int) and g == NG - 1


def bank_of(g, use):
    return (LAST_BANK_OF if is_last(g) else BANK_OF)[use]


def upto(g, use):
    bank = bank_of(g, use)
    return g * len(BANK_USES[bank]) + (LAST_USES if is_last(g) else BANK_USES)[bank].index(use) + 1


def first_group(g):
    return isinstance(g, int) and g == 0


def wait(eng, sem, value):
    if not (isinstance(value, int) and value <= 0):
        eng.wait_ge(sem, value)


def build(nc, x_d, ctx_d, mask_d, pack_d, out_d):
    with ExitStack() as stack:
        def sb(name, shape, dt=F32):
            return stack.enter_context(nc.sbuf_tensor(name, shape, dt))

        def sem(name):
            return stack.enter_context(nc.semaphore(name))

        pack = sb("pack", [128, KEPT])

        def const(name):
            return pack[:, COL[name][0]:COL[name][1]]

        ident, mask0, mask1, maskM = const("ident"), const("mask0"), const("mask1"), const("maskM")
        down = const("down").rearrange("p (c d) -> p c d", c=NB)
        identr = sb("identr", [128, 128], F32R)
        rowM = sb("rowM", [128, GB * 4], F32R)
        selW = sb("selW", [128, NC, 128], F32R)
        routerH, routerL = sb("routerH", [128, NE], F32R), sb("routerL", [128, NE], F32R)
        guH = sb("guH", [128, 2, NB, 128], F32R)
        guL = sb("guL", [128, 2, NB, 128], F32R)
        rhsq = sb("rhsq", [128, 128], BF16)
        rscale = sb("rscale", [128, 128])
        rq = sb("rq", [128, 2, 128])
        rtmp = sb("rtmp", [128, 4])
        cb1 = sb("cb1", [128, 128])
        ones = sb("ones", [128, 128])
        nhalf = sb("nhalf", [128, GB])
        m8 = sb("m8", [B, S], U8)
        mf = sb("mf", [B, S])
        mcol = sb("mcol", [128, B])
        mkeep = sb("mkeep", [128, B])
        mfill = sb("mfill", [128, B])
        mtmp = sb("mtmp", [128, 3, B])
        mkeep4, mfill4 = sb("mkeep4", [128, GB]), sb("mfill4", [128, GB])

        xin, ctx = sb("xin", [128, GB, D]), sb("ctx", [128, GB, D])
        mk8 = sb("mk8", [128, GB, S], U8)
        mrow, omk, mdiag, fill = (sb(n, [128, GB, S]) for n in ("mrow", "omk", "mdiag", "fill"))
        lnst = [sb(f"lnst{i}", [128, GB, 6]) for i in range(4)]
        lnmv = [sb(f"lnmv{i}", [128, GB, 2]) for i in range(4)]
        lnve, lnrs, lnnm = ([sb(f"{n}{i}", [128, GB]) for i in range(4)] for n in ("lnve", "lnrs", "lnnm"))
        lnx = [sb(f"lnx{i}", [128, GB, D]) for i in (0, 1, 3)]
        lnx.insert(2, lnx[0])
        lnT0, ctxT, cfT = (sb(n, [128, T]) for n in ("lnT0", "ctxT", "cfT"))
        lnT2 = lnT0
        Qm0 = sb("Qm0", [128, 4, T])
        Kg0 = sb("Kg0", [128, 2, T])
        Vm0 = sb("Vm0", [128, GB, H0, 32])
        negM0 = sb("negM0", [128, S], F32R)
        E0 = [sb(f"E0_{i}", [128, H0, S]) for i in range(2)]
        hs = sb("hs", [128, 6, S])
        hsum = [sb(f"hsum{i}", [128, S]) for i in range(2)]
        hrec = [sb(f"hrec{i}", [128, S]) for i in range(2)]
        O0T = sb("O0T", [128, T])
        x1, x2, xb, x3, y3 = (sb(n, [128, GB, D]) for n in ("x1", "x2", "xb", "x3", "y3"))
        amax, lscale, lrec = (sb(n, [128, GB]) for n in ("amax", "lscale", "lrec"))
        qz = sb("qz", [128, GB, D])
        qT = sb("qT", [128, T], BF16)
        qres = qz
        Kh1, Kl1, Qh1, Ql1 = (sb(n, [128, T], F32R) for n in ("Kh1", "Kl1", "Qh1", "Ql1"))
        KS1 = sb("KS1", [96, 4, T], F32R)
        QS1 = sb("QS1", [96, 2, 4, 4, S], F32R)
        Km1 = sb("Km1", [128, 4, T], F32R)
        Qg1 = sb("Qg1", [128, 4, T], F32R)
        VS1 = sb("VS1", [128, GB, H1, 64])
        negM1 = sb("negM1", [128, 128])
        pause, warm = sb("pause", [128, 1]), sb("warm", [128, 1])
        MX = sb("MX", [128, 4, S], F32R)
        E1 = [sb(f"E1_{i}", [128, 4, 4, S]) for i in range(2)]
        raw = E1[1][:].rearrange("p g j q -> p (g j q)")
        raw_sel, raw_gu = raw[:, 0:NC * 128], raw[:, NC * 128:(NC + 2 * NB) * 128]
        OU = sb("OU", [128, GB, 2, S])
        Rq = sb("Rq", [128, 2, 8, 4])
        Oq = sb("Oq", [128, GB, D])
        O1T = sb("O1T", [128, T])
        T3h, T3l = sb("T3h", [128, T], F32R), sb("T3l", [128, T], F32R)
        lgs = sb("lgs", [128, T])
        tk = {n: sb(f"tk_{n}", [128, GB]) for n in ("nmax", "sum", "rec")}
        tke, tkp, rank, Wt = (sb(n, [128, GB, NE]) for n in ("tke", "tkp", "rank", "Wt"))
        ge, gt, gmix = (sb(n, [128, GB, NE, NE]) for n in ("ge", "gt", "gmix"))
        Wx = sb("Wx", [128, T], F32R)
        sg = [sb(f"sg{i}", [128, T]) for i in range(2)]
        hid = [sb(f"hid{i}", [128, T]) for i in range(2)]

        psA = stack.enter_context(nc.psum_tensor("psA", [128, 1024], F32))
        bank = {"A0": psA[:, 0:512], "A1": psA[:, 512:1024]}
        for n in ("C0", "C1", "C2", "C3", "D", "O"):
            if n == "C0":
                psC = stack.enter_context(nc.psum_tensor("psC", [128, 1024], F32))
                bank["C0"], bank["C1"] = psC[:, 0:512], psC[:, 512:1024]
            elif n != "C1":
                bank[n] = stack.enter_context(nc.psum_tensor("ps" + n, [128, 512], F32))[:, :]

        def scores0(g, b):
            return psC if first_group(g) and b % 2 else psA

        k_stack, q_stack = (nc.dram_tensor(n, (3 * D, T), F32).ap() for n in ("k_stack", "q_stack"))
        k_part, q_part = (a.rearrange("(p s) t -> s p t", s=3) for a in (k_stack, q_stack))

        full = {b: sem(f"full_{b}") for b in BANK_USES}
        drained = {b: sem(f"drained_{b}") for b in BANK_USES}
        s_pack = [sem(f"s_pack{i}") for i in range(4)]
        s_mask, s_x, s_ctx, s_mk, s_out = sem("s_mask"), sem("s_x"), sem("s_ctx"), sem("s_mk"), sem("s_out")
        zeroed = sem("zeroed")
        cst = {n: sem("c_" + n) for n in ("ones", "act", "mf", "psT", "mcol", "psN", "mtmp", "masks", "rq",
                                          "psR", "cb", "wlo", "whi", "vs")}
        mk = {n: sem("mk_" + n) for n in ("row", "diag", "four", "fill")}
        ln = [{n: sem(f"ln{i}_{n}") for n in ("stats", "mv", "var", "rstd", "shift", "out", "out2")} for i in range(4)]
        scored0, m0_ready, biased0, exp0 = sem("scored0"), sem("m0_ready"), sem("biased0"), sem("exp0")
        hs_step, hsum_ready, hrec_ready, attn0, av0 = (sem(n) for n in ("hs_step", "hsum_ready", "hrec_ready", "attn0", "av0"))
        o0_drained, v0_full, v0_drained = sem("o0_drained"), sem("v0_full"), sem("v0_drained")
        q_amax, q_scale, q_rec, q_int = (sem(n) for n in ("q_amax", "q_scale", "q_rec", "q_int"))
        x2_ready, xb_ready = sem("x2_ready"), sem("xb_ready")
        kh1_ready, km1_ready, qh1_ready, qg1_dma, ones1_ready = (sem(n) for n in ("kh1_ready", "km1_ready", "qh1_ready",
                                                                                  "qg1_dma", "ones1_ready"))
        k_written, q_written, ks1_dma = sem("k_written"), sem("q_written"), sem("ks1_dma")
        qs1_dma = [sem(f"qs1_dma{i}") for i in range(2)]
        rec1, av_even = sem("rec1"), sem("av_even")
        t3h_ready = sem("t3h_ready")
        tks = {n: sem("tk_" + n) for n in ("max", "exp", "sum", "rec", "p", "gt", "ge", "mix", "max2", "rank", "w")}
        wxh_ready = sem("wxh_ready")
        y_drained = sem("y_drained")
        down_done = sem("down_done")

        def bank3(name, n=GB):
            return bank[name].rearrange("p (b d) -> p b d", b=n)

        block = stack.enter_context(nc.Block())

        def skewed(eng, stage_a, both, stage_c):
            stage_a(0)
            with eng.Fori(1, NG - 1) as g:
                both(g)
            both(NG - 1)
            stage_c(NG - 1)

        def has_next(g):
            return not (isinstance(g, int) and g == NG - 1)

        @block.sync
        def _(sp):
            def load_x(g):
                if not first_group(g):
                    sp.wait_ge(drained["A0"], upto(g - 1, "O0p"))
                sp.dma_start(xin[:], x_d[bass.ts(g, GB)].rearrange("b t d -> t b d")).then_inc(s_x, 16)

            def load_ctx(g):
                if not first_group(g):
                    sp.wait_ge(mk["row"], g)
                    sp.wait_ge(full["A0"], upto(g - 1, "cfT"))
                sp.dma_start(ctx[:], ctx_d[bass.ts(g, GB)].rearrange("b t d -> t b d")).then_inc(s_ctx, 16)
                sp.dma_start(mk8[:], mask_d[bass.ts(g, GB)].partition_broadcast(128)).then_inc(s_mk, 16)

            def keys_out(g):
                sp.wait_ge(kh1_ready, g + 1)
                sp.dma_start(k_part[0], Kh1[:].bitcast(F32)).then_inc(k_written, 16)
                sp.dma_start(k_part[2], Kh1[:].bitcast(F32)).then_inc(k_written, 16)
                sp.wait_ge(drained["A1"], upto(g, "K1"))
                sp.dma_start(k_part[1], Kl1[:].bitcast(F32)).then_inc(k_written, 16)

            def keys_in(g):
                sp.wait_ge(k_written, 48 * g + 48)
                sp.dma_start(KS1[:].bitcast(F32), k_stack.rearrange("(w r) t -> r w t", w=4)).then_inc(ks1_dma, 16)

            def queries_out(g):
                sp.wait_ge(qh1_ready, g + 1)
                for G in range(4):
                    r = slice(32 * G, 32 * G + 32)
                    sp.dma_start(Qg1[r, G, :].bitcast(F32), Qh1[r, :].bitcast(F32)).then_inc(qg1_dma, 16)
                for part in range(2):
                    sp.dma_start(q_part[part], Qh1[:].bitcast(F32)).then_inc(q_written, 16)
                sp.wait_ge(drained["A0"], upto(g, "Q1"))
                sp.dma_start(q_part[2], Ql1[:].bitcast(F32)).then_inc(q_written, 16)

            def queries_in(g, b):
                if b == 0:
                    sp.wait_ge(q_written, 48 * g + 48)
                if b >= 2:
                    use = f"s{4 * b - 5}"
                    sp.wait_ge(full[BANK_OF[use]], upto(g, use))
                src = q_stack.rearrange("(w j r) t -> j r w t", w=4, j=4)
                for j in range(4):
                    sp.dma_start(QS1[24 * j:24 * j + 24, b % 2, :, j].bitcast(F32),
                                 src[j][:, :, 128 * b:128 * b + 128]).then_inc(qs1_dma[b % 2], 16)

            def store(m):
                sp.wait_ge(y_drained, m + 1)
                sp.dma_start(out_d[bass.ts(m, GB)].rearrange("b t d -> t b d"), y3[:]).then_inc(s_out, 16)

            load_x(0)
            sp.dma_start(m8[:], mask_d).then_inc(s_mask, 16)
            at = 0
            for i, end in enumerate(SPLITS):
                sp.dma_start(pack[:, at:end], pack_d[:, at:end]).then_inc(s_pack[i], 16)
                at = end
                if i == 0:
                    load_ctx(0)
            sp.dma_start(raw[:, 0:NPACK - KEPT], pack_d[:, KEPT:]).then_inc(s_pack[3], 16)

            def stage_a(g):
                keys_out(g)
                if has_next(g):
                    load_ctx(g + 1)
                    load_x(g + 1)
                if first_group(g):
                    sp.wait_ge(zeroed, 9)
                queries_out(g)
                keys_in(g)
                queries_in(g, 0)
                queries_in(g, 1)

            def both(g):
                queries_in(g - 1, 2)
                queries_in(g - 1, 3)
                stage_a(g)
                store(g - 1)

            def stage_c(m):
                queries_in(m, 2)
                queries_in(m, 3)
                store(m)

            skewed(sp, stage_a, both, stage_c)
            sp.wait_ge(s_out, 16 * NG + 1)

        @block.gpsimd
        def _(pool):
            p = nc.gpsimd
            p.memset(nhalf[:], -0.5).then_inc(zeroed, 1)

            def zero(*tensors):
                for t in tensors:
                    a = t[:]
                    p.memset(a.bitcast(F32) if a.dtype == F32R else a, 0.0).then_inc(zeroed, 1)

            def rstd(i, g):
                pool.wait_ge(ln[i]["var"], g + 1)
                p.tensor_tensor(lnrs[i][:], lnve[i][:], nhalf[:], ALU.pow).then_inc(ln[i]["rstd"], 1)

            def masks(g):
                pool.wait_ge(mk["row"], g + 1)
                wait(pool, mk["fill"], g * GB)
                p.tensor_tensor(omk[:], ones[:].unsqueeze(1).to_broadcast([128, GB, 128]), mrow[:], ALU.subtract)
                p.tensor_tensor(mdiag[:], mrow[:], ident.unsqueeze(1).to_broadcast([128, GB, 128]),
                                ALU.mult).then_inc(mk["diag"], 1)

            def headsum(g, b):
                n = GB * g + b
                pool.wait_ge(exp0, n + 1)
                e = E0[b % 2]
                if b >= 2 or not first_group(g):
                    pool.wait_ge(hrec_ready, n - 1)
                p.tensor_tensor(hs[:, 0:4], e[:, 0:4], e[:, 4:8], ALU.add).then_inc(hs_step, 1)
                pool.wait_ge(hs_step, 2 * n + 1)
                p.tensor_tensor(hs[:, 4:6], hs[:, 0:2], hs[:, 2:4], ALU.add).then_inc(hs_step, 1)
                pool.wait_ge(hs_step, 2 * n + 2)
                p.tensor_tensor(hsum[b % 2][:], hs[:, 4], hs[:, 5], ALU.add).then_inc(hsum_ready, 1)

            def bias_residual(g):
                pool.wait_ge(x2_ready, g + 1)
                pool.wait_ge(cst["cb"], 1)
                if not first_group(g):
                    pool.wait_ge(drained["C3"], upto(g - 1, "O1p1"))
                p.tensor_tensor(xb[:], x2[:], cb1[:].unsqueeze(1).to_broadcast([128, GB, D]), ALU.add).then_inc(xb_ready, 1)

            def stage_a(g):
                p.memset(ones[:], 1.0).then_inc(cst["ones"], 1)
                pool.wait_ge(zeroed, 1)
                p.memset(y3[:], 0.0).then_inc(s_out, 1)
                rstd(0, g)
                pool.wait_ge(s_pack[0], 16)
                zero(Kg0, Vm0)
                masks(g)
                pool.wait_ge(cst["ones"], 1)
                zero(negM1, MX, lgs, Wx)
                headsum(g, 0)
                headsum(g, 1)
                headsum(g, 2)
                headsum(g, 3)
                zero(Qg1)
                zero(QS1)
                rstd(1, g)
                pool.wait_ge(s_pack[1], 16)
                bias_residual(g)
                rstd(2, g)
                rstd(0, g + 1)

            def both(g):
                masks(g)
                for b in range(GB):
                    headsum(g, b)
                rstd(3, g - 1)
                rstd(1, g)
                if has_next(g):
                    rstd(0, g + 1)
                rstd(2, g)
                bias_residual(g)

            def stage_c(m):
                rstd(3, m)

            skewed(pool, stage_a, both, stage_c)

        @block.scalar
        def _(act):
            a = nc.scalar

            def wfull(use, g):
                act.wait_ge(full[bank_of(g, use)], upto(g, use))

            def normalize(i, src, g):
                act.wait_ge(ln[i]["shift"], g + 1)
                if i == 0:
                    wait(act, full["A1"], prev(g, "lnT2"))
                elif i == 1:
                    wait(act, q_int, g)
                elif i == 2:
                    act.wait_ge(full["A0"], upto(g, "lnT0"))
                for b in range(GB // 2):
                    ins = a.activation(lnx[i][:, b], src[:, b], ACT.Identity, bias=lnnm[i][:, b:b + 1],
                                       scale=lnrs[i][:, b:b + 1])
                ins.then_inc(ln[i]["out"], 1)

            def prev(g, use):
                return 0 if first_group(g) else upto(g - 1, use)

            def a1_ln(g):
                act.wait_ge(s_x, 16 * g + 16)
                normalize(0, xin, g)

            def a1_t(g):
                wfull("lnT0", g)
                a.copy(lnT0[:], bank["A0"]).then_inc(drained["A0"], 1)
                wfull("ctxT", g)
                a.copy(ctxT[:], bank["A1"]).then_inc(drained["A1"], 1)

            def a1_k(g):
                wfull("K0", g)
                wait(act, biased0, GB * g)
                a.copy(Kg0[0:64, 0], bank["A1"][0:64])
                a.copy(Kg0[64:128, 1], bank["A1"][64:128]).then_inc(drained["A1"], 1)

            def a1_q(g):
                wfull("Q0", g)
                wait(act, biased0, GB * g)
                for j in range(4):
                    ins = a.activation(Qm0[:, j], bank["A0"], ACT.Copy, scale=mask0[:, j:j + 1])
                ins.then_inc(drained["A0"], 1)

            def a1_v(g):
                act.wait_ge(v0_full, g + 1)
                wait(act, av0, GB * g)
                dst = bass.AP(tensor=Vm0[:].tensor, offset=0, ap=[[GB * H0 * 32, 128], [64, GB * 4], [48, 2], [1, DH0]])
                a.copy(dst, bank["O"].rearrange("p (n j d) -> p n j d", j=2, d=DH0)).then_inc(v0_drained, 1)

            def a2_exp(g, b):
                n = GB * g + b
                act.wait_ge(biased0, n + 1)
                if b >= 2 or not first_group(g):
                    act.wait_ge(av0, n - 1)
                a.activation(E0[b % 2][:].rearrange("p h q -> p (h q)"), scores0(g, b)[:, :], ACT.Exp, scale=0.25).then_inc(exp0, 1)

            def a3_o0(g):
                act.wait_ge(av0, GB * g + GB)
                wait(act, full["A0"], prev(g, "O0p"))
                a.copy(O0T[:], bank["O"]).then_inc(o0_drained, 1)

            def a3_ctx(g):
                wfull("cfT", g)
                wait(act, full["A1"], prev(g, "K1"))
                a.copy(cfT[:], bank["A0"]).then_inc(drained["A0"], 1)

            def a3_k1(g):
                wfull("K1", g)
                wait(act, k_written, 48 * g)
                a.activation(Kh1[:], bank["A1"], ACT.Identity, bias=const("bk1")).then_inc(kh1_ready, 1)

            def a3_km(g):
                act.wait_ge(kh1_ready, g + 1)
                for j in range(4):
                    a.activation(Km1[:, j], Kh1[:].bitcast(F32), ACT.Copy, scale=mask1[:, j:j + 1]).then_inc(km1_ready, 1)

            def a3_v1(g):
                wfull("V1", g)
                act.wait_ge(mk["four"], g + 1)
                if first_group(g):
                    act.wait_ge(cst["vs"], 1)
                for b in range(GB):
                    dst = bass.AP(tensor=VS1[:].tensor, offset=b * H1 * 64,
                                  ap=[[GB * H1 * 64, 128], [4 * 64, 4], [72, 4], [1, DH1]])
                    src = bank["A0"][:, 128 * b:128 * b + 128].rearrange("p (w j d) -> p w j d", w=4, j=4)
                    ins = a.activation(dst, src, ACT.Copy, scale=mkeep4[:, b:b + 1])
                ins.then_inc(drained["A0"], 1)

            def a3_t2(g):
                wfull("lnT2", g)
                a.copy(lnT2[:], bank["A1"]).then_inc(drained["A1"], 1)

            def a3_q1(g):
                wfull("Q1", g)
                wait(act, q_written, 48 * g)
                wait(act, qg1_dma, 64 * g)
                a.activation(Qh1[:], bank["A0"], ACT.Identity, bias=const("bq1")).then_inc(qh1_ready, 1)

            def warm_exp():
                a.activation(warm[:], ident[:, 0:1], ACT.Exp)

            def c1_exp(m, u):
                use = f"s{u}"
                wfull(use, m)
                if u == 8:
                    act.wait_ge(av_even, 2 * m + 1)
                elif u == 12:
                    act.wait_ge(full["C3"], upto(m, "AV01"))
                a.activation(E1[u // 4 % 2][:, u % 4].rearrange("p j q -> p (j q)"), bank[BANK_OF[use]], ACT.Exp,
                             scale=SCALE1).then_inc(drained[BANK_OF[use]], 1)

            def c1_out(m, half):
                use = ("AV01", "AV23")[half]
                wfull(use, m)
                a.copy(OU[:, 2 * half:2 * half + 2].rearrange("p b w q -> p (b w q)"),
                       bank[BANK_OF[use]]).then_inc(drained[BANK_OF[use]], 1)

            def c2_oT(m, half):
                wfull(f"OT{half}", m)
                cols = slice(256 * half, 256 * half + 256)
                a.copy(O1T[:, cols], bank["C2"][:, cols]).then_inc(drained["C2"], 1)

            def c2_ln(m):
                normalize(3, x3, m)

            def c2_t(m):
                wfull("T3", m)
                a.copy(T3h[:], bank["C0"]).then_inc(t3h_ready, 1)

            def c2_router(m):
                wfull("lg", m)
                a.copy(lgs[0:NE, :], bank["C1"][0:NE, :]).then_inc(drained["C1"], 1)

            def c2_exp(m):
                act.wait_ge(drained["C2"], upto(m, "lgT"))
                a.activation(tke[:], tke[:], ACT.Exp).then_inc(tks["exp"], 1)

            def c2_w(m):
                wfull("WtT", m)
                a.copy(Wx[0:NE, :], bank["D"][0:NE, :]).then_inc(wxh_ready, 1)

            def c2_silu(m, i):
                wfull(f"G{i}", m)
                if i >= 2:
                    last = "U0" if i == 2 else f"W{i - 3}"
                    act.wait_ge(drained[bank_of(m, last)], upto(m, last))
                bG = bank_of(m, f"G{i}")
                a.activation(sg[i % 2][:], bank[bG], ACT.Silu).then_inc(drained[bG], 1)

            act.wait_ge(s_pack[0], 16)
            a.copy(identr[:], ident).then_inc(cst["act"], 1)

            def late_constants():
                act.wait_ge(s_pack[1], 16)
                act.wait_ge(s_pack[2], 16)
                act.wait_ge(s_pack[3], 16)
                a.copy(routerH[:], const("router"))
                a.copy(guH[:].rearrange("p k c f -> p (k c f)"), raw_gu)
                a.copy(rowM[:], const("rowM"))
                a.copy(selW[:].rearrange("p c k -> p (c k)"), raw_sel).then_inc(cst["whi"], 1)

            def stage_a(g):
                a1_ln(g)
                a1_t(g)
                act.wait_ge(zeroed, 3)
                a1_q(g)
                a1_k(g)
                a1_v(g)
                for b in range(GB):
                    a2_exp(g, b)
                    if b == 0:
                        late_constants()
                a3_ctx(g)
                a3_o0(g)
                a3_k1(g)
                normalize(1, x1, g)
                a3_km(g)
                a3_v1(g)
                normalize(2, x2, g)
                a3_t2(g)
                a3_q1(g)
                a1_ln(g + 1)
                a1_t(g + 1)
                act.wait_ge(zeroed, 9)

            def both(g):
                m = g - 1

                def exps(begin, end):
                    for u in range(begin, end):
                        c1_exp(m, u)

                a1_q(g)
                a1_k(g)
                a2_exp(g, 0)
                a2_exp(g, 1)
                a1_v(g)
                exps(0, 4)
                a2_exp(g, 2)
                exps(4, 10)
                a2_exp(g, 3)
                exps(10, 13)
                c1_out(m, 0)
                exps(13, 16)
                c2_oT(m, 0)
                a3_ctx(g)
                c1_out(m, 1)
                a3_o0(g)
                c2_oT(m, 1)
                a3_k1(g)
                a3_v1(g)
                c2_ln(m)
                c2_t(m)
                normalize(1, x1, g)
                c2_router(m)
                a3_km(g)
                c2_exp(m)
                c2_silu(m, 0)
                c2_silu(m, 1)
                c2_w(m)
                c2_silu(m, 2)
                normalize(2, x2, g)
                a3_t2(g)
                c2_silu(m, 3)
                c2_silu(m, 4)
                a3_q1(g)
                warm_exp()
                if has_next(g):
                    a1_ln(g + 1)
                    a1_t(g + 1)

            def stage_c(m):
                for u in range(16):
                    c1_exp(m, u)
                    if u == 11:
                        c1_out(m, 0)
                c2_oT(m, 0)
                c1_out(m, 1)
                c2_oT(m, 1)
                c2_ln(m)
                c2_t(m)
                c2_router(m)
                c2_exp(m)
                c2_silu(m, 0)
                c2_w(m)
                c2_silu(m, 1)
                for i in range(2, NB):
                    c2_silu(m, i)

            skewed(act, stage_a, both, stage_c)

        @block.vector
        def _(dve):
            v = nc.vector

            def wfull(use, g):
                dve.wait_ge(full[bank_of(g, use)], upto(g, use))

            def stats(i, src, g):
                for b in range(GB):
                    ins = v.bn_stats(lnst[i][:, b], src[:, b])
                ins.then_inc(ln[i]["stats"], 1)
                dve.wait_ge(ln[i]["stats"], g + 1)
                aggregate(i, g)

            def aggregate(i, g):
                v.memset(pause[:], 0.0)
                for b in range(GB):
                    ins = v.bn_aggr(lnmv[i][:, b], lnst[i][:, b])
                ins.then_inc(ln[i]["mv"], 1)
                dve.wait_ge(ln[i]["mv"], g + 1)
                v.tensor_scalar(lnve[i][:], lnmv[i][:, :, 1], EPS, None, ALU.add).then_inc(ln[i]["var"], 1)

            def shift(i, g):
                dve.wait_ge(ln[i]["rstd"], g + 1)
                v.scalar_tensor_tensor(out=lnnm[i][:], in0=lnmv[i][:, :, 0], scalar=-1.0, in1=lnrs[i][:],
                                       op0=ALU.mult, op1=ALU.mult).then_inc(ln[i]["shift"], 1)

            def normalize(i, src, g):
                shift(i, g)
                if i == 0 and not first_group(g):
                    dve.wait_ge(full["A1"], upto(g - 1, "lnT2"))
                elif i == 2:
                    dve.wait_ge(full["A0"], upto(g, "lnT0"))
                for b in range(GB // 2, GB):
                    ins = v.tensor_scalar(lnx[i][:, b], src[:, b], lnmv[i][:, b, 0:1], lnrs[i][:, b:b + 1], ALU.subtract,
                                          ALU.mult)
                ins.then_inc(ln[i]["out2"], 1)

            def a1_mask(g):
                dve.wait_ge(s_mk, 16 * g + 16)
                wait(dve, mk["diag"], g)
                v.tensor_copy(mrow[:], mk8[:]).then_inc(mk["row"], 1)

            def a2_max(g, b):
                dve.wait_ge(scored0, GB * g + b + 1)
                if b > 0 or not first_group(g):
                    dve.wait_ge(biased0, GB * g + b)
                v.tensor_reduce(negM0[:], scores0(g, b)[:, :].rearrange("p (h q) -> p q h", h=H0), AX.X, ALU.max,
                                negate=True).then_inc(m0_ready, 1)

            def a2_norm(g, b):
                n = GB * g + b
                dve.wait_ge(hsum_ready, n + 1)
                if b >= 2 or not first_group(g):
                    dve.wait_ge(attn0, n - 1)
                v.reciprocal(hrec[b % 2][:], hsum[b % 2][:]).then_inc(hrec_ready, 1)
                dve.wait_ge(hrec_ready, n + 1)
                e = E0[b % 2]
                v.tensor_tensor(e[:], e[:], hrec[b % 2][:].unsqueeze(1).to_broadcast([128, H0, S]), ALU.mult).then_inc(attn0, 1)

            def a3_fill(g):
                if not first_group(g):
                    dve.wait_ge(drained["A0"], upto(g - 1, "V1"))
                    dve.wait_ge(full["A0"], upto(g - 1, "cfT"))
                v.tensor_copy(mkeep4[:], mkeep[:, bass.ts(g, GB)])
                v.tensor_copy(mfill4[:], mfill[:, bass.ts(g, GB)]).then_inc(mk["four"], 1)
                dve.wait_ge(mk["four"], g + 1)
                dve.wait_ge(mk["diag"], g + 1)
                for b in range(GB):
                    v.scalar_tensor_tensor(out=fill[:, b], in0=omk[:, b], scalar=mfill4[:, b:b + 1], in1=mdiag[:, b],
                                           op0=ALU.mult, op1=ALU.add).then_inc(mk["fill"], 1)

            def a3_sums(g):
                if not first_group(g):
                    dve.wait_ge(full["D"], upto(g - 1, "AV23"))
                dst = bass.AP(tensor=VS1[:].tensor, offset=32, ap=[[GB * H1 * 64, 128], [H1 * 64, GB], [256, 4], [65, 4]])
                src = mkeep4[:].unsqueeze(2).unsqueeze(3).to_broadcast([128, GB, 4, 4])
                v.tensor_copy(dst, src).then_inc(ones1_ready, 1)

            def a3_k1(g):
                dve.wait_ge(kh1_ready, g + 1)
                wait(dve, k_written, 48 * g)
                v.scalar_tensor_tensor(out=Kl1[:], in0=bank["A1"], scalar=const("bk1"), in1=Kh1[:].bitcast(F32),
                                       op0=ALU.add, op1=ALU.subtract).then_inc(drained["A1"], 1)

            def a3_x1(g):
                wfull("O0p", g)
                v.tensor_tensor(x1[:], bank3("A0"), xin[:], ALU.add).then_inc(drained["A0"], 1)

            def a3_stats1(g):
                dve.wait_ge(drained["A0"], upto(g, "O0p"))
                stats(1, x1, g)

            def a3_quant(g):
                dve.wait_ge(ln[1]["out"], g + 1)
                dve.wait_ge(ln[1]["out2"], g + 1)
                v.tensor_reduce(amax[:], lnx[1][:], AX.X, ALU.max, apply_absolute_value=True).then_inc(q_amax, 1)
                dve.wait_ge(q_amax, g + 1)
                v.tensor_scalar(lscale[:], amax[:], 1e-12, INV127, ALU.max, ALU.mult).then_inc(q_scale, 1)
                dve.wait_ge(q_scale, g + 1)
                v.reciprocal(lrec[:], lscale[:]).then_inc(q_rec, 1)
                dve.wait_ge(q_rec, g + 1)
                for b in range(GB):
                    ins = v.tensor_scalar(qz[:, b], lnx[1][:, b], lrec[:, b:b + 1], MAGIC, ALU.mult, ALU.add)
                ins.then_inc(q_int, 1)

            def a3_qT(g):
                wfull("qT", g)
                v.tensor_scalar(qT[:], bank["A1"], -MAGIC, None, ALU.add).then_inc(drained["A1"], 1)

            def a3_x2(g):
                wfull("qmm", g)
                for b in range(GB):
                    ins = v.scalar_tensor_tensor(out=qres[:, b], in0=bank3("A0")[:, b], scalar=lscale[:, b:b + 1],
                                                 in1=rscale[:], op0=ALU.mult, op1=ALU.mult)
                ins.then_inc(drained["A0"], 1)
                dve.wait_ge(drained["A0"], upto(g, "qmm"))
                wait(dve, xb_ready, g)
                v.tensor_tensor(x2[:], x1[:], qres[:], ALU.add).then_inc(x2_ready, 1)

            def a3_stats2(g):
                dve.wait_ge(x2_ready, g + 1)
                stats(2, x2, g)

            def a3_q1(g):
                dve.wait_ge(qh1_ready, g + 1)
                wait(dve, q_written, 48 * g)
                v.scalar_tensor_tensor(out=Ql1[:], in0=bank["A0"], scalar=const("bq1"), in1=Qh1[:].bitcast(F32),
                                       op0=ALU.add, op1=ALU.subtract).then_inc(drained["A0"], 1)

            def b_max(m, u):
                use = f"max{u}"
                wfull(use, m)
                v.tensor_reduce(negM1[:, 4 * u:4 * u + 4], bank[bank_of(m, use)].rearrange("p (j k) -> p j k", j=4), AX.X,
                                ALU.max, negate=True).then_inc(drained[bank_of(m, use)], 1)

            def b_mx(m, b=None):
                if b is None:
                    wfull("MT", m)
                else:
                    wfull(f"MT{b}", m)
                    if b > 0:
                        wfull(f"s{4 * b - 1}", m)
                src = bank["D"][0:64, 0:128].unsqueeze(1).to_broadcast([64, 4, 128])
                v.tensor_tensor(MX[0:64], src, maskM[0:64].unsqueeze(2).to_broadcast([64, 4, 128]),
                                ALU.mult).then_inc(drained["D"], 1)

            def c2_rec(m, half):
                use = f"TO{half}"
                wfull(use, m)
                ps = bank[BANK_OF[use]].rearrange("p (n c) -> p n c", n=8)
                v.reciprocal(Rq[:, half], ps[:, :, 32:36]).then_inc(rec1, 1)
                dve.wait_ge(rec1, 2 * m + half + 1)
                out = Oq[:, 2 * half:2 * half + 2].rearrange("p b (n j d) -> p (b n) j d", j=4, d=DH1)
                v.tensor_tensor(out, ps[:, :, 0:32].rearrange("p n (j d) -> p n j d", j=4),
                                Rq[:, half].unsqueeze(3).to_broadcast([128, 8, 4, DH1]),
                                ALU.mult).then_inc(drained[BANK_OF[use]], 1)

            def c2_x3(m, half):
                use = f"O1p{half}"
                wfull(use, m)
                dve.wait_ge(xb_ready, m + 1)
                pair = slice(2 * half, 2 * half + 2)
                v.tensor_tensor(x3[:, pair], bank3("C3")[:, pair], xb[:, pair], ALU.add).then_inc(drained["C3"], 1)
                dve.wait_ge(drained["C3"], upto(m, use))
                for b in (2 * half, 2 * half + 1):
                    ins = v.bn_stats(lnst[3][:, b], x3[:, b])
                ins.then_inc(ln[3]["stats"], 1)
                if half:
                    dve.wait_ge(ln[3]["stats"], 2 * m + 2)
                    aggregate(3, m)

            def c2_t(m):
                dve.wait_ge(t3h_ready, m + 1)
                v.tensor_tensor(T3l[:], bank["C0"], T3h[:].bitcast(F32), ALU.subtract).then_inc(drained["C0"], 1)

            def c2_soft(m):
                wfull("lgT", m)
                lg = bank3("C2")[:, :, 0:NE]
                v.tensor_reduce(tk["nmax"][:], lg, AX.X, ALU.max, negate=True).then_inc(tks["max"], 1)
                dve.wait_ge(tks["max"], m + 1)
                v.tensor_tensor(tke[:], lg, tk["nmax"][:].unsqueeze(2).to_broadcast([128, GB, NE]), ALU.add)\
                    .then_inc(drained["C2"], 1)

            def c2_topk(m):
                dve.wait_ge(tks["exp"], m + 1)
                v.tensor_reduce(tk["sum"][:], tke[:], AX.X, ALU.add).then_inc(tks["sum"], 1)
                dve.wait_ge(tks["sum"], m + 1)
                v.reciprocal(tk["rec"][:], tk["sum"][:]).then_inc(tks["rec"], 1)
                dve.wait_ge(tks["rec"], m + 1)
                v.tensor_tensor(tkp[:], tke[:], tk["rec"][:].unsqueeze(2).to_broadcast([128, GB, NE]), ALU.mult)\
                    .then_inc(tks["p"], 1)
                dve.wait_ge(tks["p"], m + 1)
                pj = tkp[:].unsqueeze(2).to_broadcast([128, GB, NE, NE])
                pi = tkp[:].unsqueeze(3).to_broadcast([128, GB, NE, NE])
                v.tensor_tensor(gt[:], pj, pi, ALU.is_gt)
                v.tensor_tensor(ge[:], pj, pi, ALU.is_ge).then_inc(tks["ge"], 1)

            def c2_keep(m):
                dve.wait_ge(tks["ge"], m + 1)
                tri = const("tri").rearrange("p (i j) -> p i j", i=NE).unsqueeze(1).to_broadcast([128, GB, NE, NE])
                v.tensor_tensor(gmix[:], ge[:], tri, ALU.mult).then_inc(tks["mix"], 1)
                dve.wait_ge(tks["mix"], m + 1)
                v.tensor_tensor(gt[:], gt[:], gmix[:], ALU.max).then_inc(tks["max2"], 1)
                dve.wait_ge(tks["max2"], m + 1)
                v.tensor_reduce(rank[:], gt[:], AX.X, ALU.add).then_inc(tks["rank"], 1)
                dve.wait_ge(tks["rank"], m + 1)
                v.scalar_tensor_tensor(out=Wt[:], in0=rank[:], scalar=TOPK - 0.5, in1=tkp[:], op0=ALU.is_lt,
                                       op1=ALU.mult).then_inc(tks["w"], 1)

            def c2_w(m):
                dve.wait_ge(wxh_ready, m + 1)
                v.tensor_tensor(Wx[32:32 + NE, :], bank["D"][0:NE, :], Wx[0:NE, :].bitcast(F32),
                                ALU.subtract).then_inc(drained["D"], 1)

            def c2_hidden(m, i):
                bG, bU = bank_of(m, f"G{i}"), bank_of(m, f"U{i}")
                dve.wait_ge(drained[bG], upto(m, f"G{i}"))
                wfull(f"U{i}", m)
                if i == 0:
                    v.tensor_tensor(hid[0][:], sg[0][:], bank[bU], ALU.mult).then_inc(drained[bU], 1)
                else:
                    v.tensor_tensor(sg[i % 2][:], sg[i % 2][:], bank[bU], ALU.mult).then_inc(drained[bU], 1)

            def c2_weigh(m, i):
                n, bU = NB * m + i, bank_of(m, f"U{i}")
                wfull(f"W{i - 1}", m)
                dve.wait_ge(drained[bU], upto(m, f"U{i}"))
                if i >= 2:
                    dve.wait_ge(down_done, n - 1)
                v.tensor_tensor(hid[i % 2][:], sg[i % 2][:], bank["D"], ALU.mult).then_inc(drained["D"], 1)

            def c2_out(m):
                dve.wait_ge(down_done, NB * m + NB)
                dve.wait_ge(s_out, 16 * m + 1)
                v.tensor_tensor(y3[:], bank3("O"), x3[:], ALU.add).then_inc(y_drained, 1)

            def setup():
                dve.wait_ge(s_mask, 16)
                v.tensor_copy(mf[:], m8[:]).then_inc(cst["mf"], 1)
                dve.wait_ge(cst["psT"], 1)
                v.tensor_copy(mcol[:], bank["C0"][:, 0:B]).then_inc(cst["mcol"], 1)
                dve.wait_ge(cst["psN"], 1)
                dve.wait_ge(cst["mcol"], 1)
                v.tensor_scalar(mtmp[:, 0], bank["C1"][:, 0:B], 1.0, None, ALU.max).then_inc(cst["mtmp"], 1)
                v.tensor_scalar(mtmp[:, 2], bank["C1"][:, 0:B], 0.5, None, ALU.is_lt).then_inc(cst["mtmp"], 1)
                dve.wait_ge(cst["mtmp"], 2)
                v.reciprocal(mtmp[:, 1], mtmp[:, 0]).then_inc(cst["mtmp"], 1)
                v.tensor_tensor(mkeep[:], mcol[:], mtmp[:, 2], ALU.add).then_inc(cst["masks"], 1)
                dve.wait_ge(cst["mtmp"], 3)
                v.tensor_tensor(mfill[:], mcol[:], mtmp[:, 1], ALU.mult).then_inc(cst["masks"], 1)
                dve.wait_ge(cst["masks"], 2)

            def setup2():
                dve.wait_ge(s_pack[1], 16)
                v.tensor_reduce(rtmp[:, 0:1], const("rhsT"), AX.X, ALU.max, apply_absolute_value=True).then_inc(cst["rq"], 1)
                dve.wait_ge(cst["rq"], 1)
                v.tensor_scalar(rtmp[:, 1:2], rtmp[:, 0:1], 1e-12, INV127, ALU.max, ALU.mult).then_inc(cst["rq"], 1)
                dve.wait_ge(cst["rq"], 2)
                v.reciprocal(rtmp[:, 2:3], rtmp[:, 1:2]).then_inc(cst["rq"], 1)
                dve.wait_ge(cst["rq"], 3)
                v.tensor_scalar(rq[:, 0], const("rhsT"), rtmp[:, 2:3], MAGIC, ALU.mult, ALU.add).then_inc(cst["rq"], 1)
                v.tensor_copy(rq[:, 1], rtmp[:, 1:2].to_broadcast([128, 128])).then_inc(cst["rq"], 1)
                dve.wait_ge(s_out, 1)
                v.tensor_copy(y3[:, 0], const("bv1").to_broadcast([128, 128])).then_inc(cst["rq"], 1)

            def setup2_end():
                dve.wait_ge(cst["psR"], 1)
                v.tensor_scalar(rhsq[:], bank["C2"][:, 0:128], -MAGIC, None, ALU.add)
                v.tensor_copy(rscale[:], bank["C2"][:, 128:256])
                v.tensor_tensor(cb1[:], bank["C2"][:, 256:384], const("bo1"), ALU.add).then_inc(cst["cb"], 1)

            def setup3():
                dve.wait_ge(s_pack[2], 16)
                dve.wait_ge(cst["whi"], 1)
                v.tensor_tensor(routerL[:], const("router"), routerH[:].bitcast(F32), ALU.subtract)
                dve.wait_ge(s_pack[3], 16)
                v.tensor_tensor(guL[:].rearrange("p k c f -> p (k c f)"), raw_gu,
                                guH[:].rearrange("p k c f -> p (k c f)").bitcast(F32), ALU.subtract).then_inc(cst["wlo"], 1)

            def a1_stats(g):
                dve.wait_ge(s_x, 16 * g + 16)
                stats(0, xin, g)

            def stage_a(g):
                a1_stats(g)
                setup()
                dve.wait_ge(s_pack[0], 16)
                normalize(0, xin, g)
                v.memset(VS1[:], 0.0).then_inc(cst["vs"], 1)
                a1_mask(g)
                dve.wait_ge(cst["vs"], 1)
                a3_fill(g)
                a3_sums(g)
                a2_max(g, 0)
                setup2()
                a2_max(g, 1)
                a2_norm(g, 0)
                setup2_end()
                for b in range(2, GB):
                    a2_max(g, b)
                    a2_norm(g, b - 1)
                a2_norm(g, GB - 1)
                setup3()
                a3_x1(g)
                a3_stats1(g)
                a3_k1(g)
                normalize(1, x1, g)
                a3_quant(g)
                a3_qT(g)
                a3_x2(g)
                a3_stats2(g)
                a1_stats(g + 1)
                normalize(2, x2, g)
                normalize(0, xin, g + 1)
                dve.wait_ge(zeroed, 9)
                a3_q1(g)

            def both(g):
                m = g - 1

                def maxima(begin, end):
                    for u in range(begin, end):
                        b_max(m, u)

                a1_mask(g)
                maxima(0, 10)
                a2_max(g, 0)
                maxima(10, 16)
                a2_max(g, 1)
                b_mx(m)
                a2_norm(g, 0)
                a3_fill(g)
                a2_max(g, 2)
                a2_norm(g, 1)
                a2_max(g, 3)
                a2_norm(g, 2)
                a2_norm(g, GB - 1)
                c2_rec(m, 0)
                c2_rec(m, 1)
                c2_x3(m, 0)
                a3_x1(g)
                c2_x3(m, 1)
                a3_k1(g)
                normalize(3, x3, m)
                a3_stats1(g)
                a3_sums(g)
                c2_t(m)
                normalize(1, x1, g)
                a3_quant(g)
                if has_next(g):
                    a1_stats(g + 1)
                c2_soft(m)
                c2_topk(m)
                a3_qT(g)
                c2_keep(m)
                c2_hidden(m, 0)
                c2_hidden(m, 1)
                c2_w(m)
                a3_x2(g)
                c2_weigh(m, 1)
                a3_stats2(g)
                c2_hidden(m, 2)
                normalize(2, x2, g)
                c2_weigh(m, 2)
                c2_hidden(m, 3)
                c2_weigh(m, 3)
                c2_hidden(m, 4)
                a3_q1(g)
                c2_weigh(m, 4)
                if has_next(g):
                    normalize(0, xin, g + 1)
                c2_out(m)

            def stage_c(m):
                for b in range(GB):
                    for u in range(4 * b, 4 * b + 4):
                        b_max(m, u)
                    b_mx(m, b)
                c2_rec(m, 0)
                c2_rec(m, 1)
                c2_x3(m, 0)
                c2_x3(m, 1)
                normalize(3, x3, m)
                c2_t(m)
                c2_soft(m)
                c2_topk(m)
                c2_keep(m)
                c2_hidden(m, 0)
                c2_w(m)
                for i in range(1, NB):
                    c2_hidden(m, i)
                    c2_weigh(m, i)
                c2_out(m)

            skewed(dve, stage_a, both, stage_c)

        @block.tensor
        def _(pe):
            t = nc.tensor

            def claim(use, g):
                bk = bank_of(g, use)
                if bk in ("A0", "A1") or (LAST_USES if is_last(g) else BANK_USES)[bk].index(use) > 0:
                    wait(pe, drained[bk], upto(g, use) - 1)
                return bank[bk]

            def done(ins, use, g=None):
                ins.then_inc(full[bank_of(g, use)], 1)

            def wdrained(use, g):
                pe.wait_ge(drained[bank_of(g, use)], upto(g, use))

            def turn(use, src, g):
                ps = claim(use, g)
                for b in range(GB):
                    ins = t.transpose(ps[:, 128 * b:128 * b + 128], src[:, b], ident)
                done(ins, use)

            def project(use, w, xT, g):
                ps = claim(use, g)
                done(t.matmul(ps, w, xT, start=True, stop=True), use)

            def a1(g):
                pe.wait_ge(ln[0]["out"], g + 1)
                pe.wait_ge(ln[0]["out2"], g + 1)
                turn("lnT0", lnx[0], g)
                pe.wait_ge(s_ctx, 16 * g + 16)
                turn("ctxT", ctx, g)

            def a1_p(g):
                wdrained("lnT0", g)
                project("Q0", const("wq0"), lnT0[:], g)
                wdrained("ctxT", g)
                project("K0", const("wk0"), ctxT[:], g)

            def a1_v(g):
                ps = bank["O"]
                for b in range(GB):
                    ins = t.matmul(ps[:, 128 * b:128 * b + 128], ctxT[:, 128 * b:128 * b + 128], const("wv01")[:, 0:128],
                                   start=True, stop=True)
                ins.then_inc(v0_full, 1)

            def a2_scores(g, b):
                n = GB * g + b
                if b == 0:
                    pe.wait_ge(drained["A0"], upto(g, "Q0"))
                    pe.wait_ge(drained["A1"], upto(g, "K0"))
                elif not first_group(g):
                    pe.wait_ge(exp0, n)
                elif b > 1:
                    pe.wait_ge(exp0, n - 1)
                else:
                    pe.wait_ge(cst["mtmp"], 2)
                cols = slice(128 * b, 128 * b + 128)
                for k in range(2):
                    ins = t.matmul(scores0(g, b)[:, 512 * k:512 * k + 512], Kg0[:, k, cols], Qm0[:, :, cols], start=True, stop=True)
                ins.then_inc(scored0, 1)

            def a2_bias(g, b):
                n = GB * g + b
                pe.wait_ge(m0_ready, n + 1)
                mv = negM0[:].unsqueeze(1).to_broadcast([128, 4, S])
                for k in range(2):
                    ins = t.matmul(scores0(g, b)[:, 512 * k:512 * k + 512], identr[:], mv, start=False, stop=True,
                                   skip_group_check=True)
                ins.then_inc(biased0, 1)

            def a2_av(g, b):
                n = GB * g + b
                pe.wait_ge(attn0, n + 1)
                if b == 0:
                    pe.wait_ge(v0_drained, g + 1)
                cols = slice(128 * b, 128 * b + 128)
                for j in range(2):
                    for p in range(4):
                        ins = t.matmul(bank["O"][32 * p:32 * p + 32, cols], Vm0[:, b, 2 * p + j, :], E0[b % 2][:, 2 * p + j, :],
                                       start=(j == 0), stop=(j == 1), tile_position=(0, 32 * p))
                ins.then_inc(av0, 1)

            def a3_ctx(g):
                pe.wait_ge(mk["fill"], GB * g + GB)
                pe.wait_ge(exp0, GB * g + GB)
                ps = claim("cfT", g)
                for b in range(GB):
                    ins = t.matmul(ps[:, 128 * b:128 * b + 128], ctx[:, b], fill[:, b], start=True, stop=True)
                done(ins, "cfT")

            def a3_k1(g):
                wdrained("cfT", g)
                project("K1", const("wk1"), cfT[:], g)

            def a3_v1(g):
                ps = claim("V1", g)
                for b in range(GB):
                    ins = t.matmul(ps[:, 128 * b:128 * b + 128], ctxT[:, 128 * b:128 * b + 128],
                                   const("wv01")[:, 128:256], start=True, stop=True)
                done(ins, "V1")

            def a3_o0(g):
                pe.wait_ge(o0_drained, g + 1)
                ps = claim("O0p", g)
                for b in range(GB):
                    ins = t.matmul(ps[:, 128 * b:128 * b + 128], O0T[:, 128 * b:128 * b + 128], const("wo0"),
                                   start=True, stop=True)
                done(ins, "O0p")

            def a3_qT(g):
                pe.wait_ge(q_int, g + 1)
                turn("qT", qz, g)

            def a3_qmm(g):
                wdrained("qT", g)
                ps = claim("qmm", g)
                for b in range(GB):
                    ins = t.matmul(ps[:, 128 * b:128 * b + 128], qT[:, 128 * b:128 * b + 128], rhsq[:], start=True, stop=True)
                done(ins, "qmm")

            def a3_t2(g):
                pe.wait_ge(ln[2]["out"], g + 1)
                pe.wait_ge(ln[2]["out2"], g + 1)
                turn("lnT2", lnx[2], g)

            def a3_q1(g):
                wdrained("lnT2", g)
                project("Q1", const("wq1"), lnT2[:], g)

            def b_scores(m, u):
                b, G = divmod(u, 4)
                cols = slice(128 * b, 128 * b + 128)
                if u == 0:
                    pe.wait_ge(qg1_dma, 64 * m + 64)
                    pe.wait_ge(km1_ready, 4 * m + 4)
                ps = claim(f"max{u}", m)
                done(t.matmul(ps, Qg1[:, G, cols], Km1[:, :, cols], start=True, stop=True), f"max{u}", m)

            def b_turn(m, b=None):
                for u in range(12, 16) if b is None else (4 * b + 2, 4 * b + 3):
                    wdrained(f"max{u}", m)
                use = "MT" if b is None else f"MT{b}"
                ps = claim(use, m)
                done(t.transpose(ps[:, 0:128], negM1[:], ident), use, m)

            def c1_scores(m, u):
                b, G = divmod(u, 4)
                cols = slice(128 * b, 128 * b + 128)
                if u == 0:
                    pe.wait_ge(ks1_dma, 16 * m + 16)
                    if not is_last(m):
                        wdrained("MT", m)
                if G == 0:
                    if is_last(m):
                        wdrained(f"MT{b}", m)
                    pe.wait_ge(qs1_dma[b % 2], 128 * m + 64 * (b // 2) + 64)
                ps = claim(f"s{u}", m)
                t.matmul(ps, KS1[:, G, cols], QS1[:, b % 2, G].rearrange("r j q -> r (j q)"), start=True, stop=False)
                done(t.matmul(ps, rowM[:, u:u + 1].to_broadcast([128, 128]), MX[:].rearrange("p j q -> p (j q)"), start=False, stop=True), f"s{u}")

            def c1_av(m, b):
                for u in range(4 * b + 1, 4 * b + 4):
                    wdrained(f"s{u}", m)
                use = ("AV01", "AV23")[b // 2]
                if b == 0:
                    pe.wait_ge(ones1_ready, m + 1)
                    wdrained("V1", m)
                if b % 2 == 0:
                    claim(use, m)
                for w in range(2):
                    cols = slice(256 * (b % 2) + 128 * w, 256 * (b % 2) + 128 * w + 128)
                    for j in range(4):
                        for k in range(2):
                            G = 2 * w + k
                            ins = t.matmul(bank[BANK_OF[use]][64 * k:64 * k + 64, cols], VS1[:, b, 4 * G + j, :],
                                           E1[b % 2][:, G, j, :], start=(j == 0), stop=(j == 3), tile_position=(0, 64 * k))
                if b % 2:
                    done(ins, use)
                else:
                    ins.then_inc(av_even, 1)

            def c2_back(m, half):
                wdrained(("AV01", "AV23")[half], m)
                use = f"TO{half}"
                ps = claim(use, m)
                for n in range(4):
                    ins = t.transpose(ps[:, 128 * n:128 * n + 128], OU[:, 2 * half + n // 2, n % 2], ident)
                done(ins, use)

            def c2_oT(m, half):
                wdrained(f"TO{half}", m)
                ps = claim(f"OT{half}", m)
                for b in (2 * half, 2 * half + 1):
                    ins = t.transpose(ps[:, 128 * b:128 * b + 128], Oq[:, b], ident)
                done(ins, f"OT{half}")

            def c2_o(m, half):
                wdrained(f"OT{half}", m)
                ps = claim(f"O1p{half}", m)
                for b in (2 * half, 2 * half + 1):
                    ins = t.matmul(ps[:, 128 * b:128 * b + 128], O1T[:, 128 * b:128 * b + 128], const("wo1"),
                                   start=True, stop=True)
                done(ins, f"O1p{half}")

            def c2_t(m):
                pe.wait_ge(ln[3]["out"], m + 1)
                pe.wait_ge(ln[3]["out2"], m + 1)
                turn("T3", lnx[3], m)

            def split_product(ps, wh, wl):
                t.matmul(ps, wh, T3h[:], start=True, stop=False)
                t.matmul(ps, wl, T3h[:], start=False, stop=False)
                return t.matmul(ps, wh, T3l[:], start=False, stop=True)

            def c2_router(m):
                wdrained("T3", m)
                ps = claim("lg", m)
                done(split_product(ps[0:NE, :], routerH[:], routerL[:]), "lg")

            def c2_lgT(m):
                wdrained("lg", m)
                ps = claim("lgT", m)
                for b in range(GB):
                    ins = t.transpose(ps[:, 128 * b:128 * b + 128], lgs[:, 128 * b:128 * b + 128], ident)
                done(ins, "lgT")

            def c2_wT(m):
                pe.wait_ge(tks["w"], m + 1)
                ps = claim("WtT", m)
                for b in range(GB):
                    ins = t.transpose(ps[0:NE, 128 * b:128 * b + 128], Wt[:, b], ident)
                done(ins, "WtT")

            def c2_gate(m, i):
                use = f"G{i}"
                done(split_product(claim(use, m), guH[:, 0, (i - 1) % NB], guL[:, 0, (i - 1) % NB]), use, m)

            def c2_up(m, i):
                use = f"U{i}"
                done(split_product(claim(use, m), guH[:, 1, (i - 1) % NB], guL[:, 1, (i - 1) % NB]), use, m)

            def c2_w(m, i):
                if i == 1:
                    wdrained("WtT", m)
                ps = claim(f"W{i - 1}", m)
                done(t.matmul(ps, selW[:, i - 1], Wx[:], start=True, stop=True), f"W{i - 1}")

            def c2_down(m, i):
                c = (i - 1) % NB
                if i == 0:
                    wdrained("U0", m)
                    pe.wait_ge(o0_drained, min(m + 2, NG) if isinstance(m, int) else m + 2)
                else:
                    wdrained(f"W{i - 1}", m)
                for b in range(GB):
                    ins = t.matmul(bank["O"][:, 128 * b:128 * b + 128], hid[i % 2][:, 128 * b:128 * b + 128], down[:, c, :],
                                   start=(i == 0 and b == 0), stop=(i == NB - 1), skip_group_check=True)
                ins.then_inc(down_done, 1)

            def setup():
                pe.wait_ge(s_pack[0], 16)
                pe.wait_ge(cst["mf"], 1)
                t.transpose(bank["C0"][:, 0:B], mf[:], ident[0:B, 0:B]).then_inc(cst["psT"], 1)
                pe.wait_ge(cst["mcol"], 1)
                pe.wait_ge(cst["ones"], 1)
                t.matmul(bank["C1"][:, 0:B], ones[:], mcol[:], start=True, stop=True).then_inc(cst["psN"], 1)

            def setup2():
                pe.wait_ge(cst["rq"], 6)
                t.transpose(bank["C2"][:, 0:128], rq[:, 0], ident)
                t.transpose(bank["C2"][:, 128:256], rq[:, 1], ident)
                t.matmul(bank["C2"][:, 256:384], y3[:, 0], const("wo1"), start=True, stop=True).then_inc(cst["psR"], 1)

            def stage_a(g):
                setup()
                a1(g)
                a1_p(g)
                pe.wait_ge(cst["act"], 1)
                a1_v(g)
                a2_scores(g, 0)
                for b in range(GB):
                    a2_bias(g, b)
                    if b + 1 < GB:
                        a2_scores(g, b + 1)
                    if b == 0:
                        setup2()
                    else:
                        a2_av(g, b - 1)
                a3_ctx(g)
                a2_av(g, GB - 1)
                a3_o0(g)
                a3_k1(g)
                pe.wait_ge(s_pack[1], 16)
                a3_v1(g)
                a3_qT(g)
                a3_qmm(g)
                a3_t2(g)
                a3_q1(g)
                a1(g + 1)
                pe.wait_ge(cst["wlo"], 1)

            def c2_blocks(m, i):
                c2_w(m, i)
                if i + 1 < NB:
                    c2_gate(m, i + 1)
                    c2_up(m, i + 1)
                c2_down(m, i)

            def both(g):
                m = g - 1

                def maxima(begin, end):
                    for u in range(begin, end):
                        b_scores(m, u)

                def scores(begin, end):
                    for u in range(begin, end):
                        c1_scores(m, u)

                a1_p(g)
                maxima(0, 6)
                a1_v(g)
                maxima(6, 10)
                a2_scores(g, 0)
                maxima(10, 13)
                a2_bias(g, 0)
                maxima(13, 16)
                a2_scores(g, 1)
                b_turn(m)
                a2_bias(g, 1)
                scores(0, 3)
                a2_scores(g, 2)
                scores(3, 5)
                a2_av(g, 0)
                scores(5, 6)
                a2_bias(g, 2)
                c1_av(m, 0)
                scores(6, 8)
                a2_scores(g, 3)
                a2_av(g, 1)
                scores(8, 10)
                a2_bias(g, 3)
                scores(10, 12)
                c1_av(m, 1)
                a2_av(g, 2)
                scores(12, 16)
                c2_back(m, 0)
                c1_av(m, 2)
                c2_oT(m, 0)
                a3_ctx(g)
                c1_av(m, GB - 1)
                c2_o(m, 0)
                a2_av(g, GB - 1)
                c2_back(m, 1)
                c2_oT(m, 1)
                a3_o0(g)
                c2_o(m, 1)
                a3_k1(g)
                a3_v1(g)
                c2_t(m)
                c2_router(m)
                c2_gate(m, 0)
                c2_lgT(m)
                c2_gate(m, 1)
                a3_qT(g)
                a3_qmm(g)
                c2_up(m, 0)
                c2_up(m, 1)
                c2_wT(m)
                c2_down(m, 0)
                c2_blocks(m, 1)
                c2_w(m, 2)
                c2_gate(m, 3)
                c2_up(m, 3)
                a3_t2(g)
                c2_down(m, 2)
                c2_w(m, 3)
                c2_gate(m, 4)
                a3_q1(g)
                c2_up(m, 4)
                c2_down(m, 3)
                c2_blocks(m, 4)
                if has_next(g):
                    a1(g + 1)

            def stage_c(m):
                for u in range(4):
                    b_scores(m, u)
                b_turn(m, 0)
                for b in range(GB):
                    for u in range(4 * b, 4 * b + 4):
                        if b + 1 < GB:
                            b_scores(m, u + 4)
                        c1_scores(m, u)
                    if b + 1 < GB:
                        b_turn(m, b + 1)
                    if b in (1, 2):
                        c1_av(m, b - 1)
                c2_back(m, 0)
                c1_av(m, 2)
                c2_oT(m, 0)
                c1_av(m, GB - 1)
                c2_o(m, 0)
                c2_back(m, 1)
                c2_oT(m, 1)
                c2_o(m, 1)
                c2_t(m)
                c2_router(m)
                c2_gate(m, 0)
                c2_lgT(m)
                c2_gate(m, 1)
                c2_up(m, 0)
                c2_up(m, 1)
                c2_gate(m, 2)
                c2_up(m, 2)
                c2_wT(m)
                c2_down(m, 0)
                c2_w(m, 1)
                c2_down(m, 1)
                c2_blocks(m, 2)
                c2_blocks(m, 3)
                c2_blocks(m, 4)

            skewed(pe, stage_a, both, stage_c)


_INS = ["x", "ctx", "mask", "pack"]


def kernel(x, ctx_1024, mask_BxS2_bf1, L0_xattn_W_Q, L0_xattn_W_K, L0_xattn_W_V, L0_xattn_W_O, L0_ffn_rhs,
           L1_xattn_Wq, L1_xattn_bq, L1_xattn_Wk, L1_xattn_bk, L1_xattn_Wv, L1_xattn_bv, L1_xattn_Wo, L1_xattn_bo,
           L1_ffn_router_w, L1_ffn_w_gate, L1_ffn_w_up, L1_ffn_w_down, L1_ffn_ws_gate, L1_ffn_ws_up, L1_ffn_ws_down):
    import concourse.bacc as bacc
    from concourse.bass_utils import run_bass_kernel_spmd

    def arr(a):
        return np.asarray(a)

    def experts_in(w, ws):
        return np.concatenate([arr(w).transpose(1, 0, 2).reshape(D, NE * FE), arr(ws)], axis=1)

    def experts_out(w, ws):
        return np.concatenate([arr(w).reshape(NC, 128, D), arr(ws)[None]], axis=0).transpose(1, 0, 2).reshape(128, NB * D)

    p = np.arange(128)
    j4 = np.arange(4)
    e8 = np.arange(NE)
    f = np.float32
    parts = {
        "ident": np.eye(128, dtype=f),
        "wq0": arr(L0_xattn_W_Q).T, "wk0": arr(L0_xattn_W_K).T,
        "wv01": np.concatenate([arr(L0_xattn_W_V).T, arr(L1_xattn_Wv).T], axis=1),
        "mask0": (p[:, None] // DH0 % 4 == j4).astype(f), "mask1": (p[:, None] // DH1 % 4 == j4).astype(f),
        "bq1": arr(L1_xattn_bq)[:, None], "bk1": arr(L1_xattn_bk)[:, None], "bv1": arr(L1_xattn_bv)[:, None],
        "wo0": arr(L0_xattn_W_O).T, "rhsT": arr(L0_ffn_rhs).T,
        "wq1": arr(L1_xattn_Wq).T, "wk1": arr(L1_xattn_Wk).T, "wo1": arr(L1_xattn_Wo).T,
        "bo1": np.broadcast_to(arr(L1_xattn_bo), (128, D)),
        "maskM": (p[:, None] % 4 == j4).astype(f),
        "tri": np.broadcast_to((e8[None, :] < e8[:, None]).astype(f).reshape(1, NE * NE), (128, NE * NE)),
        "router": arr(L1_ffn_router_w),
        "gate": experts_in(L1_ffn_w_gate, L1_ffn_ws_gate), "up": experts_in(L1_ffn_w_up, L1_ffn_ws_up),
        "down": experts_out(L1_ffn_w_down, L1_ffn_ws_down),
        "rowM": (p[:, None] // 4 == np.arange(4 * GB)).astype(f),
        "selW": ((p[:, None, None] % 32 == 2 * np.arange(NC)[None, :, None] + (p // FE)[None, None, :])
                 & (p[:, None, None] < 64)).astype(f).reshape(128, -1),
    }
    arrays = {
        "x": np.ascontiguousarray(arr(x)),
        "ctx": np.ascontiguousarray(arr(ctx_1024)),
        "mask": np.ascontiguousarray(arr(mask_BxS2_bf1)).view(np.uint8),
        "pack": np.ascontiguousarray(np.concatenate([parts[n] for n, _ in PACK], axis=1)),
    }
    nc = bacc.Bacc("TRN2", target_bir_lowering=False, num_devices=1)
    ins = [nc.dram_tensor("in_" + n, arrays[n].shape, mybir.dt.from_np(arrays[n].dtype), kind="ExternalInput").ap() for n in _INS]
    out = nc.dram_tensor("out", (B, S, D), F32, kind="ExternalOutput").ap()
    build(nc, *ins, out)
    r = run_bass_kernel_spmd(nc, [{"in_" + n: a for n, a in arrays.items()}], core_ids=[0])
    return r.results[0]["out"]
```
